# Optimizing a Trainium2 kernel written in Bass

```python
import numpy as np
import jax
import jax.numpy as jnp

def _softmax(x, axis=-1):
    return jax.nn.softmax(x, axis=axis)

def _gelu(x):
    return jax.nn.gelu(x, approximate=True)

def _silu(x):
    return jax.nn.silu(x)

def _sigmoid(x):
    return jax.nn.sigmoid(x)

def _layernorm(x, axis=-1, eps=1e-05):
    m = jnp.mean(x, axis=axis, keepdims=True)
    v = jnp.var(x, axis=axis, keepdims=True)
    return (x - m) / jnp.sqrt(v + eps)

def _scatter_add(tgt, idx, src, axis=0):
    return tgt.at[idx].add(src)

def _segment_sum(src, seg, n):
    return jax.ops.segment_sum(src, seg, n)
kernel_name = 'mk_xattn_ffn_d2_seqx_r4_6327db'

def setup_inputs(seed: int=0):
    np.random.seed(seed)
    _w = jnp.asarray

    def _rec_inputs():
        import jax
        import jax.numpy as jnp
        _rk = jax.random.key(seed)
        x = 7.22e-05 + 1 * jax.random.normal(jax.random.fold_in(_rk, 1), (4, 1024, 256), jnp.float32)
        _lenS = 1024 - jax.random.randint(jax.random.fold_in(_rk, 7), (4,), 0, max(1, 1024 // 4) + 1, jnp.int32)
        _lenS2 = 77 - jax.random.randint(jax.random.fold_in(_rk, 8), (4,), 0, max(1, 77 // 4) + 1, jnp.int32)
        _ctx_1024P = jax.random.normal(jax.random.fold_in(_rk, 11), (4, 16, 256), jnp.float32)
        _ctx_1024c = jax.random.dirichlet(jax.random.fold_in(_rk, 511), 0.3 * jnp.ones((16,), jnp.float32), (4, 77))
        _ctx_1024t = jnp.einsum('bsk,bkd->bsd', _ctx_1024c, _ctx_1024P)
        _ctx_1024t = _ctx_1024t * jax.lax.rsqrt(jnp.mean(jnp.square(_ctx_1024t)) + 1e-12) * 0.953939
        ctx_1024 = 4.14335e-05 + 0.999786 * (_ctx_1024t + 0.3 * jax.random.normal(jax.random.fold_in(_rk, 611), (4, 77, 256), jnp.float32))
        return (x, ctx_1024)
    x, ctx_1024 = _rec_inputs()

    def _L0_xattn_setup():
        import jax, jax.numpy as jnp
        import numpy as np
        N_EMBD = 256
        N_HEAD = 16
        key = jax.random.key(seed)
        ks = jax.random.split(key, 8)
        C = N_EMBD
        s = 1.0 / np.sqrt(C)
        return {'x': jax.random.normal(ks[0], (8, 256, C), jnp.float32), 'encoder_output': jax.random.normal(ks[1], (8, 144, C), jnp.float32), 'Wq': jax.random.normal(ks[2], (C, C), jnp.float32) * s, 'bq': jnp.zeros((C,), jnp.float32), 'Wkv': jax.random.normal(ks[3], (2 * C, C), jnp.float32) * s, 'bkv': jnp.zeros((2 * C,), jnp.float32), 'Wo': jax.random.normal(ks[4], (C, C), jnp.float32) * s, 'bo': jnp.zeros((C,), jnp.float32)}
    _L0_xattn_all = _L0_xattn_setup()
    _L0_xattn_in = {k: v for k, v in _L0_xattn_all.items() if k in ('Wq', 'bq', 'Wkv', 'bkv', 'Wo', 'bo')}
    del _L0_xattn_all

    def _L0_ffn_setup():
        import jax, jax.numpy as jnp
        import numpy as np
        E = 8
        K = 2
        LN_EPS = 1e-05

        def _expert_ffn(x, w1, b1, gate, w2, b2):
            h = jax.nn.gelu((x @ w1 + b1) * gate, approximate=False)
            return h @ w2 + b2
        key = jax.random.key(seed)
        B, S, D, F = (4, 512, 256, 1024)
        F2 = F // 2
        ks = jax.random.split(key, 8)
        s = 0.02
        return {'hidden_states': jax.random.normal(ks[0], (B, S, D), jnp.float32), 'router_w': jax.random.normal(ks[1], (D, E), jnp.float32) * s, 'router_b': jnp.zeros((E,), jnp.float32), 'w1': jax.random.normal(ks[2], (E, D, F), jnp.float32) * s, 'b1': jnp.zeros((E, F), jnp.float32), 'gate': jnp.ones((E, F), jnp.float32), 'w2': jax.random.normal(ks[3], (E, F, D), jnp.float32) * s, 'b2': jnp.zeros((E, D), jnp.float32), 'sw1': jax.random.normal(ks[4], (D, F2), jnp.float32) * s, 'sb1': jnp.zeros((F2,), jnp.float32), 'sgate': jnp.ones((F2,), jnp.float32), 'sw2': jax.random.normal(ks[5], (F2, D), jnp.float32) * s, 'sb2': jnp.zeros((D,), jnp.float32), 'shared_weight': jnp.float32(0.5), 'ln_g': jnp.ones((D,), jnp.float32), 'ln_b': jnp.zeros((D,), jnp.float32)}
    _L0_ffn_all = _L0_ffn_setup()
    _L0_ffn_in = {k: v for k, v in _L0_ffn_all.items() if k in ('router_w', 'router_b', 'w1', 'b1', 'gate', 'w2', 'b2', 'sw1', 'sb1', 'sgate', 'sw2', 'sb2', 'shared_weight', 'ln_g', 'ln_b')}
    del _L0_ffn_all

    def _L1_xattn_setup():
        import jax, jax.numpy as jnp
        import numpy as np
        B, N, D, K = (4, 1024, 256, 128)
        key = jax.random.key(seed)
        ks = jax.random.split(key, 5)
        q = jax.random.normal(ks[0], (B, N, D), dtype=jnp.float32)
        k = jax.random.normal(ks[1], (B, N, D), dtype=jnp.float32)
        weight = jax.random.normal(ks[2], (D, K), dtype=jnp.float32)
        kp_w = jax.random.normal(ks[3], (D, D), dtype=jnp.float32) * (1.0 / np.sqrt(D))
        kp_b = jax.random.normal(ks[4], (D,), dtype=jnp.float32) * 0.01
        return {'q': q, 'k': k, 'weight': weight, 'kp_w': kp_w, 'kp_b': kp_b}
    _L1_xattn_all = _L1_xattn_setup()
    _L1_xattn_in = {k: v for k, v in _L1_xattn_all.items() if k in ('weight', 'kp_w', 'kp_b')}
    del _L1_xattn_all

    def _L1_ffn_setup():
        import jax, jax.numpy as jnp
        import numpy as np
        key = jax.random.key(seed)
        kx, kw = jax.random.split(key)
        x = jax.random.normal(kx, (32, 1024, 256), dtype=jnp.float32)
        weight = jax.random.normal(kw, (256, 256), dtype=jnp.float32) * 0.01
        return {'x': x, 'weight': weight}
    _L1_ffn_all = _L1_ffn_setup()
    _L1_ffn_in = {k: v for k, v in _L1_ffn_all.items() if k in ('weight',)}
    del _L1_ffn_all
    return {'x': x, 'ctx_1024': ctx_1024, 'L0_xattn_Wq': _L0_xattn_in['Wq'], 'L0_xattn_bq': _L0_xattn_in['bq'], 'L0_xattn_Wkv': _L0_xattn_in['Wkv'], 'L0_xattn_bkv': _L0_xattn_in['bkv'], 'L0_xattn_Wo': _L0_xattn_in['Wo'], 'L0_xattn_bo': _L0_xattn_in['bo'], 'L0_ffn_router_w': _L0_ffn_in['router_w'], 'L0_ffn_router_b': _L0_ffn_in['router_b'], 'L0_ffn_w1': _L0_ffn_in['w1'], 'L0_ffn_b1': _L0_ffn_in['b1'], 'L0_ffn_gate': _L0_ffn_in['gate'], 'L0_ffn_w2': _L0_ffn_in['w2'], 'L0_ffn_b2': _L0_ffn_in['b2'], 'L0_ffn_sw1': _L0_ffn_in['sw1'], 'L0_ffn_sb1': _L0_ffn_in['sb1'], 'L0_ffn_sgate': _L0_ffn_in['sgate'], 'L0_ffn_sw2': _L0_ffn_in['sw2'], 'L0_ffn_sb2': _L0_ffn_in['sb2'], 'L0_ffn_shared_weight': _L0_ffn_in['shared_weight'], 'L0_ffn_ln_g': _L0_ffn_in['ln_g'], 'L0_ffn_ln_b': _L0_ffn_in['ln_b'], 'L1_xattn_weight': _L1_xattn_in['weight'], 'L1_xattn_kp_w': _L1_xattn_in['kp_w'], 'L1_xattn_kp_b': _L1_xattn_in['kp_b'], 'L1_ffn_weight': _L1_ffn_in['weight']}

def reference(x, ctx_1024, L0_xattn_Wq, L0_xattn_bq, L0_xattn_Wkv, L0_xattn_bkv, L0_xattn_Wo, L0_xattn_bo, L0_ffn_router_w, L0_ffn_router_b, L0_ffn_w1, L0_ffn_b1, L0_ffn_gate, L0_ffn_w2, L0_ffn_b2, L0_ffn_sw1, L0_ffn_sb1, L0_ffn_sgate, L0_ffn_sw2, L0_ffn_sb2, L0_ffn_shared_weight, L0_ffn_ln_g, L0_ffn_ln_b, L1_xattn_weight, L1_xattn_kp_w, L1_xattn_kp_b, L1_ffn_weight):
    import jax
    import jax.numpy as jnp

    def _L0_xattn_ref(x, encoder_output, Wq, bq, Wkv, bkv, Wo, bo):
        import jax, jax.numpy as jnp
        import numpy as np
        N_EMBD = 256
        N_HEAD = 16
        B, T, C = x.shape
        I = encoder_output.shape[1]
        H, D = (N_HEAD, C // N_HEAD)
        q = jnp.einsum('btc,oc->bto', x, Wq) + bq
        kv = jnp.einsum('bic,oc->bio', encoder_output, Wkv) + bkv
        k, v = (kv[..., :C], kv[..., C:])
        q = q.reshape(B, T, H, D).transpose(0, 2, 1, 3)
        k = k.reshape(B, I, H, D).transpose(0, 2, 1, 3)
        v = v.reshape(B, I, H, D).transpose(0, 2, 1, 3)
        att = jnp.einsum('bhtd,bhid->bhti', q, k) * (1.0 / np.sqrt(D))
        att = jax.nn.softmax(att, axis=-1)
        y = jnp.einsum('bhti,bhid->bhtd', att, v)
        y = y.transpose(0, 2, 1, 3).reshape(B, T, C)
        return jnp.einsum('btc,oc->bto', y, Wo) + bo

    def _L0_ffn_ref(hidden_states, router_w, router_b, w1, b1, gate, w2, b2, sw1, sb1, sgate, sw2, sb2, shared_weight, ln_g, ln_b):
        import jax, jax.numpy as jnp
        import numpy as np
        E = 8
        K = 2
        LN_EPS = 1e-05

        def _expert_ffn(x, w1, b1, gate, w2, b2):
            h = jax.nn.gelu((x @ w1 + b1) * gate, approximate=False)
            return h @ w2 + b2
        x = hidden_states
        logits = jnp.einsum('bsd,de->bse', x, router_w) + router_b
        probs = jax.nn.softmax(logits, axis=-1)
        topk_p, topk_i = jax.lax.top_k(probs, K)
        topk_p = topk_p / jnp.sum(topk_p, axis=-1, keepdims=True)
        combine = jnp.sum(jax.nn.one_hot(topk_i, E, dtype=x.dtype) * topk_p[..., None], axis=-2)
        moe = jnp.zeros_like(x)
        for e in range(E):
            moe = moe + combine[..., e:e + 1] * _expert_ffn(x, w1[e], b1[e], gate[e], w2[e], b2[e])
        shared = _expert_ffn(x, sw1, sb1, sgate, sw2, sb2) * jax.nn.sigmoid(shared_weight)
        y = moe + shared
        mu = jnp.mean(y, axis=-1, keepdims=True)
        var = jnp.var(y, axis=-1, keepdims=True)
        return (y - mu) * jax.lax.rsqrt(var + LN_EPS) * ln_g + ln_b

    def _L1_xattn_ref(q, k, weight, kp_w, kp_b):
        import jax, jax.numpy as jnp
        import numpy as np
        B, N, D, K = (4, 1024, 256, 128)
        n = q.shape[1]
        k_mod = k.mean(axis=1) @ kp_w.T + kp_b
        dynamic_weight = weight[None, :, :] * k_mod[:, :, None]
        q_f = jnp.fft.rfft(q, axis=1)
        w_f = jnp.fft.rfft(dynamic_weight, n=n, axis=2)
        y_f = q_f * jnp.transpose(w_f, (0, 2, 1))
        y = jnp.fft.irfft(y_f, n=n, axis=1)
        return y.astype(q.dtype)

    def _L1_ffn_ref(x, weight):
        import jax, jax.numpy as jnp
        import numpy as np
        b_weight = jnp.sign(weight)
        return jnp.einsum('bsi,oi->bso', x, b_weight)
    x = x + _L0_xattn_ref(_layernorm(x, axis=-1), ctx_1024, L0_xattn_Wq, L0_xattn_bq, L0_xattn_Wkv, L0_xattn_bkv, L0_xattn_Wo, L0_xattn_bo)
    x = x + _L0_ffn_ref(_layernorm(x, axis=-1), L0_ffn_router_w, L0_ffn_router_b, L0_ffn_w1, L0_ffn_b1, L0_ffn_gate, L0_ffn_w2, L0_ffn_b2, L0_ffn_sw1, L0_ffn_sb1, L0_ffn_sgate, L0_ffn_sw2, L0_ffn_sb2, L0_ffn_shared_weight, L0_ffn_ln_g, L0_ffn_ln_b)
    x = x + _L1_xattn_ref(_layernorm(x, axis=-1), ctx_1024, L1_xattn_weight, L1_xattn_kp_w, L1_xattn_kp_b)
    x = x + _L1_ffn_ref(_layernorm(x, axis=-1), L1_ffn_weight)
    return x

_drawn_inputs = setup_inputs


def setup_inputs(seed=0):
    import zlib

    import numpy as np

    out = dict(_drawn_inputs(seed))
    spreads = {'L0_xattn_bq': (0.0, 0.1),
     'L0_xattn_bkv': (0.0, 0.1),
     'L0_xattn_bo': (0.0, 0.1),
     'L0_ffn_router_b': (0.0, 0.1),
     'L0_ffn_b1': (0.0, 0.1),
     'L0_ffn_gate': (1.0, 0.2),
     'L0_ffn_b2': (0.0, 0.1),
     'L0_ffn_sb1': (0.0, 0.1),
     'L0_ffn_sgate': (1.0, 0.2),
     'L0_ffn_sb2': (0.0, 0.1),
     'L0_ffn_ln_g': (1.0, 0.2),
     'L0_ffn_ln_b': (0.0, 0.1)}
    factors = {'L1_xattn_kp_b': 3.219}
    for name, (base, spread) in spreads.items():
        noise = np.random.default_rng([zlib.crc32(name.encode()), seed]).standard_normal(out[name].shape)
        drawn = base * np.exp(spread * noise) if base else spread * noise
        out[name] = jnp.asarray(drawn.astype(out[name].dtype))
    for name, factor in factors.items():
        out[name] = (out[name] * factor).astype(out[name].dtype)
    return out
```

```python
import concourse.bass as bass
from concourse import mybir

F32 = mybir.dt.float32
F16 = mybir.dt.float16
I32 = mybir.dt.int32
U32 = mybir.dt.uint32
ACT = mybir.ActivationFunctionType
ALU = mybir.AluOpType
AX = mybir.AxisListType

P = 128
B, N, D = 4, 1024, 256
T = B * N
KD = D // P
NT = T // P
GT = 4
GN = GT * P
NG = T // GN
L = 77
H, HD = 16, 16
NPAIR = H // 2
HV = HD + 1
E, FF, SF = 8, 1024, 512
NF, NSF = FF // P, SF // P
TR = 256
REG = T + TR
MT = T * 2 // TR + E - 1
ZROW = E * REG
TAPS = 128
EPS = 1e-5
WS = 64.0
PSC = 16.0
QK_SCALE = 1.0 / HD ** 0.5
G2 = 2
NG2 = NT // G2
SLOTS = N // P + 1
CC = 16
NC = D // CC
RING = 4
CH = 512


class Sig:

    def __init__(self, sem, per, steady=None):
        self.sem, self.per, self.steady = sem, per, steady

    def at(self, step, n):
        return step * self.per + n


class Memory:

    def __init__(self, nc, start, names=None):
        self.nc, self.at, self.names = nc, start, {} if names is None else names

    def __call__(self, name, shape, dt=F32):
        size = 4 if dt in (F32, I32, U32) else 2
        for n in shape[1:]:
            size *= n
        self.at = (self.at + 63) // 64 * 64
        ap = self.nc.alloc_sbuf_tensor_at(name, shape, dt, offset=self.at).ap()
        self.at += size
        assert self.at <= self.nc.sbuf_usable_end, (name, self.at)
        self.names[name] = ap
        return ap


def wait(eng, s, v, alone=False):
    if not isinstance(v, int) or v > 0:
        if not isinstance(v, int) and alone:
            v = eng.to_reg(v)
            eng.wait_ge(s.steady, 1)
        eng.wait_ge(s.sem, v)


def passes(pe, out, pairs):
    todo = [(x, z) for xh, xl, zh, zl in pairs for x, z in ((xh, zh), (xh, zl), (xl, zh))]
    for n, (x, z) in enumerate(todo):
        m = pe.matmul(out, x, z, start=n == 0, stop=n == len(todo) - 1)
    return m


def build(nc, a):
    g = {}

    def dram(name, shape, dt=F32):
        g[name] = nc.dram_tensor(name, shape, dt, kind="Internal").ap()

    steady = nc.alloc_semaphore("steady")

    signals = []

    def sig(name, per=1):
        signals.append(nc.alloc_semaphore(name))
        return Sig(signals[-1], per, steady)

    dram("ks_d", [B, P, H * L], F16)
    dram("kb_d", [B, P, KD * 8 * L], F16)
    dram("v_d", [B, L, 2 * H * HV], F16)
    dram("kx_d", [2, 3, 64, KD * B * L], F16)
    dram("qx_d", [2, 4, 64, KD * GN], F16)
    dram("x1_d", [T, D])
    dram("h2_d", [T, D])
    dram("xs_d", [ZROW + TR, D])
    dram("ys_d", [MT * TR, D])
    dram("sh_d", [T, D])
    dram("toe_d", [2, TAPS + D * 2 * TAPS], F16)

    keep = Memory(nc, nc.sbuf_base, g)
    keep("ident", [P, P])
    keep("bo", [P, D])
    keep("rb", [P, E])
    keep("bq", [P, KD])
    keep("rwh", [P, KD, E], F16)
    keep("rwl", [P, KD, E], F16)
    keep("lower", [P, P], F16)
    keep("ones", [P, P], F16)
    keep("iota8", [P, E])
    keep("sgn", [P, KD, D], F16)
    keep("kmod", [P, D // 4])
    keep("slots", [P, NT, 2], I32)
    keep("wts", [P, NT, 2])
    keep("cnt", [P, E])
    keep("tab", [1, 2, MT + 1], I32)
    keep("yslots", [P, NT, 2], I32)
    keep("woh", [P, KD, D], F16)
    keep("wol", [P, KD, D], F16)
    keep("wqh", [P, KD, D], F16)
    keep("wql", [P, KD, D], F16)
    small = keep.at
    keep("w1h", [P, E, KD, FF], F16)
    keep("w1l", [P, E, KD, FF], F16)
    keep("w2h", [P, E, NF, D], F16)
    keep("w2l", [P, E, NF, D], F16)
    free = keep.at
    late = Memory(nc, small, g)
    late("x2", [P, NT, D])
    late("h3h", [P, B * SLOTS, D], F16)
    late("h3l", [P, B * SLOTS, D], F16)
    late("toe", [P, RING, 2, CC, 2 * TAPS], F16)

    psum = [nc.alloc_psum_tensor(f"bank{i}", [P, 512], F32).ap() for i in range(8)]

    phase0(nc, a, sig, Memory(nc, free), psum, g)
    phase1(nc, a, sig, Memory(nc, free), psum, g)
    done = list(signals)
    list_tables(nc, a, sig, Memory(nc, free), psum, g, done)
    for s in done:
        nc.release_semaphore(s)
    g["toe_ld"] = [sig(f"toe_ld{r}", 2 * 16) for r in range(RING)]
    ffn(nc, a, sig, Memory(nc, free), psum, g, shared=True)
    ffn(nc, a, sig, Memory(nc, free), psum, g, shared=False)
    combine(nc, a, sig, Memory(nc, late.at), psum, g)
    convolve(nc, a, sig, Memory(nc, late.at), psum, g)
    project(nc, a, sig, Memory(nc, late.at), psum, g)


def phase0(nc, a, sig, mem, psum, g):
    (ident, woh, wol, wqh, wql, bq, bo, rwh, rwl, rb, lower, ones, iota8, sgn, kmod) = (
        g[n] for n in ("ident woh wol wqh wql bq bo rwh rwl rb lower ones iota8 sgn kmod").split())
    ks_d, kb_d, v_d, kx_d, toe_d = (g[n] for n in "ks_d kb_d v_d kx_d toe_d".split())
    BL = B * L
    w3 = mem("w3", [P, 5, KD, D])
    sg = mem("sg", [P, KD, D])
    sg2 = mem("sg2", [P, KD, D])
    rw = mem("rw", [P, KD, E])
    ctxt = mem("ctxt", [P, KD, BL])
    bk = mem("bk", [P, KD])
    bv = mem("bv", [L, D])
    kpb = mem("kpb", [P, D])
    mask = mem("mask", [P, 8])
    kt = mem("kt", [P, KD, BL])
    kh = mem("kh", [P, KD, BL], F16)
    kl = mem("kl", [P, KD, BL], F16)
    kbd = mem("kbd", [P, KD, 8, BL], F16)
    kst = mem("kst", [P, 2, NPAIR, BL], F16)
    v = mem("v", [L, B, D])
    vhl = mem("vhl", [L, B, 2, H, HV], F16)
    mean = mem("mean", [P, KD, B])
    meanb = mem("meanb", [P, KD, 4, 8, B])
    km = mem("km", [P, D])
    tw = mem("tw", [P, KD, TAPS])
    twp = mem("twp", [P, 2, KD, 2 * TAPS], F16)
    zt = mem("zt", [P, D], F32)
    zh = mem("zh", [60, KD * GN], F16)
    one = mem("one", [P, 1])
    bq0 = mem("bq0", [P, KD])
    pk = [psum[0][:, 0:BL], psum[1][:, 0:BL]]
    pv = [psum[2][0:L, 0:D], psum[3][0:L, 0:D], psum[4][0:L, 0:D], psum[5][0:L, 0:D]]
    pm = psum[6][:, 0:D]

    loaded_w = sig("loaded_w")
    loaded_c = sig("loaded_c")
    zeroed = sig("zeroed")
    k_ps = sig("k_ps")
    v_ps = sig("v_ps")
    km_ps = sig("km_ps")
    kt_done = sig("kt_done")
    kh_done = sig("kh_done")
    kl_done = sig("kl_done")
    kb_done = sig("kb_done")
    v_done = sig("v_done")
    vh_done = sig("vh_done")
    vl_done = sig("vl_done")
    mean_done = sig("mean_done")
    meanb_done = sig("meanb_done")
    km_done = sig("km_done")
    part_hi = sig("part_hi")
    part_lo = sig("part_lo")
    tw_hi = sig("tw_hi")
    tw_lo = sig("tw_lo")
    sg_done = sig("sg_done")
    kx_st = sig("kx_st")
    ks_ld = sig("ks_ld")
    ks_st = sig("ks_st")
    out0 = sig("out0")

    with nc.Block() as block:
        @block.sync
        def _(sp):
            n_w = n_c = 0
            for dst, src in ((ctxt, a["ctxT"].rearrange("(k p) n -> p k n", p=P)),
                             (w3[:, 2], a["wkT"].rearrange("(k p) n -> p k n", p=P)),
                             (bk, a["bk"]), (mask, a["mask"]),
                             (w3[:, 3], a["wvT"].rearrange("(k p) n -> p k n", p=P)),
                             (bv, a["bv"].partition_broadcast(L)),
                             (w3[:, 4], a["kpT"].rearrange("(k p) n -> p k n", p=P)),
                             (kpb, a["kpb"].partition_broadcast(P))):
                sp.dma_start(dst, src).then_inc(loaded_c.sem, 16)
                n_c += 16
            for dst, src in ((w3[:, 0], a["wqT"].rearrange("(k p) n -> p k n", p=P)),
                             (w3[:, 1], a["woT"].rearrange("(k p) n -> p k n", p=P)),
                             (sg, a["sgT"].rearrange("(k p) n -> p k n", p=P)),
                             (rw, a["rw"].rearrange("(k p) n -> p k n", p=P)),
                             (tw, a["taps"].rearrange("(k p) n -> p k n", p=P)),
                             (ident, a["ident"]), (bq0, a["bq"]), (lower, a["lower"]),
                             (ones, a["ones"]), (iota8, a["iota8"]),
                             (bo, a["bo"].partition_broadcast(P)),
                             (rb, a["rb"].partition_broadcast(P))):
                sp.dma_start(dst, src).then_inc(loaded_w.sem, 16)
                n_w += 16
            assert (n_c, n_w) == (8 * 16, 12 * 16)
            sp.wait_ge(kh_done.sem, KD)
            for part in range(2):
                sp.dma_start(kx_d[0, part], kh[0:64].rearrange("p k n -> p (k n)")).then_inc(kx_st.sem, 16)
                sp.dma_start(kx_d[1, part], kh[64:128].rearrange("p k n -> p (k n)")).then_inc(kx_st.sem, 16)
            sp.wait_ge(kl_done.sem, KD)
            sp.dma_start(kx_d[0, 2], kl[0:64].rearrange("p k n -> p (k n)")).then_inc(kx_st.sem, 16)
            sp.dma_start(kx_d[1, 2], kl[64:128].rearrange("p k n -> p (k n)")).then_inc(kx_st.sem, 16)
            sp.wait_ge(kx_st.sem, 6 * 16)
            sp.wait_ge(zeroed.sem, 1)
            for half in range(2):
                src = kx_d[half].rearrange("s (r q) n -> (s r) (q n)", q=4)
                sp.dma_start(kst[64 * half:64 * half + 48, half].rearrange("p a n -> p (a n)"),
                             src).then_inc(ks_ld.sem, 16)
                sp.dma_start(kst[64 * half + 48:64 * half + 49, half].rearrange("p a n -> p (a n)"),
                             a["negone"]).then_inc(ks_ld.sem, 16)
            sp.wait_ge(ks_ld.sem, 4 * 16)
            for b in range(B):
                sp.dma_start(ks_d[b].rearrange("p (h l) -> p h l", l=L),
                             kst[:, :, :, b * L:(b + 1) * L].rearrange("p a b l -> p (a b) l")
                             ).then_inc(out0.sem, 16)
            sp.wait_ge(kb_done.sem, KD * 8)
            for b in range(B):
                sp.dma_start(kb_d[b].rearrange("p (h l) -> p h l", l=L),
                             kbd[:, :, :, b * L:(b + 1) * L].rearrange("p a b l -> p (a b) l")
                             ).then_inc(out0.sem, 16)
            sp.wait_ge(vh_done.sem, 1)
            sp.wait_ge(vl_done.sem, 1)
            for b in range(B):
                sp.dma_start(v_d[b], vhl[:, b].rearrange("p a h v -> p (a h v)")).then_inc(out0.sem, 16)
            sp.wait_ge(tw_lo.sem, 1)
            sp.wait_ge(tw_hi.sem, 1)
            for part in range(2):
                sp.dma_start(toe_d[part:part + 1, 0:TAPS], twp[0:1, part, 0, TAPS:2 * TAPS]).then_inc(out0.sem, 16)
                sp.dma_start(toe_d[part, TAPS:].rearrange("(k p n) -> p k n", p=P, k=KD),
                             twp[:, part]).then_inc(out0.sem, 16)
            sp.dma_start(g["xs_d"][ZROW:ZROW + TR].rearrange("(k p) n -> p k n", p=P),
                         zt.unsqueeze(1).to_broadcast([P, 2, D])).then_inc(out0.sem, 16)
            for half in range(2):
                sp.dma_start(g["qx_d"][half, 3, 4:64], zh[:, :]).then_inc(out0.sem, 16)
            sp.wait_ge(out0.sem, (3 * B + 7) * 16)

        @block.tensor
        def _(pe):
            pe.wait_ge(loaded_c.sem, 8 * 16)
            for mt in range(KD):
                for k in range(KD):
                    m = pe.matmul(pk[mt], w3[:, 2, k, mt * P:(mt + 1) * P], ctxt[:, k], start=k == 0, stop=k == KD - 1)
                m.then_inc(k_ps.sem, 1)
            for b in range(B):
                for k in range(KD):
                    m = pe.matmul(pv[b], ctxt[:, k, b * L:(b + 1) * L], w3[:, 3, k], start=k == 0, stop=k == KD - 1)
                m.then_inc(v_ps.sem, 1)
            pe.wait_ge(meanb_done.sem, KD * 4)
            for k in range(KD):
                m = pe.matmul(pm, meanb[:, k].rearrange("p j i b -> p (j i b)"), w3[:, 4, k], start=k == 0, stop=k == KD - 1)
            m.then_inc(km_ps.sem, 1)

        @block.scalar
        def _(act):
            for mt in range(KD):
                act.wait_ge(k_ps.sem, mt + 1)
                act.activation(kt[:, mt], pk[mt], ACT.Identity, bias=bk[:, mt:mt + 1]).then_inc(kt_done.sem, 1)
            for mt in range(KD):
                act.wait_ge(kt_done.sem, mt + 1)
                act.activation(kh[:, mt], kt[:, mt], ACT.Copy).then_inc(kh_done.sem, 1)
            for b in range(B):
                act.wait_ge(v_done.sem, b + 1)
                m = act.activation(vhl[:, b, 0, :, 0:HD], v[:, b].rearrange("p (h d) -> p h d", d=HD), ACT.Copy)
            m.then_inc(vh_done.sem, 1)

        @block.gpsimd
        def _(pool):
            pool.memset(kst[:, :, :, :], 0.0).then_inc(zeroed.sem, 1)
            pool.memset(one[:, :], 0.0).then_inc(zeroed.steady, 1)

        @block.vector
        def _(dve):
            dve.memset(zt[:, :], 0.0)
            dve.memset(vhl[:, :, 0, :, HD:HV], 1.0)
            dve.memset(vhl[:, :, 1, :, HD:HV], 0.0)
            dve.memset(zh[:, :], 0.0)
            dve.memset(twp[:, :, :, TAPS:], 0.0)
            dve.wait_ge(loaded_c.sem, 8 * 16)
            dve.tensor_reduce(mean[:, :, :], ctxt.rearrange("p k (b l) -> p k b l", l=L), axis=AX.X, op=ALU.add).then_inc(mean_done.sem, 1)
            dve.wait_ge(mean_done.sem, 1)
            for k in range(KD):
                for j in range(4):
                    dve.tensor_scalar(meanb[:, k, j], mean[:, k].unsqueeze(1).to_broadcast([P, 8, B]), 1.0 / L, None, ALU.mult).then_inc(meanb_done.sem, 1)
            for mt in range(KD):
                dve.wait_ge(kt_done.sem, mt + 1)
                dve.wait_ge(kh_done.sem, mt + 1)
                dve.tensor_tensor(kl[:, mt], kt[:, mt], kh[:, mt], ALU.subtract).then_inc(kl_done.sem, 1)
                for j in range(8):
                    dve.tensor_scalar(kbd[:, mt, j], kh[:, mt], mask[:, j:j + 1], None, ALU.mult).then_inc(kb_done.sem, 1)
            for b in range(B):
                dve.wait_ge(v_ps.sem, b + 1)
                dve.tensor_tensor(v[:, b], pv[b], bv[:, :], ALU.add).then_inc(v_done.sem, 1)
            dve.wait_ge(v_done.sem, B)
            dve.wait_ge(vh_done.sem, 1)
            for b in range(B):
                m = dve.tensor_tensor(vhl[:, b, 1, :, 0:HD], v[:, b].rearrange("p (h d) -> p h d", d=HD), vhl[:, b, 0, :, 0:HD], ALU.subtract)
            m.then_inc(vl_done.sem, 1)
            dve.wait_ge(km_ps.sem, 1)
            dve.tensor_tensor(km[:, :], pm, kpb[:, :], ALU.add).then_inc(km_done.sem, 1)
            dve.wait_ge(km_done.sem, 1)
            for j in range(4):
                dve.tensor_copy(kmod[32 * j:32 * j + 32, :], km[32 * j:32 * j + 32, j::4])
            dve.wait_ge(loaded_w.sem, 12 * 16)
            dve.tensor_scalar(bq[:, :], bq0[:, :], PSC, None, ALU.mult)
            dve.tensor_scalar(g["cnt"][:, :], iota8[:, :], float(REG), None, ALU.mult)
            parts = ((wqh, wql, w3[:, 0]), (woh, wol, w3[:, 1]), (rwh, rwl, rw[:, :, :]))
            for hi, lo, w in parts:
                dve.tensor_scalar(hi[:, :, :], w, PSC, None, ALU.mult).then_inc(part_hi.sem, 1)
            for n, (hi, lo, w) in enumerate(parts):
                dve.wait_ge(part_hi.sem, n + 1)
                dve.scalar_tensor_tensor(lo[:, :, :], w, PSC, hi[:, :, :], ALU.mult, ALU.subtract)
            dve.tensor_copy(twp[:, 0, :, 0:TAPS], tw[:, :, :]).then_inc(tw_hi.sem, 1)
            dve.wait_ge(tw_hi.sem, 1)
            dve.tensor_tensor(twp[:, 1, :, 0:TAPS], tw[:, :, :], twp[:, 0, :, 0:TAPS], ALU.subtract).then_inc(tw_lo.sem, 1)
            dve.tensor_scalar(sg2[:, :, :], sg[:, :, :], 0.0, None, ALU.is_lt).then_inc(sg_done.sem, 1)
            dve.wait_ge(sg_done.sem, 1)
            dve.scalar_tensor_tensor(sgn[:, :, :], sg[:, :, :], 0.0, sg2[:, :, :], ALU.is_gt, ALU.subtract)


def phase1(nc, a, sig, mem, psum, g):
    (ident, woh, wol, wqh, wql, bq, bo, rwh, rwl, rb, lower, ones, iota8, slots, wts, cnt, w1h, w1l, w2h, w2l) = (
        g[n] for n in ("ident woh wol wqh wql bq bo rwh rwl rb lower ones iota8 slots wts cnt w1h w1l w2h w2l").split())
    ks_d, kb_d, v_d, qx_d, x1_d, h2_d, xs_d = (g[n] for n in "ks_d kb_d v_d qx_d x1_d h2_d xs_d".split())
    NU = 16
    HALF = GN // 2
    PB = 4
    KB = 4 * L

    xa = mem("xa", [P, GT, D])
    ha = mem("ha", [P, GT, D])
    sta = mem("sta", [P, GT, 6])
    mva = mem("mva", [P, GT, 2])
    vea = mem("vea", [P, GT])
    nma = mem("nma", [P, GT])
    rsa = mem("rsa", [P, GT])
    nba = mem("nba", [P, GT])
    hth = mem("hth", [P, KD, GN], F16)
    htl = mem("htl", [P, KD, GN], F16)
    qh = mem("qh", [P, KD, GN], F16)
    ql = mem("ql", [P, KD, GN], F16)
    kbd = mem("kbc", [P, KD * 8 * L], F16)
    mx = mem("mx", [P, GT, H])
    mts = mem("mts", [H, GN], F16)
    q2 = mem("q2", [P, NPAIR, GN], F16)
    ks = mem("ksc", [P, 2, NPAIR, L], F16)
    vc = mem("vc", [L, 2, H, HV], F16)
    p32 = mem("p32", [L, 2, GN])
    ph = mem("ph", [L, PB, GN], F16)
    pl = mem("pl", [L, PB, GN], F16)
    rec = mem("rec", [P, 2, H])
    y = mem("y", [P, 2, D])
    yth = mem("yth", [P, KD, HALF], F16)
    ytl = mem("ytl", [P, KD, HALF], F16)
    xb = mem("xb", [P, GT, D])
    x1 = mem("x1", [P, GT, D])
    h2 = mem("h2", [P, GT, D])
    stc = mem("stc", [P, GT, 6])
    mvc = mem("mvc", [P, GT, 2])
    vec = mem("vec", [P, GT])
    nmc = mem("nmc", [P, GT])
    rsc = mem("rsc", [P, GT])
    nbc = mem("nbc", [P, GT])
    cth = mem("cth", [P, KD, GN], F16)
    ctl = mem("ctl", [P, KD, GN], F16)
    lgt = mem("lgt", [P, GT, E])
    top = mem("top", [P, GT, 8])
    tix = mem("tix", [P, GT, 8], U32)
    tif = mem("tif", [P, GT, 2])
    oh0 = mem("oh0", [P, GT, E])
    oh1 = mem("oh1", [P, GT, E])
    ohs = mem("ohs", [P, GT, E], F16)
    gap = mem("gap", [P, GT])
    eg = mem("eg", [P, GT])
    den = mem("den", [P, GT])
    w0 = mem("w0", [P, GT])
    cum = mem("cum", [P, GT, E])
    row = mem("row", [P, GT, E])
    pk0 = mem("pk0", [P, GT, E])
    pk1 = mem("pk1", [P, GT, E])
    sf = mem("sf", [P, 2, GT])
    sc = mem("sc", [P, 2 * GT], I32)
    mhalf = mem("mhalf", [P, GT])
    wst = mem("wst", [P, 2, CH])

    NCK = 8
    bank_a = psum[0:2]
    bank_w = psum[2:4]
    bank_s = psum[4:6]
    bank_v = psum[6:8]
    lg_ps = bank_w[0][:, 0:GT * E]
    pf_ps = bank_w[1][:, 0:GT * E]
    tt_ps = bank_w[1][:, GT * E:2 * GT * E]

    hi_on = ["act"] * NU
    lo_on = ["dve" if n % 4 == 0 else "pool" for n in range(NU)]

    xa_ld = sig("xa_ld", 16)
    kb_ld = sig("kb_ld", 16)
    bna = sig("bna", GT)
    mv_a = sig("mv_a", GT)
    rs_a = sig("rs_a", 4)
    h_a = sig("h_a", GT)
    t_a = sig("t_a", KD)
    ht_h = sig("ht_h", KD)
    ht_l = sig("ht_l", KD)
    q_ps = sig("q_ps", KD)
    q_h = sig("q_h", KD)
    q_l = sig("q_l", KD)
    q_st = sig("q_st", 6 * 16)
    mm = sig("mm", 16)
    mxd = sig("mxd", 16)
    mt_ps = sig("mt_ps", 1)
    mt_s = sig("mt_s", 1)
    m_st = sig("m_st", 32)
    q2_ld = sig("q2_ld", 32)
    ks_ld = sig("ksc_ld", 16)
    v_ld = sig("v_ld", 16)
    xb_ld = sig("xb_ld", 16)
    xb_r = sig("xb_r", 1)
    s_ps = sig("s_ps", NU)
    p_ex = sig("p_ex", NU)
    hi = {e: sig("hi_" + e, hi_on.count(e)) for e in ("act",)}
    lo = {e: sig("lo_" + e, lo_on.count(e)) for e in ("dve", "pool")}
    pv = sig("pv", NU)
    rcd = sig("rcd", 4)
    y_d = sig("y_d", 4)
    yt_ps = sig("yt_ps", 2)
    yt_h = sig("yt_h", 2)
    yt_l = sig("yt_l", 2)
    o_ps = sig("o_ps", 2)
    x1d = sig("x1d", GT)
    x1_st = sig("x1_st", 16)
    h2_st = sig("h2_st", 16)
    bnc = sig("bnc", GT)
    mv_c = sig("mv_c", GT)
    rs_c = sig("rs_c", 4)
    h_c = sig("h_c", GT)
    t_c = sig("t_c", KD)
    ct_h = sig("ct_h", KD)
    ct_l = sig("ct_l", KD)
    lg = sig("lg", 1)
    lg_d = sig("lg_d", 1)
    gap_d = sig("gap_d", 1)
    eg_d = sig("eg_d", 1)
    oh_d = sig("oh_d", 1)
    pf = sig("pf", 1)
    cch = sig("cch", 27)
    sc_d = sig("sc_d", 1)
    scat = sig("scat", 8 * 16)
    w_ld = [sig("w_ld0", 16 * NCK // 2), sig("w_ld1", 16 * NCK // 2)]
    w_hi = sig("w_hi", NCK)
    w_lo = sig("w_lo", NCK)
    mh_d = sig("mh_d")

    def after(eng, table, on, i, n):
        e = on[n]
        wait(eng, table[e], table[e].at(i, on[:n + 1].count(e)))

    def unit(i, n):
        return (i, n) if n >= 0 else (i - 1, n + NU)

    def has(i, n=0):
        return not isinstance(i, int) or 0 <= i < NG

    def loop(eng, body):
        for i in range(-1, 2):
            body(i)
        with eng.Fori(2, NG - 1) as i:
            body(i)
        body(NG - 1)
        body(NG)

    with nc.Block() as block:
        @block.sync
        def _(sp):
            def weights(i, n):
                wait(sp, w_lo, w_lo.at(i, n - 1), True)
                if n < 4:
                    k, c = n // 2, n % 2
                    src = a["w1"][bass.ds(i, 1), k * P:(k + 1) * P, c * CH:(c + 1) * CH].rearrange("e p n -> p (e n)")
                    dst = wst[:, n % 2]
                else:
                    f = (n - 4) * 2
                    src = a["w2"][bass.ds(i, 1), f * P:(f + 2) * P, :].rearrange("e (f p) n -> p (e f) n", p=P)
                    dst = wst[:, n % 2].rearrange("p (f n) -> p f n", n=D)
                sp.dma_start(dst, src).then_inc(w_ld[n % 2].sem, 16)

            def body(i):
                s, c = i + 1, i - 1
                if has(s):
                    wait(sp, h_a, h_a.at(s, 0), True)
                    sp.dma_start(xa[:, :, :], a["x"][bass.ds(s * GN, GN), :].rearrange("(t p) n -> p t n", p=P)).then_inc(xa_ld.sem, 16)
                    wait(sp, mm, mm.at(s, 0), True)
                    sp.dma_start(kbd[:, :], kb_d[bass.ds(s // 2, 1)].rearrange("b p n -> p (b n)")).then_inc(kb_ld.sem, 16)
                if has(i):
                    wait(sp, m_st, m_st.at(i, 32), True)
                    wait(sp, q_st, q_st.at(i, 96), True)
                    wait(sp, s_ps, s_ps.at(i, 0), True)
                    for half in range(2):
                        sp.dma_start(q2[64 * half:64 * half + 64].rearrange("p a n -> p (a n)"),
                                     qx_d[half].rearrange("s (r q) n -> (s r) (q n)", q=4)).then_inc(q2_ld.sem, 16)
                    sp.dma_start(ks.rearrange("p a b l -> p (a b l)"), ks_d[bass.ds(i // 2, 1)].rearrange("b p n -> p (b n)")).then_inc(ks_ld.sem, 16)
                    weights(i, 0)
                    weights(i, 1)
                    wait(sp, pv, pv.at(i, 0), True)
                    sp.dma_start(vc.rearrange("p a h v -> p (a h v)"), v_d[bass.ds(i // 2, 1)].rearrange("b p n -> p (b n)")).then_inc(v_ld.sem, 16)
                    weights(i, 2)
                    wait(sp, x1d, x1d.at(i, 0), True)
                    sp.dma_start(xb[:, :, :], a["x"][bass.ds(i * GN, GN), :].rearrange("(t p) n -> p t n", p=P)).then_inc(xb_ld.sem, 16)
                    weights(i, 3)
                if has(s):
                    wait(sp, q2_ld, q2_ld.at(s, 0), True)
                    wait(sp, q_h, q_h.at(s, KD), True)
                    for half in range(2):
                        for part in (0, 2):
                            sp.dma_start(qx_d[half, part], qh[64 * half:64 * half + 64].rearrange("p k n -> p (k n)")).then_inc(q_st.sem, 16)
                    wait(sp, q_l, q_l.at(s, KD), True)
                    for half in range(2):
                        sp.dma_start(qx_d[half, 1], ql[64 * half:64 * half + 64].rearrange("p k n -> p (k n)")).then_inc(q_st.sem, 16)
                if has(c):
                    wait(sp, x1d, x1d.at(c, GT), True)
                    sp.dma_start(g["x1_d"][bass.ds(c * GN, GN), :].rearrange("(t p) n -> p t n", p=P), x1[:, :, :]).then_inc(x1_st.sem, 16)
                    wait(sp, h_c, h_c.at(c, GT), True)
                    sp.dma_start(h2_d[bass.ds(c * GN, GN), :].rearrange("(t p) n -> p t n", p=P), h2[:, :, :]).then_inc(h2_st.sem, 16)
                if has(i):
                    for n in range(4, NCK):
                        weights(i, n)
                if has(s):
                    wait(sp, mt_s, mt_s.at(s, 1), True)
                    for half in range(2):
                        sp.dma_start(qx_d[half, 3, 0:4].rearrange("q (k n) -> (q k) n", k=KD), mts[8 * half:8 * half + 8, :]).then_inc(m_st.sem, 16)

            loop(sp, body)
            sp.wait_ge(x1_st.sem, x1_st.at(NG, 0))
            sp.wait_ge(h2_st.sem, h2_st.at(NG, 0))
            sp.wait_ge(scat.sem, scat.at(NG, 0))

        @block.gpsimd
        def _(pool):
            def rstd(i, mv, ve, nm, rs, nb, ready, read, done):
                wait(pool, ready, ready.at(i, GT), True)
                wait(pool, read, read.at(i, 0), True)
                pool.tensor_scalar(ve[:, :], mv[:, :, 1], EPS, None, ALU.add).then_inc(done.sem, 1)
                pool.tensor_scalar(nm[:, :], mv[:, :, 0], -1.0, None, ALU.mult).then_inc(done.sem, 1)
                wait(pool, done, done.at(i, 2), True)
                pool.tensor_tensor(out=rs[:, :], in0=ve[:, :], in1=mhalf[:, :], op=ALU.pow).then_inc(done.sem, 1)
                wait(pool, done, done.at(i, 3), True)
                pool.tensor_tensor(out=nb[:, :], in0=nm[:, :], in1=rs[:, :], op=ALU.mult).then_inc(done.sem, 1)

            def low(i, n):
                b = n % PB
                after(pool, hi, hi_on, i, n)
                wait(pool, pv, pv.at(i, n - PB + 1), True)
                pool.tensor_tensor(out=pl[:, b], in0=p32[:, n % 2], in1=ph[:, b], op=ALU.subtract).then_inc(lo["pool"].sem, 1)

            def body(i):
                s, c = i + 1, i - 1
                if has(s):
                    rstd(s, mva, vea, nma, rsa, nba, mv_a, h_a, rs_a)
                for n in range(NU):
                    j, m = unit(i, n - 1)
                    if has(j) and lo_on[m] == "pool":
                        low(j, m)
                    if n == 8 and has(i):
                        wait(pool, xb_ld, xb_ld.at(i, 16), True)
                        pool.tensor_tensor(out=xb[:, :, :], in0=xb[:, :, :], in1=bo.unsqueeze(1).to_broadcast([P, GT, D]), op=ALU.add).then_inc(xb_r.sem, 1)
                    if n == 5 and has(c):
                        rstd(c, mvc, vec, nmc, rsc, nbc, mv_c, h_c, rs_c)
                    if n == 14 and has(c):
                        wait(pool, sc_d, sc_d.at(c, 1), True)
                        for k in range(2):
                            for t in range(GT):
                                pool.indirect_dma_start(out=xs_d[:, :], out_offset=bass.IndirectOffsetOnAxis(ap=sc[:, k * GT + t:k * GT + t + 1], axis=0),
                                                        in_=h2[:, t], in_offset=None).then_inc(scat.sem, 16)

            pool.memset(mhalf[:, :], -0.5).then_inc(mh_d.sem, 1)
            pool.wait_ge(mh_d.sem, 1)
            loop(pool, body)

        @block.scalar
        def _(act):
            def weights(i, n):
                wait(act, w_ld[n % 2], w_ld[n % 2].at(i, 16 * (n // 2 + 1)))
                if n < 4:
                    k, c = n // 2, n % 2
                    dst = w1h[:, bass.ds(i, 1), k, c * CH:(c + 1) * CH].rearrange("p e n -> p (e n)")
                else:
                    f = (n - 4) * 2
                    dst = w2h[:, bass.ds(i, 1), f:f + 2, :].rearrange("p e f n -> p (e f n)")
                act.activation(dst, wst[:, n % 2], ACT.Copy, scale=WS).then_inc(w_hi.sem, 1)

            def body(i):
                s, c = i + 1, i - 1
                for n in range(NU):
                    if has(i):
                        wait(act, s_ps, s_ps.at(i, n + 1))
                        j, m = unit(i, n - 2)
                        if has(j):
                            after(act, lo, lo_on, j, m)
                        act.activation(p32[:, n % 2], bank_s[n % 2][0:L, :], ACT.Exp, scale=QK_SCALE / PSC).then_inc(p_ex.sem, 1)
                    j, m = unit(i, n - 1)
                    if has(j) and hi_on[m] == "act":
                        wait(act, p_ex, p_ex.at(j, m + 1))
                        wait(act, pv, pv.at(j, m - PB + 1))
                        act.activation(ph[:, m % PB], p32[:, m % 2], ACT.Copy).then_inc(hi["act"].sem, 1)
                    if has(i) and n % 2 == 0:
                        weights(i, n // 2)
                    if n == 0 and has(s):
                        wait(act, xa_ld, xa_ld.at(s, 16))
                        wait(act, rs_a, rs_a.at(s, 4))
                        wait(act, t_a, t_a.at(s, 0))
                        for t in range(GT):
                            act.activation(ha[:, t], xa[:, t], ACT.Identity, bias=nba[:, t:t + 1], scale=rsa[:, t:t + 1]).then_inc(h_a.sem, 1)
                    if n == 2 and has(c):
                        wait(act, yt_ps, yt_ps.at(c, 2))
                        wait(act, o_ps, o_ps.at(c, 1))
                        act.activation(yth[:, :, :].rearrange("p k n -> p (k n)"), bank_w[0][:, :], ACT.Copy).then_inc(yt_h.sem, 1)
                    if n == 2 and has(s):
                        for k in range(KD):
                            wait(act, t_a, t_a.at(s, k + 1))
                            wait(act, q_ps, q_ps.at(s, 0))
                            act.activation(hth[:, k], bank_a[k][:, :], ACT.Copy).then_inc(ht_h.sem, 1)
                    if n == 4 and has(s):
                        for k in range(KD):
                            wait(act, q_ps, q_ps.at(s, k + 1))
                            wait(act, q_st, q_st.at(s, 0))
                            wait(act, mm, mm.at(s, 0))
                            act.activation(qh[:, k], bank_a[k][:, :], ACT.Identity, bias=bq[:, k:k + 1]).then_inc(q_h.sem, 1)
                    if n == 6 and has(c):
                        wait(act, rs_c, rs_c.at(c, 4))
                        wait(act, t_c, t_c.at(c, 0))
                        wait(act, scat, scat.at(c, 0))
                        wait(act, h2_st, h2_st.at(c, 0))
                        for t in range(GT):
                            act.activation(h2[:, t], x1[:, t], ACT.Identity, bias=nbc[:, t:t + 1], scale=rsc[:, t:t + 1]).then_inc(h_c.sem, 1)
                    if n == 8 and has(c):
                        for k in range(KD):
                            wait(act, t_c, t_c.at(c, k + 1))
                            wait(act, lg, lg.at(c, 0))
                            act.activation(cth[:, k], bank_w[k][:, :], ACT.Copy).then_inc(ct_h.sem, 1)
                    if n == 11 and has(i):
                        wait(act, yt_ps, yt_ps.at(i, 1))
                        wait(act, o_ps, o_ps.at(i, 0))
                        act.activation(yth[:, :, :].rearrange("p k n -> p (k n)"), bank_w[0][:, :], ACT.Copy).then_inc(yt_h.sem, 1)
                    if n == 12 and has(c):
                        wait(act, gap_d, gap_d.at(c, 1))
                        act.activation(eg[:, :], gap[:, :], ACT.Exp).then_inc(eg_d.sem, 1)
                    if n == 14 and has(s):
                        wait(act, mt_ps, mt_ps.at(s, 1))
                        wait(act, m_st, m_st.at(s, 0))
                        act.activation(mts[:, :], bank_a[0][0:H, :], ACT.Copy, scale=1.0 / PSC).then_inc(mt_s.sem, 1)

            loop(act, body)

        @block.vector
        def _(dve):
            def stats(i, x, st, mv, ready, n_ready, bn, mvs):
                wait(dve, ready, ready.at(i, n_ready))
                for t in range(GT):
                    dve.bn_stats(st[:, t], x[:, t]).then_inc(bn.sem, 1)
                for t in range(GT):
                    wait(dve, bn, bn.at(i, t + 1), True)
                    dve.bn_aggr(mv[:, t], st[:, t]).then_inc(mvs.sem, 1)

            def weights(i, n):
                wait(dve, w_hi, w_hi.at(i, n + 1))
                if n < 4:
                    k, c = n // 2, n % 2
                    at = (slice(None), bass.ds(i, 1), k, slice(c * CH, (c + 1) * CH))
                    h, l = (w[at].rearrange("p e n -> p (e n)") for w in (w1h, w1l))
                else:
                    f = (n - 4) * 2
                    at = (slice(None), bass.ds(i, 1), slice(f, f + 2), slice(None))
                    h, l = (w[at].rearrange("p e f n -> p (e f n)") for w in (w2h, w2l))
                dve.scalar_tensor_tensor(l, wst[:, n % 2], WS, h, ALU.mult, ALU.subtract).then_inc(w_lo.sem, 1)

            def values(i, half):
                wait(dve, pv, pv.at(i, 8 * half + 8))
                wait(dve, yt_ps, yt_ps.at(i, half))
                for t in range(2):
                    v3 = bank_v[t][:, 0:H * HV].rearrange("p (h v) -> p h v", v=HV)
                    dve.reciprocal(rec[:, t], v3[:, :, HD]).then_inc(rcd.sem, 1)
                for t in range(2):
                    v3 = bank_v[t][:, 0:H * HV].rearrange("p (h v) -> p h v", v=HV)
                    wait(dve, rcd, rcd.at(i, 2 * half + t + 1))
                    dve.tensor_tensor(y[:, t].rearrange("p (h d) -> p h d", d=HD), v3[:, :, 0:HD],
                                      rec[:, t].unsqueeze(2).to_broadcast([P, H, HD]), ALU.mult).then_inc(y_d.sem, 1)

            def y_low(i, half):
                wait(dve, yt_h, yt_h.at(i, half + 1))
                wait(dve, o_ps, o_ps.at(i, half))
                dve.tensor_tensor(ytl[:, :, :].rearrange("p k n -> p (k n)"), bank_w[0][:, :],
                                  yth[:, :, :].rearrange("p k n -> p (k n)"), ALU.subtract).then_inc(yt_l.sem, 1)

            def residual(i, half):
                wait(dve, o_ps, o_ps.at(i, half + 1))
                wait(dve, xb_r, xb_r.at(i, 1))
                wait(dve, h_c, h_c.at(i, 0))
                wait(dve, x1_st, x1_st.at(i, 0))
                for t in range(2):
                    dve.scalar_tensor_tensor(x1[:, 2 * half + t], bank_w[1][:, t * D:(t + 1) * D], 1.0 / PSC,
                                             xb[:, 2 * half + t], ALU.mult, ALU.add).then_inc(x1d.sem, 1)

            class Chain:

                def __init__(self, i, n):
                    self.i, self.n = i, n

                def __call__(self, instruction):
                    instruction.then_inc(cch.sem, 1)
                    self.n += 1

                def wait(self):
                    wait(dve, cch, cch.at(self.i, self.n))

            def logits(i):
                wait(dve, lg, lg.at(i, 1))
                dve.scalar_tensor_tensor(lgt[:, :, :], lg_ps.rearrange("p (t e) -> p t e", e=E), 1.0 / PSC,
                                         rb.unsqueeze(1).to_broadcast([P, GT, E]), ALU.mult, ALU.add).then_inc(lg_d.sem, 1)

            def top2(i):
                ch = Chain(i, 0)
                wait(dve, lg_d, lg_d.at(i, 1), True)
                for t in range(GT):
                    ch(dve.max(top[:, t], lgt[:, t]))
                ch.wait()
                wait(dve, eg_d, eg_d.at(i, 0))
                dve.tensor_tensor(gap[:, :], top[:, :, 1], top[:, :, 0], ALU.subtract).then_inc(gap_d.sem, 1)
                for t in range(GT):
                    ch(dve.max_index(tix[:, t], top[:, t], lgt[:, t]))
                ch.wait()
                ch(dve.tensor_copy(tif[:, :, :], tix[:, :, 0:2]))
                ch.wait()
                io = iota8.unsqueeze(1).to_broadcast([P, GT, E])
                ch(dve.tensor_tensor(oh0[:, :, :], io, tif[:, :, 0].unsqueeze(2).to_broadcast([P, GT, E]), ALU.is_equal))
                ch(dve.tensor_tensor(oh1[:, :, :], io, tif[:, :, 1].unsqueeze(2).to_broadcast([P, GT, E]), ALU.is_equal))
                ch.wait()
                wait(dve, pf, pf.at(i, 0))
                dve.tensor_tensor(ohs[:, :, :], oh0[:, :, :], oh1[:, :, :], ALU.add).then_inc(oh_d.sem, 1)
                return ch

            def place(i, n0):
                ch = Chain(i, n0)
                wait(dve, eg_d, eg_d.at(i, 1))
                ch(dve.tensor_scalar(den[:, :], eg[:, :], 1.0, None, ALU.add))
                ch.wait()
                ch(dve.reciprocal(w0[:, :], den[:, :]))
                ch.wait()
                ch(dve.tensor_copy(wts[:, bass.ds(i * GT, GT), 0], w0[:, :]))
                ch(dve.tensor_tensor(wts[:, bass.ds(i * GT, GT), 1], eg[:, :], w0[:, :], ALU.mult))
                wait(dve, pf, pf.at(i, 1))
                tot = tt_ps.rearrange("p (t e) -> p t e", e=E)
                ch(dve.tensor_copy(cum[:, 0], cnt[:, :]))
                for t in range(1, GT):
                    ch.wait()
                    ch(dve.tensor_tensor(cum[:, t], cum[:, t - 1], tot[:, t - 1], ALU.add))
                ch.wait()
                ch(dve.tensor_tensor(cnt[:, :], cum[:, GT - 1], tot[:, GT - 1], ALU.add))
                ch(dve.tensor_tensor(row[:, :, :], cum[:, :, :], pf_ps.rearrange("p (t e) -> p t e", e=E), ALU.add))
                ch.wait()
                ch(dve.tensor_tensor(pk0[:, :, :], row[:, :, :], oh0[:, :, :], ALU.mult))
                ch(dve.tensor_tensor(pk1[:, :, :], row[:, :, :], oh1[:, :, :], ALU.mult))
                ch.wait()
                ch(dve.tensor_reduce(sf[:, 0], pk0[:, :, :], axis=AX.X, op=ALU.add))
                ch(dve.tensor_reduce(sf[:, 1], pk1[:, :, :], axis=AX.X, op=ALU.add))
                ch.wait()
                wait(dve, scat, scat.at(i, 0))
                for k in range(2):
                    ch(dve.tensor_copy(slots[:, bass.ds(i * GT, GT), k], sf[:, k]))
                dve.tensor_copy(sc[:, :], sf[:, :, :].rearrange("p k t -> p (k t)")).then_inc(sc_d.sem, 1)
                return ch

            def body(i):
                s, c = i + 1, i - 1
                if has(s):
                    stats(s, xa, sta, mva, xa_ld, 16, bna, mv_a)
                for n in range(NU):
                    j, m = unit(i, n - 1)
                    if has(j) and lo_on[m] == "dve":
                        after(dve, hi, hi_on, j, m)
                        wait(dve, pv, pv.at(j, m - PB + 1))
                        dve.tensor_tensor(pl[:, m % PB], p32[:, m % 2], ph[:, m % PB], ALU.subtract).then_inc(lo["dve"].sem, 1)
                    if n == 2 and has(c):
                        values(c, 1)
                    if n == 3 and has(s):
                        for k in range(KD):
                            wait(dve, ht_h, ht_h.at(s, k + 1))
                            dve.tensor_tensor(htl[:, k], bank_a[k][:, :], hth[:, k], ALU.subtract).then_inc(ht_l.sem, 1)
                    if n == 3 and has(c):
                        y_low(c, 1)
                    if n == 4 and has(c):
                        residual(c, 1)
                        stats(c, x1, stc, mvc, x1d, GT, bnc, mv_c)
                    if n == 5 and has(s):
                        for k in range(KD):
                            wait(dve, q_h, q_h.at(s, k + 1))
                            wait(dve, q_st, q_st.at(s, 0))
                            dve.scalar_tensor_tensor(ql[:, k], bank_a[k][:, :], bq[:, k:k + 1], qh[:, k], ALU.add, ALU.subtract).then_inc(q_l.sem, 1)
                    if n == 10 and has(i):
                        values(i, 0)
                    if 6 <= n < 14 and has(s):
                        for u in (2 * (n - 6), 2 * (n - 6) + 1):
                            t, mt, half = u // 4, u // 2 % 2, u % 2
                            wait(dve, mm, mm.at(s, u + 1))
                            wait(dve, mt_ps, mt_ps.at(s, 0))
                            dve.tensor_reduce(mx[:, t, 8 * half + mt:8 * half + 8:2], bank_a[u % 2][:, 0:KB].rearrange("p (h l) -> p h l", l=L),
                                              axis=AX.X, op=ALU.max).then_inc(mxd.sem, 1)
                    if n == 9 and has(c):
                        for k in range(KD):
                            wait(dve, ct_h, ct_h.at(c, k + 1))
                            dve.tensor_tensor(ctl[:, k], bank_w[k][:, :], cth[:, k], ALU.subtract).then_inc(ct_l.sem, 1)
                    if n == 10 and has(c):
                        logits(c)
                    if n == 11 and has(i):
                        y_low(i, 0)
                    if n == 11 and has(c):
                        top2(c)
                    if n == 12 and has(i):
                        residual(i, 0)
                    if n == 13 and has(c):
                        assert place(c, 11).n == cch.per
                    if n % 2 == 1 and has(i):
                        weights(i, n // 2)

            loop(dve, body)

        @block.tensor
        def _(pe):
            def output(i, half):
                wait(pe, yt_l, yt_l.at(i, half + 1))
                wait(pe, x1d, x1d.at(i, 2 * half))
                wait(pe, ct_l, ct_l.at(i, 0))
                if half:
                    wait(pe, cch, cch.at(i, 0))
                for t in range(2):
                    at = slice(t * P, (t + 1) * P)
                    m = passes(pe, bank_w[1][:, t * D:(t + 1) * D],
                               [(yth[:, k, at], ytl[:, k, at], woh[:, k], wol[:, k]) for k in range(KD)])
                m.then_inc(o_ps.sem, 1)

            def transpose_y(i, half):
                wait(pe, y_d, y_d.at(i, 2 * half + 2))
                wait(pe, yt_l, yt_l.at(i, half))
                wait(pe, lg_d, lg_d.at(i, 0))
                for t in range(2):
                    for k in range(KD):
                        m = pe.transpose(bank_w[0][:, k * HALF + t * P:k * HALF + (t + 1) * P], y[:, t, k * P:(k + 1) * P], ident[:, :])
                m.then_inc(yt_ps.sem, 1)

            def rows_to_columns(i, h, bank, ready, done):
                wait(pe, ready, ready.at(i, GT))
                for k in range(KD):
                    for t in range(GT):
                        m = pe.transpose(bank[k][:, t * P:(t + 1) * P], h[:, t, k * P:(k + 1) * P], ident[:, :])
                    m.then_inc(done.sem, 1)

            def body(i):
                s, c = i + 1, i - 1
                for n in range(NU):
                    if has(i):
                        if n == 0:
                            wait(pe, q2_ld, q2_ld.at(i, 32))
                            wait(pe, ks_ld, ks_ld.at(i, 16))
                        wait(pe, p_ex, p_ex.at(i, n - 1))
                        for half in range(2):
                            m = pe.matmul(bank_s[n % 2][0:L, half * HALF:(half + 1) * HALF], ks[:, half, n % 8],
                                          q2[:, n % 8, n // 8 * HALF:(n // 8 + 1) * HALF], start=True, stop=True)
                        m.then_inc(s_ps.sem, 1)
                    j, m_ = unit(i, n - 2)
                    if has(j):
                        after(pe, hi, hi_on, j, m_)
                        after(pe, lo, lo_on, j, m_)
                        if m_ == 0:
                            wait(pe, v_ld, v_ld.at(j, 16))
                        if m_ % 8 == 0:
                            wait(pe, y_d, y_d.at(j, 2 * (m_ // 8)))
                        for half in range(2):
                            hd = 2 * (m_ % 8) + half
                            for t in range(2):
                                at = slice(half * HALF + t * P, half * HALF + (t + 1) * P)
                                m = passes(pe, bank_v[t][:, hd * HV:(hd + 1) * HV],
                                           [(ph[:, m_ % PB, at], pl[:, m_ % PB, at], vc[:, 0, hd], vc[:, 1, hd])])
                        m.then_inc(pv.sem, 1)
                    if n == 2 and has(c):
                        transpose_y(c, 1)
                    if n == 2 and has(s):
                        wait(pe, mt_s, mt_s.at(s, 0))
                        wait(pe, mxd, mxd.at(s, 0))
                        rows_to_columns(s, ha, bank_a, h_a, t_a)
                    if n == 3 and has(c):
                        output(c, 1)
                    if n == 4 and has(s):
                        for mt in range(KD):
                            wait(pe, ht_l, ht_l.at(s, KD))
                            m = passes(pe, bank_a[mt][:, :], [(wqh[:, k, mt * P:(mt + 1) * P], wql[:, k, mt * P:(mt + 1) * P], hth[:, k], htl[:, k]) for k in range(KD)])
                            m.then_inc(q_ps.sem, 1)
                    if 6 <= n < 14 and has(s):
                        if n == 6:
                            wait(pe, kb_ld, kb_ld.at(s, 16))
                            wait(pe, q_l, q_l.at(s, KD))
                        for u in (2 * (n - 6), 2 * (n - 6) + 1):
                            t, mt, half = u // 4, u // 2 % 2, u % 2
                            wait(pe, mxd, mxd.at(s, u - 1))
                            at = (mt * 2 + half) * KB
                            pe.matmul(bank_a[u % 2][:, 0:KB], qh[:, mt, t * P:(t + 1) * P], kbd[:, at:at + KB], start=True, stop=True).then_inc(mm.sem, 1)
                    if n == 8 and has(c):
                        rows_to_columns(c, h2, bank_w, h_c, t_c)
                    if n == 10 and has(c):
                        wait(pe, ct_l, ct_l.at(c, KD))
                        for t in range(GT):
                            at = slice(t * P, (t + 1) * P)
                            m = passes(pe, lg_ps[:, t * E:(t + 1) * E], [(cth[:, k, at], ctl[:, k, at], rwh[:, k], rwl[:, k]) for k in range(KD)])
                        m.then_inc(lg.sem, 1)
                    if n == 11 and has(i):
                        transpose_y(i, 0)
                    if n == 12 and has(i):
                        output(i, 0)
                    if n == 13 and has(c):
                        wait(pe, oh_d, oh_d.at(c, 1))
                        if has(i):
                            wait(pe, x1d, x1d.at(i, 2))
                        pe.matmul(pf_ps, lower[:, :], ohs[:, :, :].rearrange("p t e -> p (t e)"), start=True, stop=True)
                        pe.matmul(tt_ps, ones[:, :], ohs[:, :, :].rearrange("p t e -> p (t e)"), start=True, stop=True).then_inc(pf.sem, 1)
                    if n == 14 and has(s):
                        wait(pe, mxd, mxd.at(s, 16))
                        for t in range(GT):
                            m = pe.transpose(bank_a[0][0:H, t * P:(t + 1) * P], mx[:, t], ident[:, :])
                        m.then_inc(mt_ps.sem, 1)

            loop(pe, body)


def paired(eng, count, body):
    pairs = (count - 5) // 2
    for i in range(-1, 3):
        body(i, i % 2)
    with eng.Fori(0, pairs) as m:
        body(m * 2 + 3, 1)
        body(m * 2 + 4, 0)
    for i in range(2 * pairs + 3, count + 1):
        body(i, i % 2)


def exists(i, count):
    return not isinstance(i, int) or 0 <= i < count


class Chain:

    def __init__(self, eng, s):
        self.eng, self.s, self.n = eng, s, 0

    def __call__(self, instruction):
        instruction.then_inc(self.s.sem, 1)
        self.n += 1

    def wait(self):
        self.eng.wait_ge(self.s.sem, self.n)


def list_tables(nc, a, sig, mem, psum, g, done):
    iota8, cnt, tab, xs_d, slots, yslots = (g[n] for n in ("iota8", "cnt", "tab", "xs_d", "slots", "yslots"))
    MM = MT + 1
    NM = T // TR
    NS = NT * 2
    rows = mem("rows", [P, TR // P])
    tiles = mem("tiles", [P, MM])
    full = mem("full", [P, NM])
    zero = mem("zero", [P, D])
    at = mem("tail_at", [P, TR // P, E])
    ix = mem("tail_ix", [P, TR // P * E], I32)
    num = mem("num", [P, E])
    more = mem("more", [P, E, NM])
    held = [mem(f"held{k}", [P, E]) for k in range(4)]
    before = mem("before", [P, E])
    start = mem("start", [P, E])
    shift = mem("shift", [P, E])
    jump = mem("jump", [P, E])
    sf = mem("tb_sf", [P, NS])
    from_e = mem("from_e", [P, NS, E])
    jumps = mem("jumps", [P, NS, E])
    moved = mem("moved", [P, NS])
    to_f = mem("to_f", [P, NS])
    past = mem("past", [1, MM, E])
    past_n = mem("past_n", [1, MM, E])
    exp_f = mem("exp_f", [1, MM])
    first = mem("first", [1, MM])
    base = mem("base", [1, MM])
    local = mem("local", [1, MM])
    row_f = mem("row_f", [1, MM])
    tf = mem("tf", [1, 2, MM])

    const_ld = sig("tb_const_ld")
    zero_d = sig("tb_zero")
    step = sig("tb_step")
    ix_d = sig("tb_ix")
    tab_d = sig("tab_d")
    tail = sig("tail")

    with nc.Block() as block:
        @block.sync
        def _(sp):
            for dst, src in ((rows, a["rows"]), (tiles, a["tiles"])):
                sp.dma_start(dst, src).then_inc(const_ld.sem, 16)
            sp.wait_ge(const_ld.sem, 2 * 16)
            sp.wait_ge(tail.sem, TR // P * E * 16)

        @block.gpsimd
        def _(pool):
            for s in done:
                pool.sem_clear(s)
            pool.memset(zero[:, :], 0.0).then_inc(zero_d.sem, 1)
            pool.wait_ge(zero_d.sem, 1)
            pool.wait_ge(ix_d.sem, 1)
            for n in range(TR // P * E):
                pool.indirect_dma_start(out=xs_d[:, :], out_offset=bass.IndirectOffsetOnAxis(ap=ix[:, n:n + 1], axis=0),
                                        in_=zero[:, :], in_offset=None).then_inc(tail.sem, 16)

        @block.vector
        def _(dve):
            ch = Chain(dve, step)
            dve.wait_ge(const_ld.sem, 2 * 16)
            ch(dve.tensor_tensor(at[:, :, :], cnt.unsqueeze(1).to_broadcast([P, TR // P, E]),
                                 rows.unsqueeze(2).to_broadcast([P, TR // P, E]), ALU.add))
            ch(dve.tensor_scalar(start[:, :], iota8[:, :], float(REG), None, ALU.mult))
            ch(dve.tensor_scalar(full[:, :], tiles[:, 0:NM], float(TR), None, ALU.mult))
            ch(dve.tensor_copy(sf[:, :], slots.rearrange("p t k -> p (t k)")))
            ch(dve.memset(jump[:, 0:1], 0.0))
            ch.wait()
            dve.tensor_copy(ix[:, :], at[:, :, :].rearrange("p r e -> p (r e)")).then_inc(ix_d.sem, 1)
            ch(dve.tensor_tensor(num[:, :], cnt[:, :], start[:, :], ALU.subtract))
            ch.wait()
            ch(dve.tensor_tensor(more[:, :, :], num.unsqueeze(2).to_broadcast([P, E, NM]),
                                 full.unsqueeze(1).to_broadcast([P, E, NM]), ALU.is_gt))
            ch.wait()
            ch(dve.tensor_reduce(held[0][:, :], more[:, :, :], axis=AX.X, op=ALU.add))
            for k in range(3):
                ch.wait()
                ch(dve.tensor_copy(held[k + 1][:, 0:1 << k], held[k][:, 0:1 << k]))
                ch(dve.tensor_tensor(held[k + 1][:, 1 << k:], held[k][:, 1 << k:], held[k][:, :E - (1 << k)], ALU.add))
            ch.wait()
            ch(dve.tensor_tensor(past[:, :, :], tiles[0:1].unsqueeze(2).to_broadcast([1, MM, E]),
                                 held[3][0:1].unsqueeze(1).to_broadcast([1, MM, E]), ALU.is_ge))
            ch(dve.tensor_tensor(before[:, :], held[3][:, :], held[0][:, :], ALU.subtract))
            ch.wait()
            ch(dve.tensor_tensor(past_n[:, :, :], past[:, :, :], held[0][0:1].unsqueeze(1).to_broadcast([1, MM, E]), ALU.mult))
            ch(dve.tensor_reduce(exp_f[:, :], past[:, :, :], axis=AX.X, op=ALU.add))
            ch.wait()
            ch(dve.tensor_reduce(first[:, :], past_n[:, :, :], axis=AX.X, op=ALU.add))
            ch(dve.tensor_scalar(base[:, :], exp_f[:, :], float(REG), None, ALU.mult))
            ch(dve.tensor_scalar(tf[:, 0], exp_f[:, :], float(E - 1), None, ALU.min))
            ch.wait()
            ch(dve.tensor_tensor(local[:, :], tiles[0:1], first[:, :], ALU.subtract))
            ch.wait()
            ch(dve.scalar_tensor_tensor(row_f[:, :], local[:, :], float(TR), base[:, :], ALU.mult, ALU.add))
            ch.wait()
            ch(dve.tensor_scalar(tf[:, 1], row_f[:, :], float(ZROW), None, ALU.min))
            ch.wait()
            dve.tensor_copy(tab[:, :, :], tf[:, :, :]).then_inc(tab_d.sem, 1)
            ch(dve.scalar_tensor_tensor(shift[:, :], before[:, :], float(TR), start[:, :], ALU.mult, ALU.subtract))
            ch(dve.tensor_tensor(from_e[:, :, :], sf.unsqueeze(2).to_broadcast([P, NS, E]),
                                 start.unsqueeze(1).to_broadcast([P, NS, E]), ALU.is_ge))
            ch.wait()
            ch(dve.tensor_tensor(jump[:, 1:E], shift[:, 1:E], shift[:, 0:E - 1], ALU.subtract))
            ch.wait()
            ch(dve.tensor_tensor(jumps[:, :, :], from_e[:, :, :], jump.unsqueeze(1).to_broadcast([P, NS, E]), ALU.mult))
            ch.wait()
            ch(dve.tensor_reduce(moved[:, :], jumps[:, :, :], axis=AX.X, op=ALU.add))
            ch.wait()
            ch(dve.tensor_tensor(to_f[:, :], sf[:, :], moved[:, :], ALU.add))
            ch.wait()
            dve.tensor_copy(yslots.rearrange("p t k -> p (t k)"), to_f[:, :]).then_inc(tab_d.sem, 1)
            dve.wait_ge(tab_d.sem, 2)


def ffn(nc, a, sig, mem, psum, g, shared):
    ident, tab = g["ident"], g["tab"]
    name = "s_" if shared else "e_"
    nf = NSF if shared else NF
    count = T // TR if shared else MT
    NP_ = nf // 2
    NQ = nf // 4
    source, target = (g["h2_d"], g["sh_d"]) if shared else (g["xs_d"], g["ys_d"])

    xr = mem(name + "xr", [P, 2, TR // P, D])
    xh = mem(name + "xh", [P, 2, KD, TR], F16)
    xl = mem(name + "xl", [P, 2, KD, TR], F16)
    gel = mem(name + "gel", [P, NQ, 4, TR])
    gh = mem(name + "gh", [P, 2, nf, TR], F16)
    gl = mem(name + "gl", [P, 2, nf, TR], F16)
    yo = mem(name + "yo", [P, 2, TR // P, D])
    ne = 1 if shared else E
    b1 = mem(name + "b1", [P, ne, nf])
    gate = mem(name + "gate", [P, ne, nf])
    b2 = mem(name + "b2", [P, ne, D])
    gs = mem(name + "gs", [P, ne, nf])
    gb = mem(name + "gb", [P, ne, nf])
    gst = mem(name + "gst", [P, 2, nf])
    gbt = mem(name + "gbt", [P, 2, nf])
    warm = mem(name + "warm", [P, 1])
    if shared:
        sw1 = mem("sw1", [P, KD, SF])
        sw2 = mem("sw2", [P, NSF, D])
        sw1h = mem("sw1h", [P, KD, SF], F16)
        sw1l = mem("sw1l", [P, KD, SF], F16)
        sw2h = mem("sw2h", [P, NSF, D], F16)
        sw2l = mem("sw2l", [P, NSF, D], F16)
        sh = mem("sh", [P, 1])
        she = mem("she", [P, 1])
        she1 = mem("she1", [P, 1])
        sgm = mem("sgm", [P, 1])
        sgs = mem("sgs", [P, 1])
        b2s = mem("b2s", [P, D])
    bank_t = psum[0:2]
    bank_u = psum[2:4]
    bank_y = (psum[4:6], psum[6:8])

    c_ld = sig(name + "c_ld")
    w_ld = sig(name + "w_ld")
    w_hi = sig(name + "w_hi")
    w_lo = sig(name + "w_lo")
    pre = sig(name + "pre")
    she_d = sig(name + "she")
    gs_d = sig(name + "gs")
    gt_d = sig(name + "gt", 1)
    x_ld = [sig(name + f"x_ld{b}", 16) for b in range(2)]
    t_ps = sig(name + "t_ps", 1)
    x_h = sig(name + "x_h", 1)
    x_l = sig(name + "x_l", 1)
    u_ps = sig(name + "u_ps", NP_)
    g_a = sig(name + "g_a", nf)
    g_h = sig(name + "g_h", NQ)
    g_l = sig(name + "g_l", NQ)
    y_ps = sig(name + "y_ps", 1)
    y_d = sig(name + "y_d", TR // P)
    y_st = [sig(name + f"y_st{b}", 16) for b in range(2)]
    b1_src, gate_src, b2_src = (a["sb1"], a["sgate"], a["sb2"]) if shared else (a["b1"], a["gate"], a["b2"])
    n_c = (4 if shared else 3) * 16

    def expert(eng, i):
        return None if shared else eng.value_load(tab[0:1, 0, bass.ds(i, 1)], min_val=0, max_val=E - 1)

    with nc.Block() as block:
        @block.sync
        def _(sp):
            def load(i, b):
                wait(sp, t_ps, t_ps.at(i, -1), True)
                at = i * TR if shared else sp.value_load(tab[0:1, 1, bass.ds(i, 1)], min_val=0, max_val=ZROW)
                sp.dma_start(xr[:, b], source[bass.ds(at, TR), :].rearrange("(t p) n -> p t n", p=P)).then_inc(x_ld[b].sem, 16)

            def body(i, b):
                if exists(i + 2, count):
                    load(i + 2, b)
                if exists(i - 1, count):
                    wait(sp, y_d, y_d.at(i - 1, TR // P), True)
                    sp.dma_start(target[bass.ds((i - 1) * TR, TR), :].rearrange("(t p) n -> p t n", p=P), yo[:, 1 - b]).then_inc(y_st[1 - b].sem, 16)

            if shared:
                sp.dma_start(sw1[:, :, :], a["sw1"].rearrange("(k p) n -> p k n", p=P)).then_inc(w_ld.sem, 16)
            load(0, 0)
            sp.dma_start(b1.rearrange("p e f -> p (e f)") if shared else b1, b1_src).then_inc(c_ld.sem, 16)
            sp.dma_start(gate.rearrange("p e f -> p (e f)") if shared else gate, gate_src).then_inc(c_ld.sem, 16)
            sp.dma_start(b2.rearrange("p e d -> p (e d)"), b2_src.partition_broadcast(P)).then_inc(c_ld.sem, 16)
            if shared:
                sp.dma_start(sh[:, :], a["shared"].partition_broadcast(P)).then_inc(c_ld.sem, 16)
                sp.wait_ge(w_ld.sem, 16)
                sp.dma_start(sw2[:, :, :], a["sw2"].rearrange("(f p) n -> p f n", p=P)).then_inc(w_ld.sem, 16)
            paired(sp, count, body)
            for b in range(2):
                sp.wait_ge(y_st[b].sem, y_st[b].at((count + 1 - b) // 2, 0))

        @block.tensor
        def _(pe):
            def body(i, b):
                if exists(i + 1, count):
                    wait(pe, x_ld[1 - b], x_ld[1 - b].at((i + 1) // 2, 16))
                    wait(pe, x_l, x_l.at(i, 0))
                    for k in range(KD):
                        for t in range(TR // P):
                            m = pe.transpose(bank_t[1 - b][:, k * TR + t * P:k * TR + (t + 1) * P], xr[:, 1 - b, t, k * P:(k + 1) * P], ident[:, :])
                    m.then_inc(t_ps.sem, 1)
                if exists(i, count):
                    e = expert(pe, i)
                    wait(pe, x_l, x_l.at(i, 1))
                    if shared:
                        pe.wait_ge(w_lo.sem, 1)
                    for p in range(NP_):
                        wait(pe, g_a, g_a.at(i, 2 * (p - 1)))
                        for f in (2 * p, 2 * p + 1):
                            out = bank_u[p % 2][:, (f % 2) * TR:(f % 2 + 1) * TR]
                            at = slice(f * P, (f + 1) * P)
                            for k in range(KD):
                                if shared:
                                    wh, wl = sw1h[:, k, at], sw1l[:, k, at]
                                else:
                                    wh, wl = (w[:, bass.ds(e, 1), k, at].rearrange("p e n -> p (e n)") for w in (g["w1h"], g["w1l"]))
                                pe.matmul(out, wh, xh[:, b, k], start=k == 0, stop=False)
                                pe.matmul(out, wh, xl[:, b, k], start=False, stop=False)
                                m = pe.matmul(out, wl, xh[:, b, k], start=False, stop=k == KD - 1)
                        m.then_inc(u_ps.sem, 1)
                if exists(i - 1, count):
                    e = expert(pe, i - 1)
                    wait(pe, y_d, y_d.at(i - 2, 0))
                    if shared:
                        pe.wait_ge(w_lo.sem, 2)
                    for f in range(nf):
                        if f % 4 == 0:
                            wait(pe, g_l, g_l.at(i - 1, f // 4 + 1))
                        if shared:
                            wh, wl = sw2h[:, f], sw2l[:, f]
                        else:
                            wh, wl = (w[:, bass.ds(e, 1), f].rearrange("p e n -> p (e n)") for w in (g["w2h"], g["w2l"]))
                        for t in range(TR // P):
                            at = slice(t * P, (t + 1) * P)
                            out = bank_y[1 - b][t][:, 0:D]
                            pe.matmul(out, gh[:, 1 - b, f, at], wh, start=f == 0, stop=False)
                            pe.matmul(out, gh[:, 1 - b, f, at], wl, start=False, stop=False)
                            m = pe.matmul(out, gl[:, 1 - b, f, at], wh, start=False, stop=f == nf - 1)
                    m.then_inc(y_ps.sem, 1)

            paired(pe, count, body)

        @block.scalar
        def _(act):
            def body(i, b):
                if exists(i + 1, count):
                    wait(act, t_ps, t_ps.at(i + 1, 1))
                    wait(act, u_ps, u_ps.at(i, 0))
                    act.activation(xh[:, 1 - b].rearrange("p k n -> p (k n)"), bank_t[1 - b][:, :], ACT.Copy).then_inc(x_h.sem, 1)
                if exists(i, count):
                    wait(act, gt_d, gt_d.at(i, 1))
                    for f in range(nf):
                        if f % 4 == 0:
                            wait(act, g_l, g_l.at(i - 1, f // 4 + 1))
                        if f % 2 == 0:
                            wait(act, u_ps, u_ps.at(i, f // 2 + 1))
                        act.activation(gel[:, f // 4, f % 4], bank_u[f // 2 % 2][:, (f % 2) * TR:(f % 2 + 1) * TR], ACT.Gelu,
                                       bias=gbt[:, b, f:f + 1], scale=gst[:, b, f:f + 1]).then_inc(g_a.sem, 1)

            if shared:
                act.wait_ge(c_ld.sem, n_c)
                act.activation(she[:, :], sh[:, :], ACT.Exp, scale=-1.0).then_inc(she_d.sem, 1)
                act.wait_ge(w_ld.sem, 16)
                act.activation(sw1h[:, :, :].rearrange("p k n -> p (k n)"), sw1[:, :, :].rearrange("p k n -> p (k n)"), ACT.Copy, scale=WS).then_inc(w_hi.sem, 1)
                act.wait_ge(w_ld.sem, 32)
                act.activation(sw2h[:, :, :].rearrange("p k n -> p (k n)"), sw2[:, :, :].rearrange("p k n -> p (k n)"), ACT.Copy, scale=WS).then_inc(w_hi.sem, 1)
            act.wait_ge(pre.sem, 1)
            act.activation(warm[:, :], warm[:, :], ACT.Gelu)
            paired(act, count, body)

        @block.vector
        def _(dve):
            def body(i, b):
                if exists(i + 1, count):
                    if not shared:
                        e = expert(dve, i + 1)
                        wait(dve, g_a, g_a.at(i, 0), True)
                        dve.tensor_copy(gst[:, 1 - b], gs[:, bass.ds(e, 1), :].rearrange("p e f -> p (e f)"))
                        dve.tensor_copy(gbt[:, 1 - b], gb[:, bass.ds(e, 1), :].rearrange("p e f -> p (e f)")).then_inc(gt_d.sem, 1)
                    wait(dve, x_h, x_h.at(i + 1, 1))
                    wait(dve, u_ps, u_ps.at(i, 0))
                    dve.tensor_tensor(xl[:, 1 - b].rearrange("p k n -> p (k n)"), bank_t[1 - b][:, :],
                                      xh[:, 1 - b].rearrange("p k n -> p (k n)"), ALU.subtract).then_inc(x_l.sem, 1)
                for c in range(NQ):
                    if exists(i, count):
                        part = slice(4 * c, 4 * c + 4)
                        wait(dve, g_a, g_a.at(i, 4 * c + 4))
                        wait(dve, y_ps, y_ps.at(i - 1, 0))
                        dve.tensor_copy(gh[:, b, part], gel[:, c]).then_inc(g_h.sem, 1)
                        wait(dve, g_h, g_h.at(i, c + 1))
                        dve.tensor_tensor(gl[:, b, part], gel[:, c], gh[:, b, part], ALU.subtract).then_inc(g_l.sem, 1)
                if exists(i - 1, count):
                    if not shared:
                        e = expert(dve, i - 1)
                    wait(dve, y_ps, y_ps.at(i - 1, 1))
                    wait(dve, y_st[1 - b], y_st[1 - b].at((i - 1) // 2, 0))
                    for t in range(TR // P):
                        bias = b2s[:, :] if shared else b2[:, bass.ds(e, 1), :].rearrange("p e d -> p (e d)")
                        dve.scalar_tensor_tensor(yo[:, 1 - b, t], bank_y[1 - b][t][:, 0:D], sgs[:, 0:1] if shared else 1.0 / WS,
                                                 bias, ALU.mult, ALU.add).then_inc(y_d.sem, 1)

            dve.memset(warm[:, :], 0.0).then_inc(pre.sem, 1)
            dve.wait_ge(c_ld.sem, n_c)
            dve.tensor_scalar(gs[:, :, :], gate[:, :, :], 1.0 / WS, None, ALU.mult).then_inc(gs_d.sem, 1)
            dve.tensor_tensor(gb[:, :, :], b1[:, :, :], gate[:, :, :], ALU.mult).then_inc(gs_d.sem, 1)
            dve.wait_ge(gs_d.sem, 2)
            if shared:
                for b in range(2):
                    dve.tensor_copy(gst[:, b], gs[:, 0])
                    m = dve.tensor_copy(gbt[:, b], gb[:, 0])
                m.then_inc(gt_d.sem, count)
                dve.wait_ge(she_d.sem, 1)
                dve.tensor_scalar(she1[:, :], she[:, :], 1.0, None, ALU.add).then_inc(gs_d.sem, 1)
                dve.wait_ge(gs_d.sem, 3)
                dve.reciprocal(sgm[:, :], she1[:, :]).then_inc(gs_d.sem, 1)
                dve.wait_ge(gs_d.sem, 4)
                dve.tensor_scalar(sgs[:, :], sgm[:, :], 1.0 / WS, None, ALU.mult).then_inc(gs_d.sem, 1)
                dve.tensor_scalar(b2s[:, :], b2[:, 0], sgm[:, 0:1], None, ALU.mult).then_inc(gs_d.sem, 1)
                for n, (l, w, h) in enumerate(((sw1l, sw1, sw1h), (sw2l, sw2, sw2h))):
                    dve.wait_ge(w_hi.sem, n + 1)
                    dve.scalar_tensor_tensor(l[:, :, :], w[:, :, :], WS, h[:, :, :], ALU.mult, ALU.subtract).then_inc(w_lo.sem, 1)
                dve.wait_ge(gs_d.sem, 6)
            paired(dve, count, body)


def load_toeplitz(sp, g, n):
    for part in range(2):
        flat = g["toe_d"][part]
        src = bass.AP(flat.tensor, flat.offset + n * CC * 2 * TAPS, [[1, P], [1, CC * 2 * TAPS]])
        sp.dma_start(g["toe"][:, n % RING, part].rearrange("p c u -> p (c u)"), src).then_inc(g["toe_ld"][n % RING].sem, 16)


def combine(nc, a, sig, mem, psum, g):
    slots, wts, x2, h3h, h3l = (g[n] for n in ("yslots", "wts", "x2", "h3h", "h3l"))
    count = NG2
    xin = mem("c_x", [P, 2, G2, D])
    shr = mem("c_sh", [P, 2, G2, D])
    yk = mem("c_yk", [P, 2, 2, G2, D])
    ix = mem("c_ix", [P, 2, G2, 2], I32)
    wk = mem("c_w", [P, 2, G2, 2])
    u = mem("c_u", [P, G2, D])
    ysum = mem("c_y", [P, 2, G2, D])
    z = mem("c_z", [P, 2, G2, D])
    xb = mem("c_xb", [P, 2, G2, D])
    h3 = mem("c_h3", [P, 2, G2, D])
    lng = mem("c_lng", [P, D])
    lnb = mem("c_lnb", [P, D])
    mhalf = mem("c_mhalf", [P, G2])
    st = [mem(f"c_st{k}", [P, G2, 6]) for k in range(2)]
    mv = [mem(f"c_mv{k}", [P, G2, 2]) for k in range(2)]
    ve = [mem(f"c_ve{k}", [P, G2]) for k in range(2)]
    nm = [mem(f"c_nm{k}", [P, G2]) for k in range(2)]
    rs = [mem(f"c_rs{k}", [P, G2]) for k in range(2)]
    nb = [mem(f"c_nb{k}", [P, G2]) for k in range(2)]

    c_ld = sig("c_ld")
    mh = sig("c_mh")
    x_ld = [sig(f"c_x_ld{b}", 2 * 16) for b in range(2)]
    ix_d = sig("c_ix_d", 1)
    wk_d = sig("c_wk_d", 1)
    yk_ld = [sig(f"c_yk_ld{b}", 2 * G2 * 16) for b in range(2)]
    u_d = sig("c_u_d", G2)
    y_d = sig("c_y_d", G2)
    bn = [sig(f"c_bn{k}", G2) for k in range(2)]
    mvs = [sig(f"c_mv{k}", G2) for k in range(2)]
    rsd = [sig(f"c_rs{k}", 4) for k in range(2)]
    z_d = sig("c_z_d", G2)
    zg_d = sig("c_zg", 1)
    xb_d = sig("c_xb_d", 1)
    x2_d = sig("c_x2", 1)
    h_d = sig("c_h", G2)
    hh_d = sig("c_hh", 1)
    hl_d = sig("c_hl", 1)
    wrap_d = sig("c_wrap")

    def rows(dram, i, b):
        return dram.rearrange("(b s p) n -> p b s n", p=P, s=SLOTS - 1)[:, 2 * b:2 * b + 2, bass.ds(i // 2, 1)].rearrange("p b s n -> p (b s) n")

    def tokens(table, i, b):
        return table.rearrange("p (b s) n -> p b s n", b=B)[:, 2 * b:2 * b + 2, bass.ds(i // 2, 1)].rearrange("p b s n -> p (b s) n")

    def slot(i):
        return bass.ds(B + i * G2, G2)

    with nc.Block() as block:
        @block.sync
        def _(sp):
            def load(i, b):
                wait(sp, y_d, y_d.at(i - 1, 0), True)
                wait(sp, xb_d, xb_d.at(i - 1, 0), True)
                sp.dma_start(xin[:, b], rows(g["x1_d"], i, b)).then_inc(x_ld[b].sem, 16)
                sp.dma_start(shr[:, b], rows(g["sh_d"], i, b)).then_inc(x_ld[b].sem, 16)

            def body(i, b):
                if exists(i + 2, count):
                    load(i + 2, b)

            sp.dma_start(lng[:, :], a["lng"].partition_broadcast(P)).then_inc(c_ld.sem, 16)
            sp.dma_start(lnb[:, :], a["lnb"].partition_broadcast(P)).then_inc(c_ld.sem, 16)
            load(0, 0)
            for n in range(RING):
                load_toeplitz(sp, g, n)
            paired(sp, count, body)
            sp.wait_ge(c_ld.sem, 32)

        @block.gpsimd
        def _(pool):
            def rstd(k, i):
                wait(pool, mvs[k], mvs[k].at(i, G2), True)
                wait(pool, (z_d, h_d)[k], (z_d, h_d)[k].at(i, 0), True)
                pool.tensor_scalar(ve[k][:, :], mv[k][:, :, 1], EPS, None, ALU.add).then_inc(rsd[k].sem, 1)
                pool.tensor_scalar(nm[k][:, :], mv[k][:, :, 0], -1.0, None, ALU.mult).then_inc(rsd[k].sem, 1)
                wait(pool, rsd[k], rsd[k].at(i, 2), True)
                pool.tensor_tensor(out=rs[k][:, :], in0=ve[k][:, :], in1=mhalf[:, :], op=ALU.pow).then_inc(rsd[k].sem, 1)
                wait(pool, rsd[k], rsd[k].at(i, 3), True)
                pool.tensor_tensor(out=nb[k][:, :], in0=nm[k][:, :], in1=rs[k][:, :], op=ALU.mult).then_inc(rsd[k].sem, 1)

            def gather(i, b):
                wait(pool, ix_d, ix_d.at(i, 1), True)
                wait(pool, y_d, y_d.at(i - 1, 0), True)
                for t in range(G2):
                    for k in range(2):
                        pool.indirect_dma_start(out=yk[:, b, k, t], out_offset=None, in_=g["ys_d"][:, :],
                                                in_offset=bass.IndirectOffsetOnAxis(ap=ix[:, b, t, k:k + 1], axis=0)).then_inc(yk_ld[b].sem, 16)

            def body(i, b):
                if exists(i, count):
                    rstd(0, i)
                if exists(i + 2, count):
                    gather(i + 2, b)
                if exists(i, count):
                    wait(pool, x_ld[b], x_ld[b].at(i // 2, 32), True)
                    wait(pool, x2_d, x2_d.at(i - 1, 0), True)
                    pool.tensor_tensor(out=xb[:, b], in0=xin[:, b], in1=lnb.unsqueeze(1).to_broadcast([P, G2, D]), op=ALU.add).then_inc(xb_d.sem, 1)
                if exists(i - 1, count):
                    rstd(1, i - 1)

            pool.memset(mhalf[:, :], -0.5).then_inc(mh.sem, 1)
            pool.wait_ge(mh.sem, 1)
            pool.wait_ge(c_ld.sem, 32)
            gather(0, 0)
            paired(pool, count, body)

        @block.scalar
        def _(act):
            def body(i, b):
                if exists(i, count):
                    wait(act, rsd[0], rsd[0].at(i, 4))
                    wait(act, zg_d, zg_d.at(i - 1, 0))
                    for t in range(G2):
                        act.activation(z[:, b, t], ysum[:, b, t], ACT.Identity, bias=nb[0][:, t:t + 1], scale=rs[0][:, t:t + 1]).then_inc(z_d.sem, 1)
                if exists(i - 1, count):
                    wait(act, rsd[1], rsd[1].at(i - 1, 4))
                    wait(act, hl_d, hl_d.at(i - 2, 0))
                    for t in range(G2):
                        act.activation(h3[:, 1 - b, t], x2[:, bass.ds((i - 1) * G2 + t, 1)].rearrange("p t n -> p (t n)"), ACT.Identity, bias=nb[1][:, t:t + 1], scale=rs[1][:, t:t + 1]).then_inc(h_d.sem, 1)
                    wait(act, h_d, h_d.at(i - 1, G2))
                    act.activation(h3h[:, slot(i - 1)].rearrange("p t n -> p (t n)"), h3[:, 1 - b].rearrange("p t n -> p (t n)"), ACT.Copy).then_inc(hh_d.sem, 1)

            paired(act, count, body)

        @block.vector
        def _(dve):
            def stats(k, i, x):
                for t in range(G2):
                    dve.bn_stats(st[k][:, t], x(t)).then_inc(bn[k].sem, 1)
                wait(dve, rsd[k], rsd[k].at(i, 0), True)
                for t in range(G2):
                    wait(dve, bn[k], bn[k].at(i, t + 1), True)
                    dve.bn_aggr(mv[k][:, t], st[k][:, t]).then_inc(mvs[k].sem, 1)

            def index(i, b):
                wait(dve, yk_ld[b], yk_ld[b].at(i // 2, 0))
                dve.tensor_copy(ix[:, b], tokens(slots, i, b)).then_inc(ix_d.sem, 1)
                wait(dve, y_d, y_d.at(i - 1, 0))
                dve.tensor_copy(wk[:, b], tokens(wts, i, b)).then_inc(wk_d.sem, 1)

            def body(i, b):
                if exists(i + 1, count):
                    n, c = i + 1, 1 - b
                    wait(dve, yk_ld[c], yk_ld[c].at(n // 2, 2 * G2 * 16))
                    wait(dve, x_ld[c], x_ld[c].at(n // 2, 32))
                    wait(dve, wk_d, wk_d.at(n, 1))
                    wait(dve, y_d, y_d.at(n, 0))
                    for t in range(G2):
                        dve.scalar_tensor_tensor(u[:, t], yk[:, c, 1, t], wk[:, c, t, 1:2], shr[:, c, t], ALU.mult, ALU.add).then_inc(u_d.sem, 1)
                    wait(dve, z_d, z_d.at(n - 1, 0))
                    for t in range(G2):
                        wait(dve, u_d, u_d.at(n, t + 1))
                        dve.scalar_tensor_tensor(ysum[:, c, t], yk[:, c, 0, t], wk[:, c, t, 0:1], u[:, t], ALU.mult, ALU.add).then_inc(y_d.sem, 1)
                    wait(dve, y_d, y_d.at(n, G2))
                    stats(0, n, lambda t: ysum[:, c, t])
                if exists(i + 3, count):
                    index(i + 3, 1 - b)
                if exists(i, count):
                    wait(dve, z_d, z_d.at(i, G2))
                    dve.tensor_tensor(z[:, b], z[:, b], lng.unsqueeze(1).to_broadcast([P, G2, D]), ALU.mult).then_inc(zg_d.sem, 1)
                    wait(dve, xb_d, xb_d.at(i, 1))
                    wait(dve, zg_d, zg_d.at(i, 1))
                    dve.tensor_tensor(x2[:, bass.ds(i * G2, G2)], z[:, b], xb[:, b], ALU.add).then_inc(x2_d.sem, 1)
                    wait(dve, x2_d, x2_d.at(i, 1), True)
                    stats(1, i, lambda t: x2[:, bass.ds(i * G2 + t, 1)].rearrange("p t n -> p (t n)"))
                if exists(i - 1, count):
                    wait(dve, hh_d, hh_d.at(i - 1, 1))
                    dve.tensor_tensor(h3l[:, slot(i - 1)], h3[:, 1 - b], h3h[:, slot(i - 1)], ALU.subtract).then_inc(hl_d.sem, 1)

            dve.wait_ge(c_ld.sem, 32)
            index(0, 0)
            index(1, 1)
            paired(dve, count, body)
            for h, s in ((h3h, hh_d), (h3l, hl_d)):
                dve.wait_ge(s.sem, count)
                dve.tensor_copy(h[:, 0:B], h[:, NT:NT + B]).then_inc(wrap_d.sem, 1)
            dve.wait_ge(wrap_d.sem, 2)


def convolve(nc, a, sig, mem, psum, g):
    ident, x2, h3h, h3l, toe, kmod = (g[n] for n in ("ident", "x2", "h3h", "h3l", "toe", "kmod"))
    hc = mem("v_hc", [P, 2, 2, CC, B * SLOTS], F16)
    ev = mem("v_ev", [P, 2, 4, P])
    prime = mem("v_prime", [P, 2])
    bank_c = psum[0:2]
    bank_r = psum[2:4]
    GC = CC // 4

    h_cp = sig("v_h_cp", 2)
    c_ps = sig("v_c_ps", 1)
    e_d = sig("v_e_d", 1)
    r_ps = sig("v_r_ps", 1)
    x_d = sig("v_x_d", 1)

    with nc.Block() as block:
        @block.sync
        def _(sp):
            for n in range(RING, NC):
                wait(sp, c_ps, n - RING + 1)
                load_toeplitz(sp, g, n)

        @block.scalar
        def _(act):
            with act.Fori(0, NC // RING) as q:
                for r in range(RING):
                    n = q * RING + r
                    wait(act, e_d, e_d.at(n, 1))
                    for part, h in enumerate((h3h, h3l)):
                        act.activation(hc[:, r % 2, part], h[:, :, bass.ds(n * CC, CC)].rearrange("p s c -> p c s"), ACT.Copy).then_inc(h_cp.sem, 1)

        @block.tensor
        def _(pe):
            def back(n, b):
                wait(pe, e_d, e_d.at(n, 3))
                wait(pe, x_d, x_d.at(n, 1))
                for k in range(GC):
                    m = pe.transpose(bank_r[b][:, k * P:(k + 1) * P], ev[:, b, k], ident[:, :])
                m.then_inc(r_ps.sem, 1)

            with pe.Fori(0, NC // RING) as q:
                for r in range(RING):
                    n = q * RING + r
                    b = r % 2
                    wait(pe, g["toe_ld"][r], g["toe_ld"][r].at(q, 32))
                    wait(pe, h_cp, h_cp.at(n, 2))
                    wait(pe, e_d, e_d.at(n, 1))
                    for c in range(CC):
                        out = bank_c[b][32 * (c % 4):32 * (c % 4) + 32, c // 4 * P:(c // 4 + 1) * P]
                        todo = []
                        for s in (1, 0):
                            hh, hl = (hc[:, b, part, c, s * B:s * B + NT] for part in range(2))
                            th, tl = (toe[:, r, part, c, s * P:(s + 1) * P] for part in range(2))
                            todo += [(hh, th), (hh, tl), (hl, th)]
                        for k, (x, w) in enumerate(todo):
                            m = pe.matmul(out, x, w, start=k == 0, stop=k == len(todo) - 1, tile_position=(0, 32 * (c % 4)))
                    m.then_inc(c_ps.sem, 1)
                    if r:
                        back(n - 1, 1 - b)
                back(q * RING + RING - 1, 1)

        @block.vector
        def _(dve):
            dve.memset(prime[:, 0:1], 0.0).then_inc(e_d.sem, 2)
            dve.memset(prime[:, 1:2], 0.0).then_inc(x_d.sem, 2)
            with dve.Fori(0, NC // RING) as q:
                def add(n, b):
                    wait(dve, r_ps, r_ps.at(n, 1))
                    v = x2[:, :, bass.ds(n * CC, CC)].rearrange("p t (g j) -> p t g j", j=4)
                    dve.tensor_tensor(v, bank_r[b].rearrange("p (g j t) -> p t g j", g=GC, j=4), v, ALU.add).then_inc(x_d.sem, 1)

                for r in range(RING):
                    n = q * RING + r
                    wait(dve, c_ps, c_ps.at(n, 1))
                    dve.tensor_tensor(ev[:, r % 2, :, ::-1], bank_c[r % 2].rearrange("p (g u) -> p g u", u=P),
                                      kmod[:, bass.ds(n * GC, GC)].unsqueeze(2).to_broadcast([P, GC, P]), ALU.mult).then_inc(e_d.sem, 1)
                    if r:
                        add(n - 1, (r - 1) % 2)
                add(q * RING + RING - 1, 1)


def project(nc, a, sig, mem, psum, g):
    ident, x3, sgn = g["ident"], g["x2"], g["sgn"]
    count = NG2
    h = mem("f_h", [P, 2, G2, D])
    th = mem("f_th", [P, 2, KD, G2 * P], F16)
    tl = mem("f_tl", [P, 2, KD, G2 * P], F16)
    yo = mem("f_y", [P, 2, G2, D])
    mhalf = mem("f_mhalf", [P, G2])
    st = mem("f_st", [P, G2, 6])
    mv = mem("f_mv", [P, G2, 2])
    ve = mem("f_ve", [P, G2])
    nm = mem("f_nm", [P, G2])
    rs = mem("f_rs", [P, 2, G2])
    nb = mem("f_nb", [P, 2, G2])
    bank_t = psum[0:2]
    bank_o = psum[2:4]

    mh = sig("f_mh")
    bn = sig("f_bn", G2)
    mvs = sig("f_mv", G2)
    rsd = sig("f_rs", 4)
    h_d = sig("f_h", G2)
    t_ps = sig("f_t_ps", 1)
    t_h = sig("f_t_h", 1)
    t_l = sig("f_t_l", 1)
    o_ps = sig("f_o_ps", 1)
    y_d = sig("f_y_d", 1)
    y_st = [sig(f"f_y_st{b}", 16) for b in range(2)]

    with nc.Block() as block:
        @block.sync
        def _(sp):
            def body(i, b):
                if exists(i, count):
                    wait(sp, y_d, y_d.at(i, 1), True)
                    sp.dma_start(a["out"].rearrange("(b s p) n -> p b s n", p=P, s=SLOTS - 1)[:, 2 * b:2 * b + 2, bass.ds(i // 2, 1)].rearrange("p b s n -> p (b s) n"), yo[:, b]).then_inc(y_st[b].sem, 16)

            paired(sp, count, body)
            for b in range(2):
                sp.wait_ge(y_st[b].sem, y_st[b].at(count // 2, 0))

        @block.gpsimd
        def _(pool):
            def body(i, b):
                if exists(i + 1, count):
                    n, c = i + 1, 1 - b
                    wait(pool, mvs, mvs.at(n, G2), True)
                    wait(pool, h_d, h_d.at(n - 1, 0), True)
                    pool.tensor_scalar(ve[:, :], mv[:, :, 1], EPS, None, ALU.add).then_inc(rsd.sem, 1)
                    pool.tensor_scalar(nm[:, :], mv[:, :, 0], -1.0, None, ALU.mult).then_inc(rsd.sem, 1)
                    wait(pool, rsd, rsd.at(n, 2), True)
                    pool.tensor_tensor(out=rs[:, c], in0=ve[:, :], in1=mhalf[:, :], op=ALU.pow).then_inc(rsd.sem, 1)
                    wait(pool, rsd, rsd.at(n, 3), True)
                    pool.tensor_tensor(out=nb[:, c], in0=nm[:, :], in1=rs[:, c], op=ALU.mult).then_inc(rsd.sem, 1)

            pool.memset(mhalf[:, :], -0.5).then_inc(mh.sem, 1)
            pool.wait_ge(mh.sem, 1)
            paired(pool, count, body)

        @block.scalar
        def _(act):
            def body(i, b):
                if exists(i + 1, count):
                    n, c = i + 1, 1 - b
                    wait(act, rsd, rsd.at(n, 4))
                    wait(act, t_ps, t_ps.at(n - 1, 0))
                    for t in range(G2):
                        act.activation(h[:, c, t], x3[:, bass.ds(n * G2 + t, 1)].rearrange("p t n -> p (t n)"), ACT.Identity,
                                       bias=nb[:, c, t:t + 1], scale=rs[:, c, t:t + 1]).then_inc(h_d.sem, 1)
                if exists(i, count):
                    wait(act, t_ps, t_ps.at(i, 1))
                    wait(act, o_ps, o_ps.at(i - 1, 0))
                    act.activation(th[:, b].rearrange("p k n -> p (k n)"), bank_t[b][:, :], ACT.Copy).then_inc(t_h.sem, 1)

            paired(act, count, body)

        @block.tensor
        def _(pe):
            def body(i, b):
                if exists(i + 1, count):
                    n, c = i + 1, 1 - b
                    wait(pe, h_d, h_d.at(n, G2))
                    wait(pe, t_l, t_l.at(n - 1, 0))
                    for k in range(KD):
                        for t in range(G2):
                            m = pe.transpose(bank_t[c][:, (k * G2 + t) * P:(k * G2 + t + 1) * P], h[:, c, t, k * P:(k + 1) * P], ident[:, :])
                    m.then_inc(t_ps.sem, 1)
                if exists(i, count):
                    wait(pe, t_l, t_l.at(i, 1))
                    wait(pe, y_d, y_d.at(i - 1, 0))
                    for t in range(G2):
                        at = slice(t * P, (t + 1) * P)
                        todo = [(x[:, b, k, at], sgn[:, k]) for k in range(KD) for x in (th, tl)]
                        for n, (x, w) in enumerate(todo):
                            m = pe.matmul(bank_o[b][:, t * D:(t + 1) * D], x, w, start=n == 0, stop=n == len(todo) - 1)
                    m.then_inc(o_ps.sem, 1)

            paired(pe, count, body)

        @block.vector
        def _(dve):
            def body(i, b):
                if exists(i + 2, count):
                    n = i + 2
                    wait(dve, mvs, mvs.at(n, 0), True)
                    for t in range(G2):
                        dve.bn_stats(st[:, t], x3[:, bass.ds(n * G2 + t, 1)].rearrange("p t n -> p (t n)")).then_inc(bn.sem, 1)
                    wait(dve, rsd, rsd.at(n, 0), True)
                    for t in range(G2):
                        wait(dve, bn, bn.at(n, t + 1), True)
                        dve.bn_aggr(mv[:, t], st[:, t]).then_inc(mvs.sem, 1)
                if exists(i, count):
                    wait(dve, t_h, t_h.at(i, 1))
                    wait(dve, o_ps, o_ps.at(i - 1, 0))
                    dve.tensor_tensor(tl[:, b].rearrange("p k n -> p (k n)"), bank_t[b][:, :], th[:, b].rearrange("p k n -> p (k n)"), ALU.subtract).then_inc(t_l.sem, 1)
                if exists(i - 1, count):
                    n, c = i - 1, 1 - b
                    wait(dve, o_ps, o_ps.at(n, 1))
                    wait(dve, y_st[c], y_st[c].at(n // 2, 0))
                    dve.tensor_tensor(yo[:, c], bank_o[c].rearrange("p (t n) -> p t n", n=D), x3[:, bass.ds(n * G2, G2)], ALU.add).then_inc(y_d.sem, 1)

            for t in range(G2):
                dve.bn_stats(st[:, t], x3[:, t]).then_inc(bn.sem, 1)
            for t in range(G2):
                dve.wait_ge(bn.sem, t + 1)
                dve.bn_aggr(mv[:, t], st[:, t]).then_inc(mvs.sem, 1)
            paired(dve, count, body)


def layouts(inputs):
    import numpy as np

    f = {k: np.asarray(v) for k, v in inputs.items()}
    order = np.array([(2 * (2 * pp + mt) + half) * HD + r
                      for mt in range(KD) for half in range(2) for r in range(HD) for pp in range(4)])
    wk, wv = f["L0_xattn_Wkv"][:D], f["L0_xattn_Wkv"][D:]
    bk, bv = f["L0_xattn_bkv"][:D], f["L0_xattn_bkv"][D:]
    row = np.arange(P)
    owner = row // 64 * 4 + row % 4
    out = {
        "x": f["x"].reshape(T, D),
        "ctxT": f["ctx_1024"].reshape(B * L, D).T,
        "wqT": f["L0_xattn_Wq"][order].T,
        "wkT": wk[order].T,
        "wvT": wv.T,
        "woT": f["L0_xattn_Wo"].T,
        "bq": f["L0_xattn_bq"][order].reshape(KD, P).T,
        "bk": bk[order].reshape(KD, P).T,
        "bv": bv[None],
        "bo": f["L0_xattn_bo"][None],
        "rw": f["L0_ffn_router_w"],
        "rb": f["L0_ffn_router_b"][None],
        "w1": f["L0_ffn_w1"],
        "w2": f["L0_ffn_w2"],
        "b1": f["L0_ffn_b1"].reshape(E, NF, P).transpose(2, 0, 1),
        "gate": f["L0_ffn_gate"].reshape(E, NF, P).transpose(2, 0, 1),
        "b2": f["L0_ffn_b2"].reshape(1, E * D),
        "sw1": f["L0_ffn_sw1"],
        "sw2": f["L0_ffn_sw2"],
        "sb1": f["L0_ffn_sb1"].reshape(NSF, P).T,
        "sgate": f["L0_ffn_sgate"].reshape(NSF, P).T,
        "sb2": f["L0_ffn_sb2"][None],
        "shared": f["L0_ffn_shared_weight"].reshape(1, 1),
        "lng": f["L0_ffn_ln_g"][None],
        "lnb": f["L0_ffn_ln_b"][None],
        "taps": f["L1_xattn_weight"][:, ::-1],
        "kpT": f["L1_xattn_kp_w"].T,
        "kpb": f["L1_xattn_kp_b"][None],
        "sgT": f["L1_ffn_weight"].T,
        "ident": np.eye(P, dtype=np.float32),
        "lower": np.triu(np.ones((P, P), np.float16), 1),
        "ones": np.ones((P, P), np.float16),
        "iota8": np.tile(np.arange(E, dtype=np.float32), (P, 1)),
        "rows": np.arange(TR, dtype=np.float32).reshape(TR // P, P).T,
        "tiles": np.arange(MT + 1, dtype=np.float32)[None].repeat(P, 0),
        "mask": (owner[:, None] == np.arange(8)).astype(np.float32),
        "negone": np.full((1, NPAIR * B * L), -PSC, np.float16),
    }
    return {k: np.ascontiguousarray(v) for k, v in out.items()}


def kernel(**inputs):
    import numpy as np
    import concourse.bacc as bacc
    from concourse.bass_utils import run_bass_kernel_spmd

    nc = bacc.Bacc("TRN2", target_bir_lowering=False, num_devices=1)
    arrays = layouts(inputs)
    aps = {k: nc.dram_tensor(f"in_{k}", v.shape, mybir.dt.from_np(v.dtype), kind="ExternalInput").ap()
           for k, v in arrays.items()}
    aps["out"] = nc.dram_tensor("out", (T, D), F32, kind="ExternalOutput").ap()
    build(nc, aps)
    r = run_bass_kernel_spmd(nc, [{f"in_{k}": v for k, v in arrays.items()}], core_ids=[0])
    return r.results[0]["out"].reshape(B, N, D)
```

```python
import concourse.bass as bass
from concourse import mybir

F32 = mybir.dt.float32
F16 = mybir.dt.float16
I32 = mybir.dt.int32
U32 = mybir.dt.uint32
ACT = mybir.ActivationFunctionType
ALU = mybir.AluOpType
AX = mybir.AxisListType

P = 128
B, N, D = 4, 1024, 256
T = B * N
KD = D // P
NT = T // P
GT = 4
GN = GT * P
NG = T // GN
L = 77
H, HD = 16, 16
NPAIR = H // 2
HV = HD + 1
E, FF, SF = 8, 1024, 512
NF, NSF = FF // P, SF // P
TR = 256
REG = T + TR
MT = T * 2 // TR + E - 1
ZROW = E * REG
TAPS = 128
EPS = 1e-5
WS = 64.0
PSC = 16.0
QK_SCALE = 1.0 / HD ** 0.5
G2 = 2
NG2 = NT // G2
SLOTS = N // P + 1
CC = 16
NC = D // CC
RING = 4
CH = 512


LAG = 3
LO_LAG = 2
LO_DVE = (3, 4, 7, 13, 14)
SCATTER = (14, 14, 15, 16, 17, 19, 19, 20)
AT = {
    "rs_c": 6, "ha": 0, "yth1": 3, "hth": 1, "qh": 3, "h2": 6, "cth": 7, "yth0": 13, "eg": 11,
    "values1": 0, "htl": 0, "ytl1": 2, "res1": 4, "ql": 2, "values0": 10, "ctl": 7, "logits": 8,
    "ytl0": 13, "top2": 9, "res0": 15, "place": 11, "yt1": 3, "at": 2, "out1": 4, "q": 3,
    "ct": 7, "lg": 8, "yt0": 11, "out0": 15, "pf": 11, "mm": 6, "mxd": 6, "st_a": 0, "rs_a": 0,
    "mts0": 9, "mts1": 13,
}


class Sig:

    def __init__(self, sem, per, steady=None):
        self.sem, self.per, self.steady = sem, per, steady

    def at(self, step, n):
        return step * self.per + n


class Memory:

    def __init__(self, nc, start, names=None):
        self.nc, self.at, self.names = nc, start, {} if names is None else names

    def __call__(self, name, shape, dt=F32):
        size = 4 if dt in (F32, I32, U32) else 2
        for n in shape[1:]:
            size *= n
        self.at = (self.at + 63) // 64 * 64
        ap = self.nc.alloc_sbuf_tensor_at(name, shape, dt, offset=self.at).ap()
        self.at += size
        assert self.at <= self.nc.sbuf_usable_end, (name, self.at)
        self.names[name] = ap
        return ap


def wait(eng, s, v, alone=False):
    if not isinstance(v, int) or v > 0:
        if not isinstance(v, int) and alone:
            v = eng.to_reg(v)
            eng.wait_ge(s.steady, 1)
        eng.wait_ge(s.sem, v)


def passes(pe, out, pairs, first=True):
    todo = [(x, z) for xh, xl, zh, zl in pairs for x, z in ((xh, zh), (xh, zl), (xl, zh))]
    for n, (x, z) in enumerate(todo):
        m = pe.matmul(out, x, z, start=first and n == 0, stop=n == len(todo) - 1)
    return m


def build(nc, a):
    g = {}

    def dram(name, shape, dt=F32):
        g[name] = nc.dram_tensor(name, shape, dt, kind="Internal").ap()

    steady = nc.alloc_semaphore("steady")

    signals = []

    def sig(name, per=1):
        signals.append(nc.alloc_semaphore(name))
        return Sig(signals[-1], per, steady)

    dram("ks_d", [B, P, H * L], F16)
    dram("kb_d", [B, P, KD * 8 * L], F16)
    dram("v_d", [B, L, 2 * H * HV], F16)
    dram("kx_d", [2, 3, 64, KD * B * L], F16)
    dram("qx_d", [2, 4, 64, KD * GN], F16)
    dram("x1_d", [T, D])
    dram("h2_d", [T, D])
    dram("xs_d", [ZROW + TR, D])
    dram("ys_d", [MT * TR, D])
    dram("sw_d", [P, 4, KD * SF], F16)
    dram("toe_d", [2, TAPS + D * 2 * TAPS], F16)

    keep = Memory(nc, nc.sbuf_base, g)
    keep("ident", [P, P])
    keep("bo", [1, 2, D], F16)
    keep("rb", [P, E])
    keep("bq", [P, KD])
    keep("rwh", [P, KD, E], F16)
    keep("rwl", [P, KD, E], F16)
    keep("lower", [P, P], F16)
    keep("ones", [P, P], F16)
    keep("iota8", [P, E])
    keep("sgn", [P, KD, D], F16)
    keep("kmod", [P, D // 4])
    keep("slots", [P, NT, 2], I32)
    keep("wts", [P, NT, 2])
    keep("cnt", [P, E])
    keep("start", [P, E])
    keep("before", [P, E])
    keep("tab", [1, 2, MT + 1], I32)
    keep("yslots", [P, NT, 2], I32)
    keep("woh", [P, KD, D], F16)
    keep("wol", [P, KD, D], F16)
    keep("wqh", [P, KD, D], F16)
    keep("wql", [P, KD, D], F16)
    small = keep.at
    keep("w1h", [P, E, KD, FF], F16)
    keep("w1l", [P, E, KD, FF], F16)
    keep("w2h", [P, E, NF, D], F16)
    keep("w2l", [P, E, NF, D], F16)
    free = keep.at
    late = Memory(nc, small, g)
    late("x2", [P, NT, D])
    late("h3h", [P, B * SLOTS, D], F16)
    late("h3l", [P, B * SLOTS, D], F16)
    late("toe", [P, RING, 2, CC, 2 * TAPS], F16)
    mid = Memory(nc, max(free, late.at), g)
    mid("sw", [P, 4, KD * SF], F16)
    mid("sgst", [P, 2, NSF])
    mid("sgbt", [P, 2, NSF])
    mid("sgs", [P, 1])
    mid("b2p", [1, 2, D], F16)

    psum = [nc.alloc_psum_tensor(f"bank{i}", [P, 512], F32).ap() for i in range(8)]

    g["stored"] = (sig("stored_sp"), sig("stored_act"))
    attention = Memory(nc, free, g)
    attention("xa", [P, GT, D])
    g["xa_ld"] = sig("xa_ld", 16)
    phase0(nc, a, sig, Memory(nc, small), psum, g)
    phase1(nc, a, sig, Memory(nc, attention.at), psum, g)
    done = list(signals)
    experts(nc, a, sig, Memory(nc, mid.at), psum, g, done)
    for s in done:
        nc.release_semaphore(s)
    g["toe_ld"] = [sig(f"toe_ld{r}", 2 * 16) for r in range(RING)]
    combine(nc, a, sig, Memory(nc, mid.at), psum, g)
    convolve(nc, a, sig, Memory(nc, late.at), psum, g)
    project(nc, a, sig, Memory(nc, late.at), psum, g)


def phase0(nc, a, sig, mem, psum, g):
    (ident, woh, wol, wqh, wql, bq, bo, rwh, rwl, rb, lower, ones, iota8, sgn, kmod) = (
        g[n] for n in ("ident woh wol wqh wql bq bo rwh rwl rb lower ones iota8 sgn kmod").split())
    ks_d, kb_d, v_d, kx_d, toe_d = (g[n] for n in "ks_d kb_d v_d kx_d toe_d".split())
    BL = B * L
    w3 = mem("w3", [P, 5, KD, D])
    sg = mem("sg", [P, KD, D])
    sg2 = mem("sg2", [P, KD, D])
    rw = mem("rw", [P, KD, E])
    ctxt = mem("ctxt", [P, KD, BL])
    bk = mem("bk", [P, KD])
    bv = mem("bv", [L, D])
    kpb = mem("kpb", [P, D])
    mask = mem("mask", [P, 8])
    kt = mem("kt", [P, KD, BL])
    kh = mem("kh", [P, KD, BL], F16)
    kl = mem("kl", [P, KD, BL], F16)
    kbd = mem("kbd", [P, KD, 8, BL], F16)
    kst = mem("kst", [P, 2, NPAIR, BL], F16)
    v = mem("v", [L, B, D])
    vhl = mem("vhl", [L, B, 2, H, HV], F16)
    mean = mem("mean", [P, KD, B])
    meanb = mem("meanb", [P, KD, 4, 8, B])
    km = mem("km", [P, D])
    tw = mem("tw", [P, KD, TAPS])
    twp = mem("twp", [P, 2, KD, 2 * TAPS], F16)
    zt = mem("zt", [P, D], F32)
    zh = mem("zh", [60, KD * GN], F16)
    one = mem("one", [P, 1])
    bq0 = mem("bq0", [P, KD])
    bo0 = mem("bo0", [1, D])
    sw = mem("sw32", [P, 2, KD * SF])
    swp = mem("swp", [P, 4, KD * SF], F16)
    pk = [psum[0][:, 0:BL], psum[1][:, 0:BL]]
    pv = [psum[2][0:L, 0:D], psum[3][0:L, 0:D], psum[4][0:L, 0:D], psum[5][0:L, 0:D]]
    pm = psum[6][:, 0:D]

    loaded_w = sig("loaded_w")
    loaded_c = sig("loaded_c")
    zeroed = sig("zeroed")
    k_ps = sig("k_ps")
    v_ps = sig("v_ps")
    km_ps = sig("km_ps")
    kt_done = sig("kt_done")
    kh_done = sig("kh_done")
    kl_done = sig("kl_done")
    kb_done = sig("kb_done")
    v_done = sig("v_done")
    vh_done = sig("vh_done")
    vl_done = sig("vl_done")
    mean_done = sig("mean_done")
    meanb_done = sig("meanb_done")
    km_done = sig("km_done")
    part_hi = sig("part_hi")
    part_lo = sig("part_lo")
    tw_hi = sig("tw_hi")
    tw_lo = sig("tw_lo")
    sg_done = sig("sg_done")
    bo_hi = sig("bo_hi")
    sw_hi = sig("sw_hi")
    sw_lo = sig("sw_lo")
    kx_st = sig("kx_st")
    ks_ld = sig("ks_ld")
    ks_st = sig("ks_st")
    out0, out_a = g["stored"]

    with nc.Block() as block:
        @block.sync
        def _(sp):
            n_w = n_c = 0
            for dst, src in ((ctxt, a["ctxT"].rearrange("(k p) n -> p k n", p=P)),
                             (w3[:, 2], a["wkT"].rearrange("(k p) n -> p k n", p=P)),
                             (bk, a["bk"]), (mask, a["mask"]),
                             (w3[:, 3], a["wvT"].rearrange("(k p) n -> p k n", p=P)),
                             (bv, a["bv"].partition_broadcast(L)),
                             (w3[:, 4], a["kpT"].rearrange("(k p) n -> p k n", p=P)),
                             (kpb, a["kpb"].partition_broadcast(P))):
                sp.dma_start(dst, src).then_inc(loaded_c.sem, 16)
                n_c += 16
            sp.dma_start(g["xa"], a["x"][0:GN, :].rearrange("(t p) n -> p t n", p=P)).then_inc(g["xa_ld"].sem, 16)
            for dst, src in ((w3[:, 0], a["wqT"].rearrange("(k p) n -> p k n", p=P)),
                             (w3[:, 1], a["woT"].rearrange("(k p) n -> p k n", p=P)),
                             (sg, a["sgT"].rearrange("(k p) n -> p k n", p=P)),
                             (rw, a["rw"].rearrange("(k p) n -> p k n", p=P)),
                             (tw, a["taps"].rearrange("(k p) n -> p k n", p=P)),
                             (ident, a["ident"]), (bq0, a["bq"]), (lower, a["lower"]),
                             (ones, a["ones"]), (iota8, a["iota8"]),
                             (bo0, a["bo"]),
                             (rb, a["rb"].partition_broadcast(P)),
                             (sw[:, 0].rearrange("p (k n) -> p k n", k=KD), a["sw1"].rearrange("(k p) n -> p k n", p=P)),
                             (sw[:, 1].rearrange("p (k n) -> p k n", k=NSF), a["sw2"].rearrange("(k p) n -> p k n", p=P))):
                sp.dma_start(dst, src).then_inc(loaded_w.sem, 16)
                n_w += 16
            assert (n_c, n_w) == (8 * 16, 14 * 16)
            sp.wait_ge(kh_done.sem, KD)
            for part in range(2):
                sp.dma_start(kx_d[0, part], kh[0:64].rearrange("p k n -> p (k n)")).then_inc(kx_st.sem, 16)
                sp.dma_start(kx_d[1, part], kh[64:128].rearrange("p k n -> p (k n)")).then_inc(kx_st.sem, 16)
            sp.wait_ge(kl_done.sem, KD)
            sp.dma_start(kx_d[0, 2], kl[0:64].rearrange("p k n -> p (k n)")).then_inc(kx_st.sem, 16)
            sp.dma_start(kx_d[1, 2], kl[64:128].rearrange("p k n -> p (k n)")).then_inc(kx_st.sem, 16)
            sp.wait_ge(kx_st.sem, 6 * 16)
            sp.wait_ge(zeroed.sem, 1)
            for half in range(2):
                src = kx_d[half].rearrange("s (r q) n -> (s r) (q n)", q=4)
                sp.dma_start(kst[64 * half:64 * half + 48, half].rearrange("p a n -> p (a n)"),
                             src).then_inc(ks_ld.sem, 16)
                sp.dma_start(kst[64 * half + 48:64 * half + 49, half].rearrange("p a n -> p (a n)"),
                             a["negone"]).then_inc(ks_ld.sem, 16)
            sp.wait_ge(ks_ld.sem, 4 * 16)
            for b in range(B):
                sp.dma_start(ks_d[b].rearrange("p (h l) -> p h l", l=L),
                             kst[:, :, :, b * L:(b + 1) * L].rearrange("p a b l -> p (a b) l")
                             ).then_inc(out0.sem, 16)

        @block.tensor
        def _(pe):
            pe.wait_ge(loaded_c.sem, 8 * 16)
            for mt in range(KD):
                for k in range(KD):
                    m = pe.matmul(pk[mt], w3[:, 2, k, mt * P:(mt + 1) * P], ctxt[:, k], start=k == 0, stop=k == KD - 1)
                m.then_inc(k_ps.sem, 1)
            for b in range(B):
                for k in range(KD):
                    m = pe.matmul(pv[b], ctxt[:, k, b * L:(b + 1) * L], w3[:, 3, k], start=k == 0, stop=k == KD - 1)
                m.then_inc(v_ps.sem, 1)
            pe.wait_ge(meanb_done.sem, KD * 4)
            for k in range(KD):
                m = pe.matmul(pm, meanb[:, k].rearrange("p j i b -> p (j i b)"), w3[:, 4, k], start=k == 0, stop=k == KD - 1)
            m.then_inc(km_ps.sem, 1)

        @block.scalar
        def _(act):
            for mt in range(KD):
                act.wait_ge(k_ps.sem, mt + 1)
                act.activation(kt[:, mt], pk[mt], ACT.Identity, bias=bk[:, mt:mt + 1]).then_inc(kt_done.sem, 1)
            for mt in range(KD):
                act.wait_ge(kt_done.sem, mt + 1)
                act.activation(kh[:, mt], kt[:, mt], ACT.Copy).then_inc(kh_done.sem, 1)
            for b in range(B):
                act.wait_ge(v_done.sem, b + 1)
                m = act.activation(vhl[:, b, 0, :, 0:HD], v[:, b].rearrange("p (h d) -> p h d", d=HD), ACT.Copy)
            m.then_inc(vh_done.sem, 1)
            act.wait_ge(loaded_w.sem, 14 * 16)
            for k in range(2):
                act.activation(swp[:, 2 * k], sw[:, k], ACT.Copy, scale=WS).then_inc(sw_hi.sem, 1)
            act.wait_ge(kb_done.sem, KD * 8)
            for b in range(B):
                act.dma_start(kb_d[b].rearrange("p (h l) -> p h l", l=L),
                             kbd[:, :, :, b * L:(b + 1) * L].rearrange("p a b l -> p (a b) l")
                             ).then_inc(out_a.sem, 16)
            act.wait_ge(vh_done.sem, 1)
            act.wait_ge(vl_done.sem, 1)
            for b in range(B):
                act.dma_start(v_d[b], vhl[:, b].rearrange("p a h v -> p (a h v)")).then_inc(out_a.sem, 16)
            act.wait_ge(tw_lo.sem, 1)
            act.wait_ge(tw_hi.sem, 1)
            for part in range(2):
                act.dma_start(toe_d[part:part + 1, 0:TAPS], twp[0:1, part, 0, TAPS:2 * TAPS]).then_inc(out_a.sem, 16)
                act.dma_start(toe_d[part, TAPS:].rearrange("(k p n) -> p k n", p=P, k=KD),
                             twp[:, part]).then_inc(out_a.sem, 16)
            act.dma_start(g["xs_d"][ZROW:ZROW + TR].rearrange("(k p) n -> p k n", p=P),
                         zt.unsqueeze(1).to_broadcast([P, 2, D])).then_inc(out_a.sem, 16)
            for half in range(2):
                act.dma_start(g["qx_d"][half, 3, 4:64], zh[:, :]).then_inc(out_a.sem, 16)
            act.wait_ge(sw_lo.sem, 2)
            act.dma_start(g["sw_d"], swp[:, :, :]).then_inc(out_a.sem, 16)


        @block.gpsimd
        def _(pool):
            pool.memset(kst[:, :, :, :], 0.0).then_inc(zeroed.sem, 1)
            pool.memset(one[:, :], 0.0).then_inc(zeroed.steady, 1)

        @block.vector
        def _(dve):
            dve.memset(zt[:, :], 0.0)
            dve.memset(vhl[:, :, 0, :, HD:HV], 1.0)
            dve.memset(vhl[:, :, 1, :, HD:HV], 0.0)
            dve.memset(zh[:, :], 0.0)
            dve.memset(twp[:, :, :, TAPS:], 0.0)
            dve.wait_ge(loaded_c.sem, 8 * 16)
            dve.tensor_reduce(mean[:, :, :], ctxt.rearrange("p k (b l) -> p k b l", l=L), axis=AX.X, op=ALU.add).then_inc(mean_done.sem, 1)
            dve.wait_ge(mean_done.sem, 1)
            for k in range(KD):
                for j in range(4):
                    dve.tensor_scalar(meanb[:, k, j], mean[:, k].unsqueeze(1).to_broadcast([P, 8, B]), 1.0 / L, None, ALU.mult).then_inc(meanb_done.sem, 1)
            for mt in range(KD):
                dve.wait_ge(kt_done.sem, mt + 1)
                dve.wait_ge(kh_done.sem, mt + 1)
                dve.tensor_tensor(kl[:, mt], kt[:, mt], kh[:, mt], ALU.subtract).then_inc(kl_done.sem, 1)
                for j in range(8):
                    dve.tensor_scalar(kbd[:, mt, j], kh[:, mt], mask[:, j:j + 1], None, ALU.mult).then_inc(kb_done.sem, 1)
            for b in range(B):
                dve.wait_ge(v_ps.sem, b + 1)
                dve.tensor_tensor(v[:, b], pv[b], bv[:, :], ALU.add).then_inc(v_done.sem, 1)
            dve.wait_ge(v_done.sem, B)
            dve.wait_ge(vh_done.sem, 1)
            for b in range(B):
                m = dve.tensor_tensor(vhl[:, b, 1, :, 0:HD], v[:, b].rearrange("p (h d) -> p h d", d=HD), vhl[:, b, 0, :, 0:HD], ALU.subtract)
            m.then_inc(vl_done.sem, 1)
            dve.wait_ge(km_ps.sem, 1)
            dve.tensor_tensor(km[:, :], pm, kpb[:, :], ALU.add).then_inc(km_done.sem, 1)
            dve.wait_ge(km_done.sem, 1)
            for j in range(4):
                dve.tensor_copy(kmod[32 * j:32 * j + 32, :], km[32 * j:32 * j + 32, j::4])
            dve.wait_ge(loaded_w.sem, 14 * 16)
            dve.tensor_scalar(bq[:, :], bq0[:, :], PSC, None, ALU.mult)
            dve.tensor_scalar(bo[:, 0], bo0[:, :], PSC, None, ALU.mult).then_inc(bo_hi.sem, 1)
            dve.wait_ge(bo_hi.sem, 1)
            dve.scalar_tensor_tensor(bo[:, 1], bo0[:, :], PSC, bo[:, 0], ALU.mult, ALU.subtract)
            dve.tensor_scalar(g["cnt"][:, :], iota8[:, :], float(REG), None, ALU.mult)
            parts = ((wqh, wql, w3[:, 0]), (woh, wol, w3[:, 1]), (rwh, rwl, rw[:, :, :]))
            for hi, lo, w in parts:
                dve.tensor_scalar(hi[:, :, :], w, PSC, None, ALU.mult).then_inc(part_hi.sem, 1)
            for n, (hi, lo, w) in enumerate(parts):
                dve.wait_ge(part_hi.sem, n + 1)
                dve.scalar_tensor_tensor(lo[:, :, :], w, PSC, hi[:, :, :], ALU.mult, ALU.subtract)
            dve.tensor_copy(twp[:, 0, :, 0:TAPS], tw[:, :, :]).then_inc(tw_hi.sem, 1)
            dve.wait_ge(tw_hi.sem, 1)
            dve.tensor_tensor(twp[:, 1, :, 0:TAPS], tw[:, :, :], twp[:, 0, :, 0:TAPS], ALU.subtract).then_inc(tw_lo.sem, 1)
            for k in range(2):
                dve.wait_ge(sw_hi.sem, k + 1)
                dve.scalar_tensor_tensor(swp[:, 2 * k + 1], sw[:, k], WS, swp[:, 2 * k], ALU.mult, ALU.subtract).then_inc(sw_lo.sem, 1)
            dve.tensor_scalar(sg2[:, :, :], sg[:, :, :], 0.0, None, ALU.is_lt).then_inc(sg_done.sem, 1)
            dve.wait_ge(sg_done.sem, 1)
            dve.scalar_tensor_tensor(sgn[:, :, :], sg[:, :, :], 0.0, sg2[:, :, :], ALU.is_gt, ALU.subtract)


def phase1(nc, a, sig, mem, psum, g):
    (ident, woh, wol, wqh, wql, bq, bo, rwh, rwl, rb, lower, ones, iota8, slots, wts, cnt, tab, w1h, w1l, w2h, w2l) = (
        g[n] for n in ("ident woh wol wqh wql bq bo rwh rwl rb lower ones iota8 slots wts cnt tab w1h w1l w2h w2l").split())
    ks_d, kb_d, v_d, qx_d, x1_d, h2_d, xs_d = (g[n] for n in "ks_d kb_d v_d qx_d x1_d h2_d xs_d".split())
    NU = 16
    HALF = GN // 2
    PB = 4
    XB = 4
    KB = 4 * L

    xa = g["xa"]
    ha = xa
    sta = mem("sta", [P, GT, 6])
    mva = mem("mva", [P, GT, 2])
    vea = mem("vea", [P, GT])
    nma = mem("nma", [P, GT])
    rsa = mem("rsa", [P, GT])
    nba = mem("nba", [P, GT])
    hth = mem("hth", [P, KD, GN], F16)
    htl = mem("htl", [P, KD, GN], F16)
    qh = mem("qh", [P, KD, GN], F16)
    ql = mem("ql", [P, KD, GN], F16)
    kbd = mem("kbc", [P, KD * 8 * L], F16)
    mx = mem("mx", [P, GT, H])
    mts = mem("mts", [H, GN], F16)
    tables = Memory(nc, mem.at)
    q2 = mem("q2", [P, NPAIR, GN], F16)
    after_q2 = mem.at
    ks = mem("ksc", [P, 2, 2, NPAIR, L], F16)
    vc = mem("vc", [L, 2, 2, H, HV], F16)
    p32 = mem("p32", [L, XB, GN])
    ph = mem("ph", [L, PB, GN], F16)
    pl = mem("pl", [L, PB, GN], F16)
    rec = mem("rec", [P, 2, H])
    y = mem("y", [P, 2, D])
    yth = mem("yth", [P, KD, HALF], F16)
    ytl = mem("ytl", [P, KD, HALF], F16)
    x1 = mem("x1", [P, GT, D])
    h2 = mem("h2", [P, GT, D])
    stc = mem("stc", [P, GT, 6])
    mvc = mem("mvc", [P, GT, 2])
    vec = mem("vec", [P, GT])
    nmc = mem("nmc", [P, GT])
    rsc = mem("rsc", [P, GT])
    nbc = mem("nbc", [P, GT])
    cth = mem("cth", [P, KD, GN], F16)
    ctl = mem("ctl", [P, KD, GN], F16)
    lgt = mem("lgt", [P, GT, E])
    top = mem("top", [P, GT, 8])
    tix = mem("tix", [P, GT, 8], U32)
    tif = mem("tif", [P, GT, 2])
    oh0 = mem("oh0", [P, GT, E])
    oh1 = mem("oh1", [P, GT, E])
    ohs = mem("ohs", [P, GT, E], F16)
    gap = mem("gap", [P, GT])
    eg = mem("eg", [P, GT])
    den = mem("den", [P, GT])
    w0 = mem("w0", [P, GT])
    cum = mem("cum", [P, GT, E])
    row = mem("row", [P, GT, E])
    pk0 = mem("pk0", [P, GT, E])
    pk1 = mem("pk1", [P, GT, E])
    sf = mem("sf", [P, 2, GT])
    sc = mem("sc", [P, 2 * GT], I32)
    mhalf = mem("mhalf", [P, GT])
    MM = MT + 1
    NM = T // TR
    before, start = g["before"], g["start"]
    zero = tables("zero", [P, D])
    ends = tables("ends", [1, E], I32)
    tiles = tables("tiles", [P, MM])
    full = tables("full", [P, NM])
    num = tables("num", [P, E])
    more = tables("more", [P, E, NM])
    held = [tables(f"held{k}", [P, E]) for k in range(4)]
    past = tables("past", [1, MM, E])
    past_n = tables("past_n", [1, MM, E])
    exp_f, first, base, local, row_f = (tables(n, [1, MM]) for n in ("exp_f", "first", "base", "local", "row_f"))
    tf = tables("tf", [1, 2, MM])
    assert tables.at <= after_q2
    wst = mem("wst", [P, 2, CH])

    NCK = 8
    bank_a = psum[0:2]
    bank_w = psum[2:4]
    bank_s = psum[4:6]
    bank_v = psum[6:8]
    lg_ps = bank_w[0][:, 0:GT * E]
    pf_ps = bank_w[1][:, 0:GT * E]
    tt_ps = bank_w[1][:, GT * E:2 * GT * E]

    hi_on = ["act"] * NU
    lo_on = ["dve" if n in LO_DVE else "pool" for n in range(NU)]

    xa_ld = g["xa_ld"]
    kb_ld = sig("kb_ld", 16)
    bna = sig("bna", GT)
    mv_a = sig("mv_a", GT)
    rs_a = sig("rs_a", 4)
    h_a = sig("h_a", GT)
    t_a = sig("t_a", KD)
    ht_h = sig("ht_h", KD)
    ht_l = sig("ht_l", KD)
    q_ps = sig("q_ps", KD)
    q_h = sig("q_h", KD)
    q_l = sig("q_l", KD)
    q_st = sig("q_st", 6 * 16)
    mm = sig("mm", 16)
    mxd = sig("mxd", 16)
    mt_ps = sig("mt_ps", 2)
    mt_s = sig("mt_s", 2)
    m_st = [sig(f"m_st{k}", 32) for k in range(2)]
    q2_ld = [sig(f"q2_ld{k}", 32) for k in range(2)]
    ks_ld = sig("ksc_ld", 16)
    v_ld = sig("v_ld", 16)
    xb_ld = sig("xb_ld", 16)
    s_ps = sig("s_ps", NU)
    p_ex = sig("p_ex", NU)
    hi = {e: sig("hi_" + e, hi_on.count(e)) for e in ("act",)}
    lo = {e: sig("lo_" + e, lo_on.count(e)) for e in ("dve", "pool")}
    pv = sig("pv", NU)
    rcd = sig("rcd", 4)
    y_d = sig("y_d", 4)
    yt_ps = sig("yt_ps", 2)
    yt_h = sig("yt_h", 2)
    yt_l = sig("yt_l", 2)
    o_ps = sig("o_ps", 2)
    x1d = sig("x1d", GT)
    x1_st = sig("x1_st", 16)
    h2_st = sig("h2_st", 16)
    bnc = sig("bnc", GT)
    mv_c = sig("mv_c", GT)
    rs_c = sig("rs_c", 4)
    h_c = sig("h_c", GT)
    t_c = sig("t_c", KD)
    ct_h = sig("ct_h", KD)
    ct_l = sig("ct_l", KD)
    lg = sig("lg", 1)
    lg_d = sig("lg_d", 1)
    gap_d = sig("gap_d", 1)
    eg_d = sig("eg_d", 1)
    oh_d = sig("oh_d", 1)
    pf = sig("pf", 1)
    cch = sig("cch", 27)
    sc_d = sig("sc_d", 1)
    scat = sig("scat", 8 * 16)
    const_ld = sig("tb_const_ld")
    zero_d = sig("tb_zero")
    step = sig("tb_step")
    ends_d = sig("tb_ends")
    tab_d = sig("tab_d")
    tail = sig("tail")
    w_ld = [sig("w_ld0", 16 * NCK // 2), sig("w_ld1", 16 * NCK // 2)]
    w_hi = sig("w_hi", NCK)
    w_lo = sig("w_lo", NCK)
    mh_d = sig("mh_d")

    def after(eng, table, on, i, n):
        e = on[n]
        wait(eng, table[e], table[e].at(i, on[:n + 1].count(e)))

    def unit(i, n):
        return (i, n) if n >= 0 else (i - 1, n + NU)

    def has(i, n=0):
        return not isinstance(i, int) or 0 <= i < NG

    def parity(i):
        return i % 2

    def loop(eng, body, ahead=1):
        for i in range(-1, 2):
            body(i)
        with eng.Fori(2, NG - ahead) as i:
            body(i)
        for i in range(NG - ahead, NG + 2):
            body(i)

    with nc.Block() as block:
        @block.sync
        def _(sp):
            def weights(i, n):
                wait(sp, w_lo, w_lo.at(i, n - 1), True)
                if n < 4:
                    k, c = n // 2, n % 2
                    src = a["w1"][bass.ds(i, 1), k * P:(k + 1) * P, c * CH:(c + 1) * CH].rearrange("e p n -> p (e n)")
                    dst = wst[:, n % 2]
                else:
                    f = (n - 4) * 2
                    src = a["w2"][bass.ds(i, 1), f * P:(f + 2) * P, :].rearrange("e (f p) n -> p (e f) n", p=P)
                    dst = wst[:, n % 2].rearrange("p (f n) -> p f n", n=D)
                sp.dma_start(dst, src).then_inc(w_ld[n % 2].sem, 16)

            def queries(i, part):
                at = slice(part * HALF, (part + 1) * HALF)
                for half in range(2):
                    sp.dma_start(q2[64 * half:64 * half + 64, :, at],
                                 qx_d[half].rearrange("s (r q) (k n) -> (s r) (q k) n", q=4, k=KD)[:, :, at]).then_inc(q2_ld[part].sem, 16)

            def maxima(i, part):
                wait(sp, mt_s, mt_s.at(i, part + 1), True)
                at = slice(part * HALF, (part + 1) * HALF)
                for half in range(2):
                    sp.dma_start(qx_d[half, 3, 0:4].rearrange("q (k n) -> (q k) n", k=KD)[:, at], mts[8 * half:8 * half + 8, at]).then_inc(m_st[part].sem, 16)

            def body(i):
                s, c = i + 1, i - 1
                if has(i):
                    wait(sp, m_st[1], m_st[1].at(i, 32), True)
                    wait(sp, s_ps, s_ps.at(i, 0), True)
                    queries(i, 1)
                if has(s):
                    if not has(i):
                        wait(sp, g["stored"][0], B * 16)
                        wait(sp, g["stored"][1], (2 * B + 8) * 16)
                    wait(sp, mm, mm.at(s, 0), True)
                    sp.dma_start(kbd[:, :], kb_d[bass.ds(s // 2, 1)].rearrange("b p n -> p (b n)")).then_inc(kb_ld.sem, 16)
                if has(i):
                    for n in range(4):
                        weights(i, n)
                if has(s):
                    wait(sp, q2_ld[0], q2_ld[0].at(s, 0), True)
                    wait(sp, q2_ld[1], q2_ld[1].at(s, 0), True)
                    wait(sp, q_h, q_h.at(s, KD), True)
                    for half in range(2):
                        for part in (0, 2):
                            sp.dma_start(qx_d[half, part], qh[64 * half:64 * half + 64].rearrange("p k n -> p (k n)")).then_inc(q_st.sem, 16)
                    wait(sp, q_l, q_l.at(s, KD), True)
                    for half in range(2):
                        sp.dma_start(qx_d[half, 1], ql[64 * half:64 * half + 64].rearrange("p k n -> p (k n)")).then_inc(q_st.sem, 16)
                    if has(s + 1):
                        wait(sp, t_a, t_a.at(s, KD), True)
                        sp.dma_start(xa[:, :, :], a["x"][bass.ds((s + 1) * GN, GN), :].rearrange("(t p) n -> p t n", p=P)).then_inc(xa_ld.sem, 16)
                    wait(sp, ks_ld, ks_ld.at(s, 0), True)
                    sp.dma_start(ks[:, bass.ds(parity(s), 1)].rearrange("p g a b l -> p (g a b l)"), ks_d[bass.ds(s // 2, 1)].rearrange("b p n -> p (b n)")).then_inc(ks_ld.sem, 16)
                    wait(sp, v_ld, v_ld.at(s, 0), True)
                    wait(sp, pv, pv.at(i, 0), True)
                    sp.dma_start(vc[:, bass.ds(parity(s), 1)].rearrange("p g a h v -> p (g a h v)"), v_d[bass.ds(s // 2, 1)].rearrange("b p n -> p (b n)")).then_inc(v_ld.sem, 16)
                if has(c):
                    wait(sp, x1d, x1d.at(c, GT), True)
                    sp.dma_start(g["x1_d"][bass.ds(c * GN, GN), :].rearrange("(t p) n -> p t n", p=P), x1[:, :, :]).then_inc(x1_st.sem, 16)
                    wait(sp, h_c, h_c.at(c, GT), True)
                    sp.dma_start(h2_d[bass.ds(c * GN, GN), :].rearrange("(t p) n -> p t n", p=P), h2[:, :, :]).then_inc(h2_st.sem, 16)
                if has(i):
                    wait(sp, h_c, h_c.at(i, 0), True)
                    wait(sp, x1_st, x1_st.at(i, 0), True)
                    sp.dma_start(x1[:, :, :], a["x"][bass.ds(i * GN, GN), :].rearrange("(t p) n -> p t n", p=P)).then_inc(xb_ld.sem, 16)
                    for n in range(4, 7):
                        weights(i, n)
                if has(s):
                    maxima(s, 0)
                if has(i):
                    weights(i, 7)
                if has(s):
                    wait(sp, m_st[0], m_st[0].at(s, 32), True)
                    wait(sp, q_st, q_st.at(s, 96), True)
                    wait(sp, s_ps, s_ps.at(i, 8), True)
                    queries(s, 0)
                    maxima(s, 1)

            loop(sp, body, 2)
            wait(sp, s_ps, s_ps.at(NG, 0))
            sp.dma_start(tiles[:, :], a["tiles"]).then_inc(const_ld.sem, 16)
            sp.wait_ge(zero_d.sem, 1)
            sp.wait_ge(ends_d.sem, 1)
            for e in range(E):
                end = sp.value_load(ends[0:1, e:e + 1], min_val=0, max_val=ZROW - TR)
                sp.dma_start(xs_d[bass.ds(end, TR), :].rearrange("(t p) n -> p t n", p=P), zero.unsqueeze(1).to_broadcast([P, TR // P, D])).then_inc(tail.sem, 16)
            sp.wait_ge(tail.sem, E * 16)
            sp.wait_ge(x1_st.sem, x1_st.at(NG, 0))
            sp.wait_ge(h2_st.sem, h2_st.at(NG, 0))
            sp.wait_ge(scat.sem, scat.at(NG, 0))

        @block.gpsimd
        def _(pool):
            def rstd(i, mv, ve, nm, rs, nb, ready, read, done):
                wait(pool, ready, ready.at(i, GT), True)
                wait(pool, read, read.at(i, 0), True)
                pool.tensor_scalar(ve[:, :], mv[:, :, 1], EPS, None, ALU.add).then_inc(done.sem, 1)
                pool.tensor_scalar(nm[:, :], mv[:, :, 0], -1.0, None, ALU.mult).then_inc(done.sem, 1)
                wait(pool, done, done.at(i, 2), True)
                pool.tensor_tensor(out=rs[:, :], in0=ve[:, :], in1=mhalf[:, :], op=ALU.pow).then_inc(done.sem, 1)
                wait(pool, done, done.at(i, 3), True)
                pool.tensor_tensor(out=nb[:, :], in0=nm[:, :], in1=rs[:, :], op=ALU.mult).then_inc(done.sem, 1)

            def low(i, n):
                b = n % PB
                after(pool, hi, hi_on, i, n)
                wait(pool, pv, pv.at(i, n - PB + 1), True)
                pool.tensor_tensor(out=pl[:, b], in0=p32[:, n % XB], in1=ph[:, b], op=ALU.subtract).then_inc(lo["pool"].sem, 1)

            def body(i):
                s, c = i + 1, i - 1
                for n in range(NU):
                    if n == AT["rs_a"] and has(s):
                        rstd(s, mva, vea, nma, rsa, nba, mv_a, h_a, rs_a)
                    j, m = unit(i, n - LO_LAG)
                    if has(j) and lo_on[m] == "pool":
                        low(j, m)
                    if n == AT["rs_c"] and has(c):
                        rstd(c, mvc, vec, nmc, rsc, nbc, mv_c, h_c, rs_c)
                    for q, at in enumerate(SCATTER):
                        j = c - at // NU
                        if n == at % NU and has(j):
                            wait(pool, sc_d, sc_d.at(j, 1), True)
                            pool.indirect_dma_start(out=xs_d[:, :], out_offset=bass.IndirectOffsetOnAxis(ap=sc[:, q:q + 1], axis=0),
                                                    in_=h2[:, q % GT], in_offset=None).then_inc(scat.sem, 16)

            pool.memset(mhalf[:, :], -0.5).then_inc(mh_d.sem, 1)
            pool.wait_ge(mh_d.sem, 1)
            loop(pool, body)

        @block.scalar
        def _(act):
            def weights(i, n):
                wait(act, w_ld[n % 2], w_ld[n % 2].at(i, 16 * (n // 2 + 1)))
                if n < 4:
                    k, c = n // 2, n % 2
                    dst = w1h[:, bass.ds(i, 1), k, c * CH:(c + 1) * CH].rearrange("p e n -> p (e n)")
                else:
                    f = (n - 4) * 2
                    dst = w2h[:, bass.ds(i, 1), f:f + 2, :].rearrange("p e f n -> p (e f n)")
                act.activation(dst, wst[:, n % 2], ACT.Copy, scale=WS).then_inc(w_hi.sem, 1)

            def body(i):
                s, c = i + 1, i - 1
                for n in range(NU):
                    if has(i):
                        wait(act, s_ps, s_ps.at(i, n + 1))
                        j, m = unit(i, n - XB)
                        if has(j):
                            after(act, lo, lo_on, j, m)
                        act.activation(p32[:, n % XB], bank_s[n % 2][0:L, :], ACT.Exp, scale=QK_SCALE / PSC).then_inc(p_ex.sem, 1)
                    j, m = unit(i, n - 1)
                    if has(j) and hi_on[m] == "act":
                        wait(act, p_ex, p_ex.at(j, m + 1))
                        wait(act, pv, pv.at(j, m - PB + 1))
                        act.activation(ph[:, m % PB], p32[:, m % XB], ACT.Copy).then_inc(hi["act"].sem, 1)
                    if has(i) and n % 2 == 0:
                        weights(i, n // 2)
                    if n == AT["ha"] and has(s):
                        wait(act, xa_ld, xa_ld.at(s, 16))
                        wait(act, rs_a, rs_a.at(s, 4))
                        wait(act, t_a, t_a.at(s, 0))
                        for t in range(GT):
                            act.activation(ha[:, t], xa[:, t], ACT.Identity, bias=nba[:, t:t + 1], scale=rsa[:, t:t + 1]).then_inc(h_a.sem, 1)
                    if n == AT["yth1"] and has(c):
                        wait(act, yt_ps, yt_ps.at(c, 2))
                        wait(act, o_ps, o_ps.at(c, 1))
                        act.activation(yth[:, :, :].rearrange("p k n -> p (k n)"), bank_w[0][:, :], ACT.Copy).then_inc(yt_h.sem, 1)
                    if n == AT["hth"] and has(s):
                        for k in range(KD):
                            wait(act, t_a, t_a.at(s, k + 1))
                            wait(act, q_ps, q_ps.at(s, 0))
                            act.activation(hth[:, k], bank_a[k][:, :], ACT.Copy).then_inc(ht_h.sem, 1)
                    if n == AT["qh"] and has(s):
                        for k in range(KD):
                            wait(act, q_ps, q_ps.at(s, k + 1))
                            wait(act, q_st, q_st.at(s, 0))
                            wait(act, mm, mm.at(s, 0))
                            act.activation(qh[:, k], bank_a[k][:, :], ACT.Identity, bias=bq[:, k:k + 1]).then_inc(q_h.sem, 1)
                    if n == AT["h2"] and has(c):
                        wait(act, rs_c, rs_c.at(c, 4))
                        wait(act, t_c, t_c.at(c, 0))
                        wait(act, scat, scat.at(c, 0))
                        wait(act, h2_st, h2_st.at(c, 0))
                        for t in range(GT):
                            act.activation(h2[:, t], x1[:, t], ACT.Identity, bias=nbc[:, t:t + 1], scale=rsc[:, t:t + 1]).then_inc(h_c.sem, 1)
                    if n == AT["cth"] and has(c):
                        for k in range(KD):
                            wait(act, t_c, t_c.at(c, k + 1))
                            wait(act, lg, lg.at(c, 0))
                            act.activation(cth[:, k], bank_w[k][:, :], ACT.Copy).then_inc(ct_h.sem, 1)
                    if n == AT["yth0"] and has(i):
                        wait(act, yt_ps, yt_ps.at(i, 1))
                        wait(act, o_ps, o_ps.at(i, 0))
                        act.activation(yth[:, :, :].rearrange("p k n -> p (k n)"), bank_w[0][:, :], ACT.Copy).then_inc(yt_h.sem, 1)
                    if n == AT["eg"] and has(c):
                        wait(act, gap_d, gap_d.at(c, 1))
                        act.activation(eg[:, :], gap[:, :], ACT.Exp).then_inc(eg_d.sem, 1)
                    for part in range(2):
                        if n == AT[f"mts{part}"] and has(s):
                            at = slice(part * HALF, (part + 1) * HALF)
                            wait(act, mt_ps, mt_ps.at(s, part + 1))
                            wait(act, m_st[part], m_st[part].at(s, 0))
                            act.activation(mts[:, at], bank_a[0][0:H, at], ACT.Copy, scale=1.0 / PSC).then_inc(mt_s.sem, 1)

            loop(act, body)

        @block.vector
        def _(dve):
            def stats(i, x, st, mv, ready, n_ready, bn, mvs):
                wait(dve, ready, ready.at(i, n_ready))
                for t in range(GT):
                    dve.bn_stats(st[:, t], x[:, t]).then_inc(bn.sem, 1)
                for t in range(GT):
                    wait(dve, bn, bn.at(i, t + 1), True)
                    dve.bn_aggr(mv[:, t], st[:, t]).then_inc(mvs.sem, 1)

            def weights(i, n):
                wait(dve, w_hi, w_hi.at(i, n + 1))
                if n < 4:
                    k, c = n // 2, n % 2
                    at = (slice(None), bass.ds(i, 1), k, slice(c * CH, (c + 1) * CH))
                    h, l = (w[at].rearrange("p e n -> p (e n)") for w in (w1h, w1l))
                else:
                    f = (n - 4) * 2
                    at = (slice(None), bass.ds(i, 1), slice(f, f + 2), slice(None))
                    h, l = (w[at].rearrange("p e f n -> p (e f n)") for w in (w2h, w2l))
                dve.scalar_tensor_tensor(l, wst[:, n % 2], WS, h, ALU.mult, ALU.subtract).then_inc(w_lo.sem, 1)

            def values(i, half):
                wait(dve, pv, pv.at(i, 8 * half + 8))
                wait(dve, yt_ps, yt_ps.at(i, half))
                for t in range(2):
                    v3 = bank_v[t][:, 0:H * HV].rearrange("p (h v) -> p h v", v=HV)
                    dve.reciprocal(rec[:, t], v3[:, :, HD]).then_inc(rcd.sem, 1)
                for t in range(2):
                    v3 = bank_v[t][:, 0:H * HV].rearrange("p (h v) -> p h v", v=HV)
                    wait(dve, rcd, rcd.at(i, 2 * half + t + 1))
                    dve.tensor_tensor(y[:, t].rearrange("p (h d) -> p h d", d=HD), v3[:, :, 0:HD],
                                      rec[:, t].unsqueeze(2).to_broadcast([P, H, HD]), ALU.mult).then_inc(y_d.sem, 1)

            def y_low(i, half):
                wait(dve, yt_h, yt_h.at(i, half + 1))
                wait(dve, o_ps, o_ps.at(i, half))
                dve.tensor_tensor(ytl[:, :, :].rearrange("p k n -> p (k n)"), bank_w[0][:, :],
                                  yth[:, :, :].rearrange("p k n -> p (k n)"), ALU.subtract).then_inc(yt_l.sem, 1)

            def residual(i, half):
                wait(dve, o_ps, o_ps.at(i, half + 1))
                wait(dve, xb_ld, xb_ld.at(i, 16))
                for t in range(2):
                    dve.scalar_tensor_tensor(x1[:, 2 * half + t], bank_w[1][:, t * D:(t + 1) * D], 1.0 / PSC,
                                             x1[:, 2 * half + t], ALU.mult, ALU.add).then_inc(x1d.sem, 1)

            class Chain:

                def __init__(self, i, n):
                    self.i, self.n = i, n

                def __call__(self, instruction):
                    instruction.then_inc(cch.sem, 1)
                    self.n += 1

                def wait(self):
                    wait(dve, cch, cch.at(self.i, self.n))

            def logits(i):
                wait(dve, lg, lg.at(i, 1))
                dve.scalar_tensor_tensor(lgt[:, :, :], lg_ps.rearrange("p (t e) -> p t e", e=E), 1.0 / PSC,
                                         rb.unsqueeze(1).to_broadcast([P, GT, E]), ALU.mult, ALU.add).then_inc(lg_d.sem, 1)

            def top2(i):
                ch = Chain(i, 0)
                wait(dve, lg_d, lg_d.at(i, 1), True)
                for t in range(GT):
                    ch(dve.max(top[:, t], lgt[:, t]))
                ch.wait()
                wait(dve, eg_d, eg_d.at(i, 0))
                dve.tensor_tensor(gap[:, :], top[:, :, 1], top[:, :, 0], ALU.subtract).then_inc(gap_d.sem, 1)
                for t in range(GT):
                    ch(dve.max_index(tix[:, t], top[:, t], lgt[:, t]))
                ch.wait()
                ch(dve.tensor_copy(tif[:, :, :], tix[:, :, 0:2]))
                ch.wait()
                io = iota8.unsqueeze(1).to_broadcast([P, GT, E])
                ch(dve.tensor_tensor(oh0[:, :, :], io, tif[:, :, 0].unsqueeze(2).to_broadcast([P, GT, E]), ALU.is_equal))
                ch(dve.tensor_tensor(oh1[:, :, :], io, tif[:, :, 1].unsqueeze(2).to_broadcast([P, GT, E]), ALU.is_equal))
                ch.wait()
                wait(dve, pf, pf.at(i, 0))
                dve.tensor_tensor(ohs[:, :, :], oh0[:, :, :], oh1[:, :, :], ALU.add).then_inc(oh_d.sem, 1)
                return ch

            def place(i, n0):
                ch = Chain(i, n0)
                wait(dve, eg_d, eg_d.at(i, 1))
                ch(dve.tensor_scalar(den[:, :], eg[:, :], 1.0, None, ALU.add))
                ch.wait()
                ch(dve.reciprocal(w0[:, :], den[:, :]))
                ch.wait()
                ch(dve.tensor_copy(wts[:, bass.ds(i * GT, GT), 0], w0[:, :]))
                ch(dve.tensor_tensor(wts[:, bass.ds(i * GT, GT), 1], eg[:, :], w0[:, :], ALU.mult))
                wait(dve, pf, pf.at(i, 1))
                tot = tt_ps.rearrange("p (t e) -> p t e", e=E)
                ch(dve.tensor_copy(cum[:, 0], cnt[:, :]))
                for t in range(1, GT):
                    ch.wait()
                    ch(dve.tensor_tensor(cum[:, t], cum[:, t - 1], tot[:, t - 1], ALU.add))
                ch.wait()
                ch(dve.tensor_tensor(cnt[:, :], cum[:, GT - 1], tot[:, GT - 1], ALU.add))
                ch(dve.tensor_tensor(row[:, :, :], cum[:, :, :], pf_ps.rearrange("p (t e) -> p t e", e=E), ALU.add))
                ch.wait()
                ch(dve.tensor_tensor(pk0[:, :, :], row[:, :, :], oh0[:, :, :], ALU.mult))
                ch(dve.tensor_tensor(pk1[:, :, :], row[:, :, :], oh1[:, :, :], ALU.mult))
                ch.wait()
                ch(dve.tensor_reduce(sf[:, 0], pk0[:, :, :], axis=AX.X, op=ALU.add))
                ch(dve.tensor_reduce(sf[:, 1], pk1[:, :, :], axis=AX.X, op=ALU.add))
                ch.wait()
                wait(dve, scat, scat.at(i, 0))
                for k in range(2):
                    ch(dve.tensor_copy(slots[:, bass.ds(i * GT, GT), k], sf[:, k]))
                dve.tensor_copy(sc[:, :], sf[:, :, :].rearrange("p k t -> p (k t)")).then_inc(sc_d.sem, 1)
                return ch

            def body(i):
                s, c = i + 1, i - 1
                for n in range(NU):
                    if n == AT["st_a"] and has(s):
                        stats(s, xa, sta, mva, xa_ld, 16, bna, mv_a)
                    j, m = unit(i, n - LO_LAG)
                    if has(j) and lo_on[m] == "dve":
                        after(dve, hi, hi_on, j, m)
                        wait(dve, pv, pv.at(j, m - PB + 1))
                        dve.tensor_tensor(pl[:, m % PB], p32[:, m % XB], ph[:, m % PB], ALU.subtract).then_inc(lo["dve"].sem, 1)
                    if n == AT["values1"] and has(c):
                        values(c, 1)
                    if n == AT["htl"] and has(s):
                        for k in range(KD):
                            wait(dve, ht_h, ht_h.at(s, k + 1))
                            dve.tensor_tensor(htl[:, k], bank_a[k][:, :], hth[:, k], ALU.subtract).then_inc(ht_l.sem, 1)
                    if n == AT["ytl1"] and has(c):
                        y_low(c, 1)
                    if n == AT["res1"] and has(c):
                        residual(c, 1)
                        stats(c, x1, stc, mvc, x1d, GT, bnc, mv_c)
                    if n == AT["ql"] and has(s):
                        for k in range(KD):
                            wait(dve, q_h, q_h.at(s, k + 1))
                            wait(dve, q_st, q_st.at(s, 0))
                            dve.scalar_tensor_tensor(ql[:, k], bank_a[k][:, :], bq[:, k:k + 1], qh[:, k], ALU.add, ALU.subtract).then_inc(q_l.sem, 1)
                    if n == AT["values0"] and has(i):
                        values(i, 0)
                    if AT["mxd"] <= n < AT["mxd"] + 8 and has(s):
                        for u in (2 * (n - AT["mxd"]), 2 * (n - AT["mxd"]) + 1):
                            t, mt, half = u // 4, u // 2 % 2, u % 2
                            wait(dve, mm, mm.at(s, u + 1))
                            wait(dve, mt_ps, mt_ps.at(s, 0))
                            dve.tensor_reduce(mx[:, t, 8 * half + mt:8 * half + 8:2], bank_a[u % 2][:, 0:KB].rearrange("p (h l) -> p h l", l=L),
                                              axis=AX.X, op=ALU.max).then_inc(mxd.sem, 1)
                    if n == AT["ctl"] and has(c):
                        for k in range(KD):
                            wait(dve, ct_h, ct_h.at(c, k + 1))
                            dve.tensor_tensor(ctl[:, k], bank_w[k][:, :], cth[:, k], ALU.subtract).then_inc(ct_l.sem, 1)
                    if n == AT["logits"] and has(c):
                        logits(c)
                    if n == AT["ytl0"] and has(i):
                        y_low(i, 0)
                    if n == AT["top2"] and has(c):
                        top2(c)
                    if n == AT["res0"] and has(i):
                        residual(i, 0)
                    if n == AT["place"] and has(c):
                        assert place(c, 11).n == cch.per
                    if n % 2 == 1 and has(i):
                        weights(i, n // 2)

            loop(dve, body)
            ch = Count(dve, step)
            dve.memset(zero[:, :], 0.0).then_inc(zero_d.sem, 1)
            dve.tensor_copy(ends[:, :], cnt[0:1, :]).then_inc(ends_d.sem, 1)
            dve.wait_ge(const_ld.sem, 16)
            ch(dve.tensor_scalar(start[:, :], iota8[:, :], float(REG), None, ALU.mult))
            ch(dve.tensor_scalar(full[:, :], tiles[:, 0:NM], float(TR), None, ALU.mult))
            ch.wait()
            ch(dve.tensor_tensor(num[:, :], cnt[:, :], start[:, :], ALU.subtract))
            ch.wait()
            ch(dve.tensor_tensor(more[:, :, :], num.unsqueeze(2).to_broadcast([P, E, NM]),
                                 full.unsqueeze(1).to_broadcast([P, E, NM]), ALU.is_gt))
            ch.wait()
            ch(dve.tensor_reduce(held[0][:, :], more[:, :, :], axis=AX.X, op=ALU.add))
            for k in range(3):
                ch.wait()
                ch(dve.tensor_copy(held[k + 1][:, 0:1 << k], held[k][:, 0:1 << k]))
                ch(dve.tensor_tensor(held[k + 1][:, 1 << k:], held[k][:, 1 << k:], held[k][:, :E - (1 << k)], ALU.add))
            ch.wait()
            ch(dve.tensor_tensor(past[:, :, :], tiles[0:1].unsqueeze(2).to_broadcast([1, MM, E]),
                                 held[3][0:1].unsqueeze(1).to_broadcast([1, MM, E]), ALU.is_ge))
            ch(dve.tensor_tensor(before[:, :], held[3][:, :], held[0][:, :], ALU.subtract))
            ch.wait()
            ch(dve.tensor_tensor(past_n[:, :, :], past[:, :, :], held[0][0:1].unsqueeze(1).to_broadcast([1, MM, E]), ALU.mult))
            ch(dve.tensor_reduce(exp_f[:, :], past[:, :, :], axis=AX.X, op=ALU.add))
            ch.wait()
            ch(dve.tensor_reduce(first[:, :], past_n[:, :, :], axis=AX.X, op=ALU.add))
            ch(dve.tensor_scalar(base[:, :], exp_f[:, :], float(REG), None, ALU.mult))
            ch(dve.tensor_scalar(tf[:, 0], exp_f[:, :], float(E - 1), None, ALU.min))
            ch.wait()
            ch(dve.tensor_tensor(local[:, :], tiles[0:1], first[:, :], ALU.subtract))
            ch.wait()
            ch(dve.scalar_tensor_tensor(row_f[:, :], local[:, :], float(TR), base[:, :], ALU.mult, ALU.add))
            ch.wait()
            ch(dve.tensor_scalar(tf[:, 1], row_f[:, :], float(ZROW), None, ALU.min))
            ch.wait()
            dve.tensor_copy(tab[:, :, :], tf[:, :, :]).then_inc(tab_d.sem, 1)
            dve.wait_ge(tab_d.sem, 1)

        @block.tensor
        def _(pe):
            def output(i, half):
                wait(pe, yt_l, yt_l.at(i, half + 1))
                wait(pe, x1d, x1d.at(i, 2 * half))
                wait(pe, ct_l, ct_l.at(i, 0))
                if not half:
                    wait(pe, cch, cch.at(i, 0))
                for t in range(2):
                    at = slice(t * P, (t + 1) * P)
                    out = bank_w[1][:, t * D:(t + 1) * D]
                    for part in range(2):
                        pe.matmul(out, ones[0:1, :], bo[:, part], start=part == 0, stop=False)
                    m = passes(pe, out, [(yth[:, k, at], ytl[:, k, at], woh[:, k], wol[:, k]) for k in range(KD)], first=False)
                m.then_inc(o_ps.sem, 1)

            def transpose_y(i, half):
                wait(pe, y_d, y_d.at(i, 2 * half + 2))
                wait(pe, yt_l, yt_l.at(i, half))
                wait(pe, lg_d, lg_d.at(i, 0))
                for t in range(2):
                    for k in range(KD):
                        m = pe.transpose(bank_w[0][:, k * HALF + t * P:k * HALF + (t + 1) * P], y[:, t, k * P:(k + 1) * P], ident[:, :])
                m.then_inc(yt_ps.sem, 1)

            def rows_to_columns(i, h, bank, ready, done):
                wait(pe, ready, ready.at(i, GT))
                for k in range(KD):
                    for t in range(GT):
                        m = pe.transpose(bank[k][:, t * P:(t + 1) * P], h[:, t, k * P:(k + 1) * P], ident[:, :])
                    m.then_inc(done.sem, 1)

            def body(i):
                s, c = i + 1, i - 1
                for n in range(NU):
                    if has(i):
                        if n == 0:
                            wait(pe, ks_ld, ks_ld.at(i, 16))
                        if n % 8 == 0:
                            wait(pe, q2_ld[n // 8], q2_ld[n // 8].at(i, 32))
                        wait(pe, p_ex, p_ex.at(i, n - 1))
                        for half in range(2):
                            m = pe.matmul(bank_s[n % 2][0:L, half * HALF:(half + 1) * HALF], ks[:, bass.ds(parity(i), 1), half, n % 8].rearrange("p g l -> p (g l)"),
                                          q2[:, n % 8, n // 8 * HALF:(n // 8 + 1) * HALF], start=True, stop=True)
                        m.then_inc(s_ps.sem, 1)
                    j, m_ = unit(i, n - LAG)
                    if has(j):
                        after(pe, hi, hi_on, j, m_)
                        after(pe, lo, lo_on, j, m_)
                        if m_ == 0:
                            wait(pe, v_ld, v_ld.at(j, 16))
                        if m_ % 8 == 0:
                            wait(pe, y_d, y_d.at(j, 2 * (m_ // 8)))
                        for half in range(2):
                            hd = 2 * (m_ % 8) + half
                            for t in range(2):
                                at = slice(half * HALF + t * P, half * HALF + (t + 1) * P)
                                m = passes(pe, bank_v[t][:, hd * HV:(hd + 1) * HV],
                                           [(ph[:, m_ % PB, at], pl[:, m_ % PB, at], *(vc[:, bass.ds(parity(j), 1), k, hd].rearrange("p g v -> p (g v)") for k in range(2)))])
                        m.then_inc(pv.sem, 1)
                    if n == AT["yt1"] and has(c):
                        transpose_y(c, 1)
                    if n == AT["at"] and has(s):
                        wait(pe, mt_s, mt_s.at(s, 0))
                        wait(pe, mxd, mxd.at(s, 0))
                        rows_to_columns(s, ha, bank_a, h_a, t_a)
                    if n == AT["out1"] and has(c):
                        output(c, 1)
                    if n == AT["q"] and has(s):
                        for mt in range(KD):
                            wait(pe, ht_l, ht_l.at(s, KD))
                            m = passes(pe, bank_a[mt][:, :], [(wqh[:, k, mt * P:(mt + 1) * P], wql[:, k, mt * P:(mt + 1) * P], hth[:, k], htl[:, k]) for k in range(KD)])
                            m.then_inc(q_ps.sem, 1)
                    for part in range(2):
                        if n == AT["mm"] + 4 * (part + 1) and has(s):
                            wait(pe, mxd, mxd.at(s, 8 * (part + 1)))
                            for t in (2 * part, 2 * part + 1):
                                m = pe.transpose(bank_a[0][0:H, t * P:(t + 1) * P], mx[:, t], ident[:, :])
                            m.then_inc(mt_ps.sem, 1)
                    if AT["mm"] <= n < AT["mm"] + 8 and has(s):
                        if n == AT["mm"]:
                            wait(pe, kb_ld, kb_ld.at(s, 16))
                            wait(pe, q_l, q_l.at(s, KD))
                        for u in (2 * (n - AT["mm"]), 2 * (n - AT["mm"]) + 1):
                            t, mt, half = u // 4, u // 2 % 2, u % 2
                            if u == 8:
                                wait(pe, mt_s, mt_s.at(s, 1))
                            wait(pe, mxd, mxd.at(s, u - 1))
                            at = (mt * 2 + half) * KB
                            pe.matmul(bank_a[u % 2][:, 0:KB], qh[:, mt, t * P:(t + 1) * P], kbd[:, at:at + KB], start=True, stop=True).then_inc(mm.sem, 1)
                    if n == AT["ct"] and has(c):
                        rows_to_columns(c, h2, bank_w, h_c, t_c)
                    if n == AT["lg"] and has(c):
                        wait(pe, ct_l, ct_l.at(c, KD))
                        for t in range(GT):
                            at = slice(t * P, (t + 1) * P)
                            m = passes(pe, lg_ps[:, t * E:(t + 1) * E], [(cth[:, k, at], ctl[:, k, at], rwh[:, k], rwl[:, k]) for k in range(KD)])
                        m.then_inc(lg.sem, 1)
                    if n == AT["yt0"] and has(i):
                        transpose_y(i, 0)
                    if n == AT["out0"] and has(i):
                        output(i, 0)
                    if n == AT["pf"] and has(c):
                        wait(pe, oh_d, oh_d.at(c, 1))
                        wait(pe, x1d, x1d.at(i, 0))
                        pe.matmul(pf_ps, lower[:, :], ohs[:, :, :].rearrange("p t e -> p (t e)"), start=True, stop=True)
                        pe.matmul(tt_ps, ones[:, :], ohs[:, :, :].rearrange("p t e -> p (t e)"), start=True, stop=True).then_inc(pf.sem, 1)

            loop(pe, body)


def paired(eng, count, body, first=3, drain=1, lead=1):
    pairs = (count - 2 - first) // 2
    for i in range(-lead, first):
        body(i, i % 2)
    with eng.Fori(0, pairs) as m:
        body(m * 2 + first, first % 2)
        body(m * 2 + first + 1, (first + 1) % 2)
    for i in range(2 * pairs + first, count + drain):
        body(i, i % 2)


def exists(i, count):
    return not isinstance(i, int) or 0 <= i < count


class Count:

    def __init__(self, eng, s):
        self.eng, self.s, self.n = eng, s, 0

    def __call__(self, instruction):
        instruction.then_inc(self.s.sem, 1)
        self.n += 1

    def wait(self):
        self.eng.wait_ge(self.s.sem, self.n)


def experts(nc, a, sig, mem, psum, g, done):
    tab, xs_d, slots, yslots, ident = (g[n] for n in ("tab", "xs_d", "slots", "yslots", "ident"))
    sw, sgs, b2p, sgst, sgbt = (g[n] for n in ("sw", "sgs", "b2p", "sgst", "sgbt"))
    before, start = g["before"], g["start"]
    NS = NT * 2
    shift = mem("shift", [P, E])
    jump = mem("jump", [P, E])
    sf = mem("tb_sf", [P, NS])
    from_e = mem("from_e", [P, NS, E])
    moved = mem("moved", [P, NS])
    to_f = mem("to_f", [P, NS])
    count = MT
    xr = mem("e_xr", [P, 2, TR // P, D])
    xh = mem("e_xh", [P, 2, KD, TR], F16)
    xl = mem("e_xl", [P, 2, KD, TR], F16)
    gel = mem("e_gel", [P, NF // 4, 4, TR])
    gh = mem("e_gh", [P, 2, NF, TR], F16)
    gl = mem("e_gl", [P, 2, NF, TR], F16)
    yo = mem("e_yo", [P, 2, TR // P, D])
    b1 = mem("e_b1", [P, E, NF])
    gate = mem("e_gate", [P, E, NF])
    b2 = mem("e_b2", [P, E, D])
    gs = mem("e_gs", [P, E, NF])
    gb = mem("e_gb", [P, E, NF])
    gst = mem("e_gst", [P, 2, NF])
    gbt = mem("e_gbt", [P, 2, NF])
    warm = mem("e_warm", [P, 1])
    sb1 = mem("sb1", [P, NSF])
    sgate = mem("sgate", [P, NSF])
    sb2 = mem("sb2", [1, D])
    sh = mem("sh", [P, 1])
    she = mem("she", [P, 1])
    she1 = mem("she1", [P, 1])
    sgm = mem("sgm", [P, 1])
    bank_t = psum[0:2]
    bank_u = psum[2:4]
    bank_y = (psum[4:6], psum[6:8])

    c_ld = sig("e_c_ld")
    w_ld = sig("e_w_ld")
    s_d = sig("e_s_d")
    step = sig("e_step")
    tab_d = sig("e_tab_d")
    pre = sig("e_pre")
    she_d = sig("e_she")
    gs_d = sig("e_gs")
    gt_d = sig("e_gt", 1)
    x_ld = [sig(f"e_x_ld{b}", 16) for b in range(2)]
    t_ps = sig("e_t_ps", 1)
    x_h = sig("e_x_h", 1)
    x_l = sig("e_x_l", 1)
    u_ps = sig("e_u_ps", NF // 2)
    g_a = sig("e_g_a", NF)
    g_h = sig("e_g_h", NF // 4)
    g_l = sig("e_g_l", NF // 4)
    y_ps = sig("e_y_ps", 1)
    y_d = sig("e_y_d", TR // P)
    y_st = [sig(f"e_y_st{b}", 16) for b in range(2)]

    def expert(eng, i):
        return eng.value_load(tab[0:1, 0, bass.ds(i, 1)], min_val=0, max_val=E - 1)

    with nc.Block() as block:
        @block.sync
        def _(sp):
            def load(i, b):
                wait(sp, t_ps, t_ps.at(i, -1), True)
                at = sp.value_load(tab[0:1, 1, bass.ds(i, 1)], min_val=0, max_val=ZROW)
                sp.dma_start(xr[:, b], xs_d[bass.ds(at, TR), :].rearrange("(t p) n -> p t n", p=P)).then_inc(x_ld[b].sem, 16)

            def body(i, b):
                if exists(i + 2, count):
                    load(i + 2, b)
                if exists(i - 1, count):
                    wait(sp, y_d, y_d.at(i - 1, TR // P), True)
                    sp.dma_start(g["ys_d"][bass.ds((i - 1) * TR, TR), :].rearrange("(t p) n -> p t n", p=P), yo[:, 1 - b]).then_inc(y_st[1 - b].sem, 16)

            load(0, 0)
            for dst, src in ((b1, a["b1"]), (gate, a["gate"]), (b2.rearrange("p e d -> p (e d)"), a["b2"].partition_broadcast(P))):
                sp.dma_start(dst, src).then_inc(c_ld.sem, 16)
            for dst, src in ((sw, g["sw_d"]), (sb1, a["sb1"]), (sgate, a["sgate"]), (sb2[:, :], a["sb2"]), (sh[:, :], a["shared"].partition_broadcast(P))):
                sp.dma_start(dst, src).then_inc(w_ld.sem, 16)
            paired(sp, count, body)
            for b in range(2):
                sp.wait_ge(y_st[b].sem, y_st[b].at((count + 1 - b) // 2, 0))

        @block.gpsimd
        def _(pool):
            for s in done:
                pool.sem_clear(s)

        @block.tensor
        def _(pe):
            def body(i, b):
                if exists(i + 1, count):
                    wait(pe, x_ld[1 - b], x_ld[1 - b].at((i + 1) // 2, 16))
                    wait(pe, x_l, x_l.at(i, 0))
                    for k in range(KD):
                        for t in range(TR // P):
                            m = pe.transpose(bank_t[1 - b][:, k * TR + t * P:k * TR + (t + 1) * P], xr[:, 1 - b, t, k * P:(k + 1) * P], ident[:, :])
                    m.then_inc(t_ps.sem, 1)
                if exists(i, count):
                    e = expert(pe, i)
                    wait(pe, x_l, x_l.at(i, 1))
                    for p in range(NF // 2):
                        wait(pe, g_a, g_a.at(i, 2 * (p - 1)))
                        for f in (2 * p, 2 * p + 1):
                            out = bank_u[p % 2][:, (f % 2) * TR:(f % 2 + 1) * TR]
                            at = slice(f * P, (f + 1) * P)
                            for k in range(KD):
                                wh, wl = (w[:, bass.ds(e, 1), k, at].rearrange("p e n -> p (e n)") for w in (g["w1h"], g["w1l"]))
                                pe.matmul(out, wh, xh[:, b, k], start=k == 0, stop=False)
                                pe.matmul(out, wh, xl[:, b, k], start=False, stop=False)
                                m = pe.matmul(out, wl, xh[:, b, k], start=False, stop=k == KD - 1)
                        m.then_inc(u_ps.sem, 1)
                if exists(i - 1, count):
                    e = expert(pe, i - 1)
                    wait(pe, y_d, y_d.at(i - 2, 0))
                    for f in range(NF):
                        if f % 4 == 0:
                            wait(pe, g_l, g_l.at(i - 1, f // 4 + 1))
                        wh, wl = (w[:, bass.ds(e, 1), f].rearrange("p e n -> p (e n)") for w in (g["w2h"], g["w2l"]))
                        for t in range(TR // P):
                            at = slice(t * P, (t + 1) * P)
                            out = bank_y[1 - b][t][:, 0:D]
                            pe.matmul(out, gh[:, 1 - b, f, at], wh, start=f == 0, stop=False)
                            pe.matmul(out, gh[:, 1 - b, f, at], wl, start=False, stop=False)
                            m = pe.matmul(out, gl[:, 1 - b, f, at], wh, start=False, stop=f == NF - 1)
                    m.then_inc(y_ps.sem, 1)

            paired(pe, count, body)

        @block.scalar
        def _(act):
            def body(i, b):
                if exists(i + 1, count):
                    wait(act, t_ps, t_ps.at(i + 1, 1))
                    wait(act, u_ps, u_ps.at(i, 0))
                    act.activation(xh[:, 1 - b].rearrange("p k n -> p (k n)"), bank_t[1 - b][:, :], ACT.Copy).then_inc(x_h.sem, 1)
                if exists(i, count):
                    wait(act, gt_d, gt_d.at(i, 1))
                    for f in range(NF):
                        if f % 4 == 0:
                            wait(act, g_l, g_l.at(i - 1, f // 4 + 1))
                        if f % 2 == 0:
                            wait(act, u_ps, u_ps.at(i, f // 2 + 1))
                        act.activation(gel[:, f // 4, f % 4], bank_u[f // 2 % 2][:, (f % 2) * TR:(f % 2 + 1) * TR], ACT.Gelu,
                                       bias=gbt[:, b, f:f + 1], scale=gst[:, b, f:f + 1]).then_inc(g_a.sem, 1)

            act.wait_ge(pre.sem, 1)
            act.activation(warm[:, :], warm[:, :], ACT.Gelu)
            paired(act, count, body)
            act.wait_ge(w_ld.sem, 5 * 16)
            act.activation(she[:, :], sh[:, :], ACT.Exp, scale=-1.0).then_inc(she_d.sem, 1)

        @block.vector
        def _(dve):
            def body(i, b):
                if exists(i + 1, count):
                    e = expert(dve, i + 1)
                    wait(dve, g_a, g_a.at(i, 0), True)
                    dve.tensor_copy(gst[:, 1 - b], gs[:, bass.ds(e, 1), :].rearrange("p e f -> p (e f)"))
                    dve.tensor_copy(gbt[:, 1 - b], gb[:, bass.ds(e, 1), :].rearrange("p e f -> p (e f)")).then_inc(gt_d.sem, 1)
                    wait(dve, x_h, x_h.at(i + 1, 1))
                    wait(dve, u_ps, u_ps.at(i, 0))
                    dve.tensor_tensor(xl[:, 1 - b].rearrange("p k n -> p (k n)"), bank_t[1 - b][:, :],
                                      xh[:, 1 - b].rearrange("p k n -> p (k n)"), ALU.subtract).then_inc(x_l.sem, 1)
                for c in range(NF // 4):
                    if exists(i, count):
                        part = slice(4 * c, 4 * c + 4)
                        wait(dve, g_a, g_a.at(i, 4 * c + 4))
                        wait(dve, y_ps, y_ps.at(i - 1, 0))
                        dve.tensor_copy(gh[:, b, part], gel[:, c]).then_inc(g_h.sem, 1)
                        wait(dve, g_h, g_h.at(i, c + 1))
                        dve.tensor_tensor(gl[:, b, part], gel[:, c], gh[:, b, part], ALU.subtract).then_inc(g_l.sem, 1)
                if exists(i - 1, count):
                    e = expert(dve, i - 1)
                    wait(dve, y_ps, y_ps.at(i - 1, 1))
                    wait(dve, y_st[1 - b], y_st[1 - b].at((i - 1) // 2, 0))
                    for t in range(TR // P):
                        bias = b2[:, bass.ds(e, 1), :].rearrange("p e d -> p (e d)")
                        dve.scalar_tensor_tensor(yo[:, 1 - b, t], bank_y[1 - b][t][:, 0:D], 1.0 / WS,
                                                 bias, ALU.mult, ALU.add).then_inc(y_d.sem, 1)

            dve.memset(warm[:, :], 0.0).then_inc(pre.sem, 1)
            dve.wait_ge(c_ld.sem, 3 * 16)
            dve.tensor_scalar(gs[:, :, :], gate[:, :, :], 1.0 / WS, None, ALU.mult).then_inc(gs_d.sem, 1)
            dve.tensor_tensor(gb[:, :, :], b1[:, :, :], gate[:, :, :], ALU.mult).then_inc(gs_d.sem, 1)
            dve.wait_ge(gs_d.sem, 2)
            ch = Count(dve, step)
            ch(dve.tensor_copy(sf[:, :], slots.rearrange("p t k -> p (t k)")))
            ch(dve.memset(jump[:, 0:1], 0.0))
            paired(dve, count, body)
            ch(dve.scalar_tensor_tensor(shift[:, :], before[:, :], float(TR), start[:, :], ALU.mult, ALU.subtract))
            ch(dve.tensor_tensor(from_e[:, :, :], sf.unsqueeze(2).to_broadcast([P, NS, E]),
                                 start.unsqueeze(1).to_broadcast([P, NS, E]), ALU.is_ge))
            ch.wait()
            ch(dve.tensor_tensor(jump[:, 1:E], shift[:, 1:E], shift[:, 0:E - 1], ALU.subtract))
            ch.wait()
            ch(dve.tensor_tensor(from_e[:, :, :], from_e[:, :, :], jump.unsqueeze(1).to_broadcast([P, NS, E]), ALU.mult))
            ch.wait()
            ch(dve.tensor_reduce(moved[:, :], from_e[:, :, :], axis=AX.X, op=ALU.add))
            ch.wait()
            ch(dve.tensor_tensor(to_f[:, :], sf[:, :], moved[:, :], ALU.add))
            ch.wait()
            dve.tensor_copy(yslots.rearrange("p t k -> p (t k)"), to_f[:, :]).then_inc(tab_d.sem, 1)
            dve.wait_ge(w_ld.sem, 5 * 16)
            for b in range(2):
                dve.tensor_scalar(sgst[:, b], sgate[:, :], 1.0 / WS, None, ALU.mult)
                dve.tensor_tensor(sgbt[:, b], sb1[:, :], sgate[:, :], ALU.mult)
            dve.wait_ge(she_d.sem, 1)
            dve.tensor_scalar(she1[:, :], she[:, :], 1.0, None, ALU.add).then_inc(s_d.sem, 1)
            dve.wait_ge(s_d.sem, 1)
            dve.reciprocal(sgm[:, :], she1[:, :]).then_inc(s_d.sem, 1)
            dve.wait_ge(s_d.sem, 2)
            dve.tensor_scalar(sgs[:, :], sgm[:, :], 1.0 / WS, None, ALU.mult).then_inc(s_d.sem, 1)
            dve.tensor_scalar(b2p[:, 0], sb2[:, :], WS, None, ALU.mult).then_inc(s_d.sem, 1)
            dve.wait_ge(s_d.sem, 4)
            dve.scalar_tensor_tensor(b2p[:, 1], sb2[:, :], WS, b2p[:, 0], ALU.mult, ALU.subtract)
            dve.wait_ge(tab_d.sem, 1)


def load_toeplitz(sp, g, n):
    for part in range(2):
        flat = g["toe_d"][part]
        src = bass.AP(flat.tensor, flat.offset + n * CC * 2 * TAPS, [[1, P], [1, CC * 2 * TAPS]])
        sp.dma_start(g["toe"][:, n % RING, part].rearrange("p c u -> p (c u)"), src).then_inc(g["toe_ld"][n % RING].sem, 16)


def combine(nc, a, sig, mem, psum, g):
    ident, slots, wts, x2, h3h, h3l = (g[n] for n in ("ident", "yslots", "wts", "x2", "h3h", "h3l"))
    sgs, b2p, sgst, sgbt, ones = (g[n] for n in ("sgs", "b2p", "sgst", "sgbt", "ones"))
    sw1h, sw1l = (g["sw"][:, n].rearrange("p (k n) -> p k n", k=KD) for n in range(2))
    sw2h, sw2l = (g["sw"][:, n].rearrange("p (f n) -> p f n", f=NSF) for n in range(2, 4))
    count = NG2
    GR = G2 * P
    xr = mem("c_xr", [P, 2, G2, D])
    xh = mem("c_xh", [P, 2, KD, GR], F16)
    xl = mem("c_xl", [P, 2, KD, GR], F16)
    gel = mem("c_gel", [P, NSF, GR])
    gh = mem("c_gh", [P, 2, NSF, GR], F16)
    gl = mem("c_gl", [P, 2, NSF, GR], F16)
    xin = mem("c_x", [P, 2, G2, D])
    yk = mem("c_yk", [P, 2, 2, G2, D])
    ix = mem("c_ix", [P, 2, G2, 2], I32)
    u = mem("c_u", [P, G2, D])
    v = mem("c_v", [P, G2, D])
    ysum = mem("c_y", [P, 2, G2, D])
    z = mem("c_z", [P, 2, G2, D])
    h3 = mem("c_h3", [P, 2, G2, D])
    lng = mem("c_lng", [P, D])
    lnb = mem("c_lnb", [P, D])
    warm = mem("c_warm", [P, 1])
    mhalf = mem("c_mhalf", [P, G2])
    st = [mem(f"c_st{k}", [P, G2, 6]) for k in range(2)]
    mv = [mem(f"c_mv{k}", [P, G2, 2]) for k in range(2)]
    ve = [mem(f"c_ve{k}", [P, G2]) for k in range(2)]
    rs = [mem(f"c_rs{k}", [P, G2]) for k in range(2)]
    nb = [mem(f"c_nb{k}", [P, G2]) for k in range(2)]
    bank_t = psum[0:2]
    bank_u = psum[2:4]
    bank_y = (psum[4:6], psum[6:8])

    c_ld = sig("c_ld")
    mh = sig("c_mh")
    pre = sig("c_pre")
    r_ld = [sig(f"c_r_ld{b}", 16) for b in range(2)]
    t_ps = sig("c_t_ps", 1)
    x_h = sig("c_x_h", 1)
    x_l = sig("c_x_l", 1)
    u_ps = sig("c_u_ps", NSF // 2)
    g_a = sig("c_g_a", NSF)
    g_h = sig("c_g_h", 1)
    g_l = sig("c_g_l", 1)
    y_ps = sig("c_y_ps", 1)
    x_ld = [sig(f"c_x_ld{b}", 16) for b in range(2)]
    ix_d = sig("c_ix_d", 1)
    yk_ld = [sig(f"c_yk_ld{b}", 2 * G2 * 16) for b in range(2)]
    u_d = sig("c_u_d", G2)
    v_d = sig("c_v_d", G2)
    y_d = sig("c_y_d", G2)
    bn = [sig(f"c_bn{k}", G2) for k in range(2)]
    mvs = [sig(f"c_mv{k}", G2) for k in range(2)]
    rsd = [sig(f"c_rs{k}", 4) for k in range(2)]
    z_d = sig("c_z_d", G2)
    zg_d = sig("c_zg", 1)
    xb_d = sig("c_xb_d", 1)
    x2_d = sig("c_x2", 1)
    h_d = sig("c_h", G2)
    hh_d = sig("c_hh", 1)
    hl_d = sig("c_hl", 1)
    wrap_d = sig("c_wrap")

    def rows(dram, i, b):
        return dram.rearrange("(b s p) n -> p b s n", p=P, s=SLOTS - 1)[:, 2 * b:2 * b + 2, bass.ds(i // 2, 1)].rearrange("p b s n -> p (b s) n")

    def tokens(table, i, b):
        return table.rearrange("p (b s) n -> p b s n", b=B)[:, 2 * b:2 * b + 2, bass.ds(i // 2, 1)].rearrange("p b s n -> p (b s) n")

    def slot(i):
        return bass.ds(B + i * G2, G2)

    with nc.Block() as block:
        @block.sync
        def _(sp):
            def load(i, b):
                wait(sp, t_ps, t_ps.at(i, -1), True)
                sp.dma_start(xr[:, b], rows(g["h2_d"], i, b)).then_inc(r_ld[b].sem, 16)

            def residual(i, b):
                wait(sp, x2_d, x2_d.at(i, -1), True)
                sp.dma_start(xin[:, b], rows(g["x1_d"], i, b)).then_inc(x_ld[b].sem, 16)

            def body(i, b):
                if exists(i + 2, count):
                    load(i + 2, b)
                if exists(i, count):
                    residual(i, b)
                if isinstance(i, int) and count - RING < i <= count:
                    load_toeplitz(sp, g, i - (count - RING + 1))

            sp.dma_start(lng[:, :], a["lng"].partition_broadcast(P)).then_inc(c_ld.sem, 16)
            sp.dma_start(lnb[:, :], a["lnb"].partition_broadcast(P)).then_inc(c_ld.sem, 16)
            load(0, 0)
            paired(sp, count, body, 5)
            sp.wait_ge(c_ld.sem, 32)

        @block.gpsimd
        def _(pool):
            def rstd(k, i):
                wait(pool, mvs[k], mvs[k].at(i, G2), True)
                wait(pool, (z_d, h_d)[k], (z_d, h_d)[k].at(i, 0), True)
                pool.tensor_scalar(ve[k][:, :], mv[k][:, :, 1], EPS, None, ALU.add).then_inc(rsd[k].sem, 1)
                pool.tensor_scalar(nb[k][:, :], mv[k][:, :, 0], -1.0, None, ALU.mult).then_inc(rsd[k].sem, 1)
                wait(pool, rsd[k], rsd[k].at(i, 2), True)
                pool.tensor_tensor(out=rs[k][:, :], in0=ve[k][:, :], in1=mhalf[:, :], op=ALU.pow).then_inc(rsd[k].sem, 1)
                wait(pool, rsd[k], rsd[k].at(i, 3), True)
                pool.tensor_tensor(out=nb[k][:, :], in0=nb[k][:, :], in1=rs[k][:, :], op=ALU.mult).then_inc(rsd[k].sem, 1)

            def gather(i, b):
                wait(pool, ix_d, ix_d.at(i, 1), True)
                wait(pool, v_d, v_d.at(i - 1, 0), True)
                for t in range(G2):
                    for k in range(2):
                        pool.indirect_dma_start(out=yk[:, b, k, t], out_offset=None, in_=g["ys_d"][:, :],
                                                in_offset=bass.IndirectOffsetOnAxis(ap=ix[:, b, t, k:k + 1], axis=0)).then_inc(yk_ld[b].sem, 16)

            def body(i, b):
                if exists(i - 2, count):
                    rstd(0, i - 2)
                if exists(i - 3, count):
                    rstd(1, i - 3)
                if exists(i - 1, count):
                    wait(pool, x_ld[1 - b], x_ld[1 - b].at((i - 1) // 2, 16), True)
                    pool.tensor_tensor(out=xin[:, 1 - b], in0=xin[:, 1 - b], in1=lnb.unsqueeze(1).to_broadcast([P, G2, D]), op=ALU.add).then_inc(xb_d.sem, 1)
                if exists(i + 1, count):
                    gather(i + 1, 1 - b)

            pool.memset(mhalf[:, :], -0.5).then_inc(mh.sem, 1)
            pool.wait_ge(mh.sem, 1)
            pool.wait_ge(c_ld.sem, 32)
            paired(pool, count, body, 5, 3)

        @block.scalar
        def _(act):
            def body(i, b):
                if exists(i + 1, count):
                    wait(act, t_ps, t_ps.at(i + 1, 1))
                    wait(act, u_ps, u_ps.at(i, 0))
                    act.activation(xh[:, 1 - b].rearrange("p k n -> p (k n)"), bank_t[1 - b][:, :], ACT.Copy).then_inc(x_h.sem, 1)
                if exists(i - 1, count):
                    n, c = i - 1, 1 - b
                    wait(act, yk_ld[c], yk_ld[c].at(n // 2, 2 * G2 * 16))
                    wait(act, v_d, v_d.at(n, 0))
                    w = tokens(wts, n, c)
                    for t in range(G2):
                        act.activation(u[:, t], yk[:, c, 1, t], ACT.Copy, scale=w[:, t, 1:2]).then_inc(u_d.sem, 1)
                if exists(i, count):
                    wait(act, g_l, g_l.at(i, 0))
                    for f in range(NSF):
                        if f % 2 == 0:
                            wait(act, u_ps, u_ps.at(i, f // 2 + 1))
                        act.activation(gel[:, f], bank_u[f // 2 % 2][:, (f % 2) * GR:(f % 2 + 1) * GR], ACT.Gelu,
                                       bias=sgbt[:, b, f:f + 1], scale=sgst[:, b, f:f + 1]).then_inc(g_a.sem, 1)
                    wait(act, g_a, g_a.at(i, NSF))
                    wait(act, y_ps, y_ps.at(i - 1, 0))
                    act.activation(gh[:, b].rearrange("p f n -> p (f n)"), gel[:, :, :].rearrange("p f n -> p (f n)"), ACT.Copy).then_inc(g_h.sem, 1)
                if exists(i - 2, count):
                    wait(act, rsd[0], rsd[0].at(i - 2, 4))
                    wait(act, x2_d, x2_d.at(i - 3, 0))
                    for t in range(G2):
                        act.activation(z[:, b, t], ysum[:, b, t], ACT.Identity, bias=nb[0][:, t:t + 1], scale=rs[0][:, t:t + 1]).then_inc(z_d.sem, 1)
                if exists(i - 3, count):
                    wait(act, rsd[1], rsd[1].at(i - 3, 4))
                    wait(act, hl_d, hl_d.at(i - 4, 0))
                    for t in range(G2):
                        act.activation(h3[:, 1 - b, t], x2[:, bass.ds((i - 3) * G2 + t, 1)].rearrange("p t n -> p (t n)"), ACT.Identity, bias=nb[1][:, t:t + 1], scale=rs[1][:, t:t + 1]).then_inc(h_d.sem, 1)
                    wait(act, h_d, h_d.at(i - 3, G2))
                    act.activation(h3h[:, slot(i - 3)].rearrange("p t n -> p (t n)"), h3[:, 1 - b].rearrange("p t n -> p (t n)"), ACT.Copy).then_inc(hh_d.sem, 1)

            act.wait_ge(pre.sem, 1)
            act.activation(warm[:, :], warm[:, :], ACT.Gelu)
            paired(act, count, body, 5, 3)

        @block.vector
        def _(dve):
            def stats(k, i, x):
                wait(dve, mvs[k], mvs[k].at(i, 0), True)
                for t in range(G2):
                    dve.bn_stats(st[k][:, t], x(t)).then_inc(bn[k].sem, 1)
                wait(dve, rsd[k], rsd[k].at(i, 0), True)
                for t in range(G2):
                    wait(dve, bn[k], bn[k].at(i, t + 1), True)
                    dve.bn_aggr(mv[k][:, t], st[k][:, t]).then_inc(mvs[k].sem, 1)

            def index(i, b):
                wait(dve, yk_ld[b], yk_ld[b].at(i // 2, 0))
                dve.tensor_copy(ix[:, b], tokens(slots, i, b)).then_inc(ix_d.sem, 1)

            def body(i, b):
                if exists(i + 1, count):
                    wait(dve, x_h, x_h.at(i + 1, 1))
                    wait(dve, u_ps, u_ps.at(i, 0))
                    dve.tensor_tensor(xl[:, 1 - b].rearrange("p k n -> p (k n)"), bank_t[1 - b][:, :],
                                      xh[:, 1 - b].rearrange("p k n -> p (k n)"), ALU.subtract).then_inc(x_l.sem, 1)
                if exists(i + 2, count):
                    index(i + 2, b)
                if exists(i - 1, count):
                    n, c = i - 1, 1 - b
                    w = tokens(wts, n, c)
                    wait(dve, y_d, y_d.at(n, 0))
                    for t in range(G2):
                        wait(dve, u_d, u_d.at(n, t + 1))
                        dve.scalar_tensor_tensor(v[:, t], yk[:, c, 0, t], w[:, t, 0:1], u[:, t], ALU.mult, ALU.add).then_inc(v_d.sem, 1)
                if exists(i - 2, count):
                    wait(dve, z_d, z_d.at(i - 2, G2))
                    dve.tensor_tensor(z[:, b], z[:, b], lng.unsqueeze(1).to_broadcast([P, G2, D]), ALU.mult).then_inc(zg_d.sem, 1)
                    wait(dve, xb_d, xb_d.at(i - 2, 1))
                    wait(dve, zg_d, zg_d.at(i - 2, 1))
                    dve.tensor_tensor(x2[:, bass.ds((i - 2) * G2, G2)], z[:, b], xin[:, b], ALU.add).then_inc(x2_d.sem, 1)
                    wait(dve, x2_d, x2_d.at(i - 2, 1), True)
                    stats(1, i - 2, lambda t: x2[:, bass.ds((i - 2) * G2 + t, 1)].rearrange("p t n -> p (t n)"))
                if exists(i, count):
                    wait(dve, g_h, g_h.at(i, 1))
                    wait(dve, y_ps, y_ps.at(i - 1, 0))
                    dve.tensor_tensor(gl[:, b], gel[:, :, :], gh[:, b], ALU.subtract).then_inc(g_l.sem, 1)
                if exists(i - 1, count):
                    wait(dve, y_ps, y_ps.at(i - 1, 1))
                    wait(dve, z_d, z_d.at(i - 2, 0))
                    for t in range(G2):
                        wait(dve, v_d, v_d.at(i - 1, t + 1))
                        dve.scalar_tensor_tensor(ysum[:, 1 - b, t], bank_y[1 - b][t][:, 0:D], sgs[:, 0:1], v[:, t], ALU.mult, ALU.add).then_inc(y_d.sem, 1)
                    wait(dve, y_d, y_d.at(i - 1, G2))
                    stats(0, i - 1, lambda t: ysum[:, 1 - b, t])
                if exists(i - 3, count):
                    wait(dve, hh_d, hh_d.at(i - 3, 1))
                    dve.tensor_tensor(h3l[:, slot(i - 3)], h3[:, 1 - b], h3h[:, slot(i - 3)], ALU.subtract).then_inc(hl_d.sem, 1)

            dve.memset(warm[:, :], 0.0).then_inc(pre.sem, 1)
            dve.wait_ge(c_ld.sem, 32)
            index(0, 0)
            paired(dve, count, body, 5, 3)
            for h, s in ((h3h, hh_d), (h3l, hl_d)):
                dve.wait_ge(s.sem, count)
                dve.tensor_copy(h[:, 0:B], h[:, NT:NT + B]).then_inc(wrap_d.sem, 1)
            dve.wait_ge(wrap_d.sem, 2)

        @block.tensor
        def _(pe):
            def body(i, b):
                if exists(i + 1, count):
                    wait(pe, r_ld[1 - b], r_ld[1 - b].at((i + 1) // 2, 16))
                    wait(pe, x_l, x_l.at(i, 0))
                    for k in range(KD):
                        for t in range(G2):
                            m = pe.transpose(bank_t[1 - b][:, k * GR + t * P:k * GR + (t + 1) * P], xr[:, 1 - b, t, k * P:(k + 1) * P], ident[:, :])
                    m.then_inc(t_ps.sem, 1)
                if exists(i, count):
                    wait(pe, x_l, x_l.at(i, 1))
                    for p in range(NSF // 2):
                        wait(pe, g_a, g_a.at(i, 2 * (p - 1)))
                        for f in (2 * p, 2 * p + 1):
                            at = slice(f * P, (f + 1) * P)
                            m = passes(pe, bank_u[p][:, (f % 2) * GR:(f % 2 + 1) * GR],
                                       [(sw1h[:, k, at], sw1l[:, k, at], xh[:, b, k], xl[:, b, k]) for k in range(KD)])
                        m.then_inc(u_ps.sem, 1)
                if exists(i - 1, count):
                    wait(pe, g_l, g_l.at(i - 1, 1))
                    wait(pe, y_d, y_d.at(i - 2, 0))
                    for t in range(G2):
                        at = slice(t * P, (t + 1) * P)
                        out = bank_y[1 - b][t][:, 0:D]
                        for part in range(2):
                            pe.matmul(out, ones[0:1, :], b2p[:, part], start=part == 0, stop=False)
                        m = passes(pe, out, [(gh[:, 1 - b, f, at], gl[:, 1 - b, f, at], sw2h[:, f], sw2l[:, f]) for f in range(NSF)], first=False)
                    m.then_inc(y_ps.sem, 1)

            paired(pe, count, body, 5)


def convolve(nc, a, sig, mem, psum, g):
    ident, x2, h3h, h3l, toe, kmod = (g[n] for n in ("ident", "x2", "h3h", "h3l", "toe", "kmod"))
    hc = mem("v_hc", [P, 2, 2, CC, B * SLOTS], F16)
    ev = mem("v_ev", [P, 2, 4, P])
    prime = mem("v_prime", [P, 2])
    bank_c = psum[0:2]
    bank_r = psum[2:4]
    GC = CC // 4

    h_cp = sig("v_h_cp", 2)
    c_ps = sig("v_c_ps", 1)
    e_d = sig("v_e_d", 1)
    r_ps = sig("v_r_ps", 1)
    x_d = sig("v_x_d", 1)

    with nc.Block() as block:
        @block.sync
        def _(sp):
            for n in range(RING, NC):
                wait(sp, c_ps, n - RING + 1)
                load_toeplitz(sp, g, n)

        @block.scalar
        def _(act):
            with act.Fori(0, NC // RING) as q:
                for r in range(RING):
                    n = q * RING + r
                    wait(act, e_d, e_d.at(n, 1))
                    for part, h in enumerate((h3h, h3l)):
                        act.activation(hc[:, r % 2, part], h[:, :, bass.ds(n * CC, CC)].rearrange("p s c -> p c s"), ACT.Copy).then_inc(h_cp.sem, 1)

        @block.tensor
        def _(pe):
            def back(n, b):
                wait(pe, e_d, e_d.at(n, 3))
                wait(pe, x_d, x_d.at(n, 1))
                for k in range(GC):
                    m = pe.transpose(bank_r[b][:, k * P:(k + 1) * P], ev[:, b, k], ident[:, :])
                m.then_inc(r_ps.sem, 1)

            with pe.Fori(0, NC // RING) as q:
                for r in range(RING):
                    n = q * RING + r
                    b = r % 2
                    wait(pe, g["toe_ld"][r], g["toe_ld"][r].at(q, 32))
                    wait(pe, h_cp, h_cp.at(n, 2))
                    wait(pe, e_d, e_d.at(n, 1))
                    for g4 in range(GC):
                        for k in range(6):
                            for j in range(4):
                                c = g4 * 4 + j
                                s = 1 - k // 3
                                hh, hl = (hc[:, b, part, c, s * B:s * B + NT] for part in range(2))
                                th, tl = (toe[:, r, part, c, s * P:(s + 1) * P] for part in range(2))
                                x, w = ((hh, th), (hh, tl), (hl, th))[k % 3]
                                m = pe.matmul(bank_c[b][32 * j:32 * j + 32, g4 * P:(g4 + 1) * P], x, w,
                                              start=k == 0, stop=k == 5, tile_position=(0, 32 * j))
                    m.then_inc(c_ps.sem, 1)
                    if r:
                        back(n - 1, 1 - b)
                back(q * RING + RING - 1, 1)

        @block.vector
        def _(dve):
            dve.memset(prime[:, 0:1], 0.0).then_inc(e_d.sem, 2)
            dve.memset(prime[:, 1:2], 0.0).then_inc(x_d.sem, 2)
            with dve.Fori(0, NC // RING) as q:
                def add(n, b):
                    wait(dve, r_ps, r_ps.at(n, 1))
                    v = x2[:, :, bass.ds(n * CC, CC)].rearrange("p t (g j) -> p t g j", j=4)
                    dve.tensor_tensor(v, bank_r[b].rearrange("p (g j t) -> p t g j", g=GC, j=4), v, ALU.add).then_inc(x_d.sem, 1)

                for r in range(RING):
                    n = q * RING + r
                    wait(dve, c_ps, c_ps.at(n, 1))
                    dve.tensor_tensor(ev[:, r % 2, :, ::-1], bank_c[r % 2].rearrange("p (g u) -> p g u", u=P),
                                      kmod[:, bass.ds(n * GC, GC)].unsqueeze(2).to_broadcast([P, GC, P]), ALU.mult).then_inc(e_d.sem, 1)
                    if r:
                        add(n - 1, (r - 1) % 2)
                add(q * RING + RING - 1, 1)


def project(nc, a, sig, mem, psum, g):
    ident, x3, sgn = g["ident"], g["x2"], g["sgn"]
    count = NG2
    h = mem("f_h", [P, 2, G2, D])
    th = mem("f_th", [P, 2, KD, G2 * P], F16)
    tl = mem("f_tl", [P, 2, KD, G2 * P], F16)
    yo = mem("f_y", [P, 2, G2, D])
    mhalf = mem("f_mhalf", [P, G2])
    st = mem("f_st", [P, G2, 6])
    mv = mem("f_mv", [P, G2, 2])
    ve = mem("f_ve", [P, G2])
    nm = mem("f_nm", [P, G2])
    rs = mem("f_rs", [P, 2, G2])
    nb = mem("f_nb", [P, 2, G2])
    bank_t = psum[0:2]
    bank_o = psum[2:4]

    mh = sig("f_mh")
    bn = sig("f_bn", G2)
    mvs = sig("f_mv", G2)
    rsd = sig("f_rs", 4)
    h_d = sig("f_h", G2)
    t_ps = sig("f_t_ps", 1)
    t_h = sig("f_t_h", 1)
    t_l = sig("f_t_l", 1)
    o_ps = sig("f_o_ps", 1)
    y_d = sig("f_y_d", 1)
    y_st = [sig(f"f_y_st{b}", 16) for b in range(2)]

    with nc.Block() as block:
        @block.sync
        def _(sp):
            def body(i, b):
                if exists(i, count):
                    wait(sp, y_d, y_d.at(i, 1), True)
                    sp.dma_start(a["out"].rearrange("(b s p) n -> p b s n", p=P, s=SLOTS - 1)[:, 2 * b:2 * b + 2, bass.ds(i // 2, 1)].rearrange("p b s n -> p (b s) n"), yo[:, b]).then_inc(y_st[b].sem, 16)

            paired(sp, count, body, 3, 1, 3)
            for b in range(2):
                sp.wait_ge(y_st[b].sem, y_st[b].at(count // 2, 0))

        @block.gpsimd
        def _(pool):
            def body(i, b):
                if exists(i + 2, count):
                    n, c = i + 2, b
                    wait(pool, mvs, mvs.at(n, G2), True)
                    wait(pool, h_d, h_d.at(n - 1, 0), True)
                    pool.tensor_scalar(ve[:, :], mv[:, :, 1], EPS, None, ALU.add).then_inc(rsd.sem, 1)
                    pool.tensor_scalar(nm[:, :], mv[:, :, 0], -1.0, None, ALU.mult).then_inc(rsd.sem, 1)
                    wait(pool, rsd, rsd.at(n, 2), True)
                    pool.tensor_tensor(out=rs[:, c], in0=ve[:, :], in1=mhalf[:, :], op=ALU.pow).then_inc(rsd.sem, 1)
                    wait(pool, rsd, rsd.at(n, 3), True)
                    pool.tensor_tensor(out=nb[:, c], in0=nm[:, :], in1=rs[:, c], op=ALU.mult).then_inc(rsd.sem, 1)

            pool.memset(mhalf[:, :], -0.5).then_inc(mh.sem, 1)
            pool.wait_ge(mh.sem, 1)
            paired(pool, count, body, 3, 1, 3)

        @block.scalar
        def _(act):
            def body(i, b):
                if exists(i, count):
                    wait(act, t_ps, t_ps.at(i, 1))
                    wait(act, o_ps, o_ps.at(i - 1, 0))
                    act.activation(th[:, b].rearrange("p k n -> p (k n)"), bank_t[b][:, :], ACT.Copy).then_inc(t_h.sem, 1)
                if exists(i + 1, count):
                    n, c = i + 1, 1 - b
                    wait(act, rsd, rsd.at(n, 4))
                    wait(act, t_ps, t_ps.at(n - 1, 0))
                    for t in range(G2):
                        act.activation(h[:, c, t], x3[:, bass.ds(n * G2 + t, 1)].rearrange("p t n -> p (t n)"), ACT.Identity,
                                       bias=nb[:, c, t:t + 1], scale=rs[:, c, t:t + 1]).then_inc(h_d.sem, 1)

            paired(act, count, body, 3, 1, 3)

        @block.tensor
        def _(pe):
            def body(i, b):
                if exists(i + 1, count):
                    n, c = i + 1, 1 - b
                    wait(pe, h_d, h_d.at(n, G2))
                    wait(pe, t_l, t_l.at(n - 1, 0))
                    for k in range(KD):
                        for t in range(G2):
                            m = pe.transpose(bank_t[c][:, (k * G2 + t) * P:(k * G2 + t + 1) * P], h[:, c, t, k * P:(k + 1) * P], ident[:, :])
                    m.then_inc(t_ps.sem, 1)
                if exists(i, count):
                    wait(pe, t_l, t_l.at(i, 1))
                    wait(pe, y_d, y_d.at(i - 1, 0))
                    for t in range(G2):
                        at = slice(t * P, (t + 1) * P)
                        todo = [(x[:, b, k, at], sgn[:, k]) for k in range(KD) for x in (th, tl)]
                        for n, (x, w) in enumerate(todo):
                            m = pe.matmul(bank_o[b][:, t * D:(t + 1) * D], x, w, start=n == 0, stop=n == len(todo) - 1)
                    m.then_inc(o_ps.sem, 1)

            paired(pe, count, body, 3, 1, 3)

        @block.vector
        def _(dve):
            def body(i, b):
                if exists(i, count):
                    wait(dve, t_h, t_h.at(i, 1))
                    wait(dve, o_ps, o_ps.at(i - 1, 0))
                    dve.tensor_tensor(tl[:, b].rearrange("p k n -> p (k n)"), bank_t[b][:, :], th[:, b].rearrange("p k n -> p (k n)"), ALU.subtract).then_inc(t_l.sem, 1)
                if exists(i - 1, count):
                    n, c = i - 1, 1 - b
                    wait(dve, o_ps, o_ps.at(n, 1))
                    wait(dve, y_st[c], y_st[c].at(n // 2, 0))
                    dve.tensor_tensor(yo[:, c], bank_o[c].rearrange("p (t n) -> p t n", n=D), x3[:, bass.ds(n * G2, G2)], ALU.add).then_inc(y_d.sem, 1)
                if exists(i + 3, count):
                    n = i + 3
                    wait(dve, mvs, mvs.at(n, 0), True)
                    for t in range(G2):
                        dve.bn_stats(st[:, t], x3[:, bass.ds(n * G2 + t, 1)].rearrange("p t n -> p (t n)")).then_inc(bn.sem, 1)
                    wait(dve, rsd, rsd.at(n, 0), True)
                    for t in range(G2):
                        wait(dve, bn, bn.at(n, t + 1), True)
                        dve.bn_aggr(mv[:, t], st[:, t]).then_inc(mvs.sem, 1)

            paired(dve, count, body, 3, 1, 3)


def layouts(inputs):
    import numpy as np

    f = {k: np.asarray(v) for k, v in inputs.items()}
    order = np.array([(2 * (2 * pp + mt) + half) * HD + r
                      for mt in range(KD) for half in range(2) for r in range(HD) for pp in range(4)])
    wk, wv = f["L0_xattn_Wkv"][:D], f["L0_xattn_Wkv"][D:]
    bk, bv = f["L0_xattn_bkv"][:D], f["L0_xattn_bkv"][D:]
    row = np.arange(P)
    owner = row // 64 * 4 + row % 4
    out = {
        "x": f["x"].reshape(T, D),
        "ctxT": f["ctx_1024"].reshape(B * L, D).T,
        "wqT": f["L0_xattn_Wq"][order].T,
        "wkT": wk[order].T,
        "wvT": wv.T,
        "woT": f["L0_xattn_Wo"].T,
        "bq": f["L0_xattn_bq"][order].reshape(KD, P).T,
        "bk": bk[order].reshape(KD, P).T,
        "bv": bv[None],
        "bo": f["L0_xattn_bo"][None],
        "rw": f["L0_ffn_router_w"],
        "rb": f["L0_ffn_router_b"][None],
        "w1": f["L0_ffn_w1"],
        "w2": f["L0_ffn_w2"],
        "b1": f["L0_ffn_b1"].reshape(E, NF, P).transpose(2, 0, 1),
        "gate": f["L0_ffn_gate"].reshape(E, NF, P).transpose(2, 0, 1),
        "b2": f["L0_ffn_b2"].reshape(1, E * D),
        "sw1": f["L0_ffn_sw1"],
        "sw2": f["L0_ffn_sw2"],
        "sb1": f["L0_ffn_sb1"].reshape(NSF, P).T,
        "sgate": f["L0_ffn_sgate"].reshape(NSF, P).T,
        "sb2": f["L0_ffn_sb2"][None],
        "shared": f["L0_ffn_shared_weight"].reshape(1, 1),
        "lng": f["L0_ffn_ln_g"][None],
        "lnb": f["L0_ffn_ln_b"][None],
        "taps": f["L1_xattn_weight"][:, ::-1],
        "kpT": f["L1_xattn_kp_w"].T,
        "kpb": f["L1_xattn_kp_b"][None],
        "sgT": f["L1_ffn_weight"].T,
        "ident": np.eye(P, dtype=np.float32),
        "lower": np.triu(np.ones((P, P), np.float16), 1),
        "ones": np.ones((P, P), np.float16),
        "iota8": np.tile(np.arange(E, dtype=np.float32), (P, 1)),
        "tiles": np.arange(MT + 1, dtype=np.float32)[None].repeat(P, 0),
        "mask": (owner[:, None] == np.arange(8)).astype(np.float32),
        "negone": np.full((1, NPAIR * B * L), -PSC, np.float16),
    }
    return {k: np.ascontiguousarray(v) for k, v in out.items()}


def kernel(**inputs):
    import numpy as np
    import concourse.bacc as bacc
    from concourse.bass_utils import run_bass_kernel_spmd

    nc = bacc.Bacc("TRN2", target_bir_lowering=False, num_devices=1)
    arrays = layouts(inputs)
    aps = {k: nc.dram_tensor(f"in_{k}", v.shape, mybir.dt.from_np(v.dtype), kind="ExternalInput").ap()
           for k, v in arrays.items()}
    aps["out"] = nc.dram_tensor("out", (T, D), F32, kind="ExternalOutput").ap()
    build(nc, aps)
    r = run_bass_kernel_spmd(nc, [{f"in_{k}": v for k, v in arrays.items()}], core_ids=[0])
    return r.results[0]["out"].reshape(B, N, D)
```
